# Optimizing a Trainium2 kernel written in Bass

```python
import numpy as np
import jax
import jax.numpy as jnp

def _softmax(x, axis=-1):
    return jax.nn.softmax(x, axis=axis)

def _gelu(x):
    return jax.nn.gelu(x, approximate=True)

def _silu(x):
    return jax.nn.silu(x)

def _sigmoid(x):
    return jax.nn.sigmoid(x)

def _layernorm(x, axis=-1, eps=1e-05):
    m = jnp.mean(x, axis=axis, keepdims=True)
    v = jnp.var(x, axis=axis, keepdims=True)
    return (x - m) / jnp.sqrt(v + eps)

def _scatter_add(tgt, idx, src, axis=0):
    return tgt.at[idx].add(src)

def _segment_sum(src, seg, n):
    return jax.ops.segment_sum(src, seg, n)
kernel_name = 'mk_seq_preln_d2_jaxref_r4_c357a1'

def setup_inputs(seed: int=0):
    np.random.seed(seed)
    _w = jnp.asarray

    def _L0_attn_setup():
        import jax, jax.numpy as jnp
        import numpy as np
        B, S, D, H = (4, 2048, 256, 16)
        DH = D // H
        key = jax.random.key(seed)
        ks = jax.random.split(key, 11)
        sc = 0.02
        return {'x': jax.random.normal(ks[0], (B, S, D), dtype=jnp.float32), 'Wp': jax.random.normal(ks[1], (D, D), dtype=jnp.float32) * sc, 'bp': jnp.zeros((D,), dtype=jnp.float32), 'Wq': jax.random.normal(ks[2], (D, D), dtype=jnp.float32) * sc, 'bq': jnp.zeros((D,), dtype=jnp.float32), 'Wk': jax.random.normal(ks[3], (D, D), dtype=jnp.float32) * sc, 'bk': jnp.zeros((D,), dtype=jnp.float32), 'Wv': jax.random.normal(ks[4], (D, D), dtype=jnp.float32) * sc, 'bv': jnp.zeros((D,), dtype=jnp.float32), 'Wo': jax.random.normal(ks[5], (D, D), dtype=jnp.float32) * sc, 'bo': jnp.zeros((D,), dtype=jnp.float32)}
    _L0_attn_in = _L0_attn_setup()

    def _L0_ffn_setup():
        import jax, jax.numpy as jnp
        import numpy as np
        D_MODEL = 256
        N_EXPERTS = 8
        TOP_K = 2
        key = jax.random.key(seed)
        k1, k2, k3, k4 = jax.random.split(key, 4)
        B, S, D, E = (4, 512, D_MODEL, N_EXPERTS)
        dff = 4 * D
        lim = float(np.sqrt(6.0 / (D + dff)))
        return {'x': jax.random.normal(k1, (B, S, D), dtype=jnp.float32), 'router_w': jax.random.normal(k2, (D, E), dtype=jnp.float32) * (1.0 / np.sqrt(D)), 'router_b': jnp.zeros((E,), dtype=jnp.float32), 'expert_up': jax.random.uniform(k3, (E, dff, D), dtype=jnp.float32, minval=-lim, maxval=lim), 'expert_down': jax.random.uniform(k4, (E, D, dff), dtype=jnp.float32, minval=-lim, maxval=lim)}
    _L0_ffn_in = _L0_ffn_setup()

    def _L1_attn_setup():
        import jax, jax.numpy as jnp
        import numpy as np
        B, T, DM, H, DH = (4, 512, 256, 16, 64)
        DI = H * DH
        CLIP = 1.0
        LN_EPS = 1e-05
        key = jax.random.key(seed)
        ks = jax.random.split(key, 9)

        def xav(k, shape):
            lim = float(np.sqrt(6.0 / (shape[0] + shape[1])))
            return jax.random.uniform(k, shape, jnp.float32, -lim, lim)

        def kai(k, shape):
            lim = float(1.0 / np.sqrt(shape[1]))
            return jax.random.uniform(k, shape, jnp.float32, -lim, lim)
        return {'x': jax.random.normal(ks[0], (B, T, DM), jnp.float32), 'Wq': xav(ks[1], (DI, DM)), 'Wk': xav(ks[2], (DI, DM)), 'Wv': xav(ks[3], (DI, DM)), 'Wa': kai(ks[4], (DI, DM)), 'ba': jnp.full((DI,), 3.0, jnp.float32), 'Wb': kai(ks[5], (H, DM)), 'bb': jnp.zeros((H,), jnp.float32), 'Wg': kai(ks[6], (H, DM)), 'bg': jnp.zeros((H,), jnp.float32), 'WaR': kai(ks[7], (DI, DM)), 'baR': jnp.full((DI,), 3.0, jnp.float32), 'Wo': xav(ks[8], (DM, DI)), 'ln_w': jnp.ones((DM,), jnp.float32), 'ln_b': jnp.zeros((DM,), jnp.float32)}
    _L1_attn_in = _L1_attn_setup()

    def _L1_ffn_setup():
        import jax, jax.numpy as jnp
        import numpy as np
        BLOCK = 16
        _GRID = jnp.array([0.0, 0.5, 1.0, 1.5, 2.0, 3.0, 4.0, 6.0], dtype=jnp.float32)
        _MID = jnp.array([0.25, 0.75, 1.25, 1.75, 2.5, 3.5, 5.0], dtype=jnp.float32)

        def fp4_quant_dequant(x):
            shape = x.shape
            xb = x.reshape(shape[:-1] + (shape[-1] // BLOCK, BLOCK))
            scale = jnp.max(jnp.abs(xb), axis=-1, keepdims=True) / 6.0
            scale = jnp.maximum(scale, jnp.float32(1e-12))
            xn = xb / scale
            idx = jnp.searchsorted(_MID, jnp.abs(xn))
            q = _GRID[idx] * jnp.sign(xn) * scale
            return q.reshape(shape)

        def fp4_linear(x, w):
            xq = fp4_quant_dequant(x)
            wq = fp4_quant_dequant(w)
            return jnp.einsum('bsk,nk->bsn', xq, wq)
        key = jax.random.key(seed)
        k1, k2, k3, k4 = jax.random.split(key, 4)
        H, I = (256, 704)
        x = jax.random.normal(k1, (4, 1024, H), dtype=jnp.float32)
        w_gate = jax.random.normal(k2, (I, H), dtype=jnp.float32) * 0.02
        w_up = jax.random.normal(k3, (I, H), dtype=jnp.float32) * 0.02
        w_down = jax.random.normal(k4, (H, I), dtype=jnp.float32) * 0.02
        return {'x': x, 'w_gate': w_gate, 'w_up': w_up, 'w_down': w_down}
    _L1_ffn_in = _L1_ffn_setup()
    _d = {'L0_attn_x': _L0_attn_in['x'], 'L0_attn_Wp': _L0_attn_in['Wp'], 'L0_attn_bp': _L0_attn_in['bp'], 'L0_attn_Wq': _L0_attn_in['Wq'], 'L0_attn_bq': _L0_attn_in['bq'], 'L0_attn_Wk': _L0_attn_in['Wk'], 'L0_attn_bk': _L0_attn_in['bk'], 'L0_attn_Wv': _L0_attn_in['Wv'], 'L0_attn_bv': _L0_attn_in['bv'], 'L0_attn_Wo': _L0_attn_in['Wo'], 'L0_attn_bo': _L0_attn_in['bo'], 'L0_ffn_router_w': _L0_ffn_in['router_w'], 'L0_ffn_router_b': _L0_ffn_in['router_b'], 'L0_ffn_expert_up': _L0_ffn_in['expert_up'], 'L0_ffn_expert_down': _L0_ffn_in['expert_down'], 'L1_attn_Wq': _L1_attn_in['Wq'], 'L1_attn_Wk': _L1_attn_in['Wk'], 'L1_attn_Wv': _L1_attn_in['Wv'], 'L1_attn_Wa': _L1_attn_in['Wa'], 'L1_attn_ba': _L1_attn_in['ba'], 'L1_attn_Wb': _L1_attn_in['Wb'], 'L1_attn_bb': _L1_attn_in['bb'], 'L1_attn_Wg': _L1_attn_in['Wg'], 'L1_attn_bg': _L1_attn_in['bg'], 'L1_attn_WaR': _L1_attn_in['WaR'], 'L1_attn_baR': _L1_attn_in['baR'], 'L1_attn_Wo': _L1_attn_in['Wo'], 'L1_attn_ln_w': _L1_attn_in['ln_w'], 'L1_attn_ln_b': _L1_attn_in['ln_b'], 'L1_ffn_w_gate': _L1_ffn_in['w_gate'], 'L1_ffn_w_up': _L1_ffn_in['w_up'], 'L1_ffn_w_down': _L1_ffn_in['w_down']}
    _x0 = _d['L0_attn_x']
    _d['L0_attn_x'] = jax.random.normal(jax.random.fold_in(jax.random.key(seed), 1), (4, 1024, 256), dtype=_x0.dtype)
    del _x0
    return _d

def reference(L0_attn_x, L0_attn_Wp, L0_attn_bp, L0_attn_Wq, L0_attn_bq, L0_attn_Wk, L0_attn_bk, L0_attn_Wv, L0_attn_bv, L0_attn_Wo, L0_attn_bo, L0_ffn_router_w, L0_ffn_router_b, L0_ffn_expert_up, L0_ffn_expert_down, L1_attn_Wq, L1_attn_Wk, L1_attn_Wv, L1_attn_Wa, L1_attn_ba, L1_attn_Wb, L1_attn_bb, L1_attn_Wg, L1_attn_bg, L1_attn_WaR, L1_attn_baR, L1_attn_Wo, L1_attn_ln_w, L1_attn_ln_b, L1_ffn_w_gate, L1_ffn_w_up, L1_ffn_w_down):

    def _L0_attn_ref(x, Wp, bp, Wq, bq, Wk, bk, Wv, bv, Wo, bo):
        import jax, jax.numpy as jnp
        import numpy as np
        B, S, D, H = (4, 2048, 256, 16)
        DH = D // H
        b, s, d = x.shape
        scale = 1.0 / jnp.sqrt(jnp.asarray(DH, dtype=x.dtype))
        xp = x @ Wp.T + bp
        q = ((xp @ Wq.T + bq) * scale).reshape(b, s, H, DH)
        k = (xp @ Wk.T + bk).reshape(b, s, H, DH)
        v = (xp @ Wv.T + bv).reshape(b, s, H, DH)
        i = jnp.arange(s)
        idx = jnp.stack([(i - 1) % s, i, (i + 1) % s], axis=1)
        kn = k[:, idx]
        vn = v[:, idx]
        scores = jnp.einsum('bshd,bsnhd->bshn', q, kn)
        attn = jax.nn.softmax(scores, axis=-1)
        out = jnp.einsum('bshn,bsnhd->bshd', attn, vn).reshape(b, s, d)
        return out @ Wo.T + bo

    def _L0_ffn_ref(x, router_w, router_b, expert_up, expert_down):
        import jax, jax.numpy as jnp
        import numpy as np
        D_MODEL = 256
        N_EXPERTS = 8
        TOP_K = 2
        B, S, D = x.shape
        E = expert_up.shape[0]
        x_flat = x.reshape(-1, D)
        logits = x_flat @ router_w + router_b
        probs = jax.nn.softmax(logits, axis=-1)
        top_w, top_idx = jax.lax.top_k(probs, TOP_K)
        comb = jnp.sum(top_w[..., None] * jax.nn.one_hot(top_idx, E, dtype=x.dtype), axis=1)
        output = jnp.zeros_like(x_flat)
        for e in range(E):
            h = jax.nn.gelu(x_flat @ expert_up[e].T, approximate=False)
            out_e = h @ expert_down[e].T
            output = output + comb[:, e:e + 1] * out_e
        return output.reshape(B, S, D)

    def _L1_attn_ref(x, Wq, Wk, Wv, Wa, ba, Wb, bb, Wg, bg, WaR, baR, Wo, ln_w, ln_b):
        import jax, jax.numpy as jnp
        import numpy as np
        B, T, DM, H, DH = (4, 512, 256, 16, 64)
        DI = H * DH
        CLIP = 1.0
        LN_EPS = 1e-05
        Bs, Ts, _ = x.shape
        residual = x
        mu = jnp.mean(x, -1, keepdims=True)
        var = jnp.mean((x - mu) ** 2, -1, keepdims=True)
        xn = (x - mu) / jnp.sqrt(var + LN_EPS) * ln_w + ln_b
        q = (xn @ Wq.T).reshape(Bs, Ts, H, DH)
        k = (xn @ Wk.T).reshape(Bs, Ts, H, DH)
        v = (xn @ Wv.T).reshape(Bs, Ts, H, DH)
        alpha = jax.nn.sigmoid(xn @ Wa.T + ba).reshape(Bs, Ts, H, DH)
        aR = jax.nn.sigmoid(xn @ WaR.T + baR).reshape(Bs, Ts, H, DH)
        beta = jax.nn.sigmoid(xn @ Wb.T + bb)
        gamma = jax.nn.sigmoid(xn @ Wg.T + bg)
        tm = lambda a: jnp.moveaxis(a, 1, 0)
        xs = (tm(q), tm(k), tm(v), tm(alpha), tm(aR), tm(beta), tm(gamma))
        S0 = jnp.zeros((Bs, H, DH, DH), x.dtype)

        def step(carry, inp):
            S, R = carry
            q_t, k_t, v_t, a_t, aR_t, b_t, g_t = inp
            kn = k_t / jnp.maximum(jnp.linalg.norm(k_t, axis=-1, keepdims=True), 1e-12)
            pred = jnp.einsum('bhji,bhj->bhi', S, kn)
            r = jnp.clip(v_t - pred, -CLIP, CLIP)
            S = a_t[..., None] * S
            kp = jnp.einsum('bhd,bhde->bhe', kn, S)
            S = S + b_t[..., None, None] * kn[..., None] * (v_t - kp)[..., None, :]
            o = jnp.einsum('bhji,bhj->bhi', S, q_t)
            R = aR_t[..., None] * R
            kpR = jnp.einsum('bhd,bhde->bhe', kn, R)
            R = R + g_t[..., None, None] * kn[..., None] * (r - kpR)[..., None, :]
            o = o + jnp.einsum('bhji,bhj->bhi', R, q_t)
            return ((S, R), o)
        _, os = jax.lax.scan(step, (S0, S0), xs)
        out = jnp.moveaxis(os, 0, 1).reshape(Bs, Ts, DI) @ Wo.T
        return out + residual

    def _L1_ffn_ref(x, w_gate, w_up, w_down):
        import jax, jax.numpy as jnp
        import numpy as np
        BLOCK = 16
        _GRID = jnp.array([0.0, 0.5, 1.0, 1.5, 2.0, 3.0, 4.0, 6.0], dtype=jnp.float32)
        _MID = jnp.array([0.25, 0.75, 1.25, 1.75, 2.5, 3.5, 5.0], dtype=jnp.float32)

        def fp4_quant_dequant(x):
            shape = x.shape
            xb = x.reshape(shape[:-1] + (shape[-1] // BLOCK, BLOCK))
            scale = jnp.max(jnp.abs(xb), axis=-1, keepdims=True) / 6.0
            scale = jnp.maximum(scale, jnp.float32(1e-12))
            xn = xb / scale
            idx = jnp.searchsorted(_MID, jnp.abs(xn))
            q = _GRID[idx] * jnp.sign(xn) * scale
            return q.reshape(shape)

        def fp4_linear(x, w):
            xq = fp4_quant_dequant(x)
            wq = fp4_quant_dequant(w)
            return jnp.einsum('bsk,nk->bsn', xq, wq)
        gate = fp4_linear(x, w_gate)
        y = fp4_linear(x, w_up)
        h = jax.nn.silu(gate) * y
        return fp4_linear(h, w_down)
    x = L0_attn_x
    x = x + _L0_attn_ref(_layernorm(x, axis=-1), L0_attn_Wp, L0_attn_bp, L0_attn_Wq, L0_attn_bq, L0_attn_Wk, L0_attn_bk, L0_attn_Wv, L0_attn_bv, L0_attn_Wo, L0_attn_bo)
    x = x + _L0_ffn_ref(_layernorm(x, axis=-1), L0_ffn_router_w, L0_ffn_router_b, L0_ffn_expert_up, L0_ffn_expert_down)
    x = x + _L1_attn_ref(_layernorm(x, axis=-1), L1_attn_Wq, L1_attn_Wk, L1_attn_Wv, L1_attn_Wa, L1_attn_ba, L1_attn_Wb, L1_attn_bb, L1_attn_Wg, L1_attn_bg, L1_attn_WaR, L1_attn_baR, L1_attn_Wo, L1_attn_ln_w, L1_attn_ln_b)
    x = x + _L1_ffn_ref(_layernorm(x, axis=-1), L1_ffn_w_gate, L1_ffn_w_up, L1_ffn_w_down)
    return x

_drawn_inputs = setup_inputs


def setup_inputs(seed=0):
    import zlib

    import numpy as np

    out = dict(_drawn_inputs(seed))
    spreads = {'L0_attn_bp': (0.0, 0.357),
     'L0_attn_bq': (0.0, 0.8),
     'L0_attn_bk': (0.0, 0.8),
     'L0_attn_bv': (0.0, 0.1),
     'L0_attn_bo': (0.0, 0.1),
     'L0_ffn_router_b': (0.0, 0.1),
     'L1_attn_ba': (3.0, 0.2),
     'L1_attn_bb': (0.0, 0.519),
     'L1_attn_bg': (0.0, 0.538),
     'L1_attn_baR': (3.0, 0.2),
     'L1_attn_ln_w': (1.0, 0.2),
     'L1_attn_ln_b': (0.0, 0.1)}
    factors = {'L0_attn_Wq': 8.0,
     'L0_attn_Wk': 8.0,
     'L1_ffn_w_gate': 5.232,
     'L1_ffn_w_up': 5.067,
     'L1_ffn_w_down': 5.039}
    for name, (base, spread) in spreads.items():
        noise = np.random.default_rng([zlib.crc32(name.encode()), seed]).standard_normal(out[name].shape)
        drawn = base * np.exp(spread * noise) if base else spread * noise
        out[name] = jnp.asarray(drawn.astype(out[name].dtype))
    for name, factor in factors.items():
        out[name] = (out[name] * factor).astype(out[name].dtype)
    return out
```

```python
from contextlib import ExitStack

import numpy as np

import concourse.bass as bass
from concourse import mybir

ALU = mybir.AluOpType
ACT = mybir.ActivationFunctionType
F32 = mybir.dt.float32
BF16 = mybir.dt.bfloat16
U32 = mybir.dt.uint32
AX = mybir.AxisListType.X

P = 128
D = 256
KD = D // P
LN_EPS = 1e-5


class Chain:

    def __init__(self, eng, sem, per_trip=0):
        self.eng, self.sem, self.base, self.per_trip, self.n, self.trip = eng, sem, 0, per_trip, 0, None

    def enter(self, trip, per_trip):
        self.base += self.n
        self.n, self.trip, self.per_trip = 0, trip, per_trip

    def leave(self, trips):
        assert self.n == self.per_trip, (self.n, self.per_trip)
        self.base += trips * self.per_trip
        self.n, self.trip = 0, None

    def link(self, ins, apart=False):
        self.n += 1
        ins.then_inc(self.sem, 1)
        at = self.base + self.n
        at = at if self.trip is None else self.trip * self.per_trip + at
        if apart and self.trip is not None:
            wait_apart(self.eng, self.sem, at)
        else:
            self.eng.wait_ge(self.sem, at)


def wait_apart(eng, sem, at):
    eng.wait_ge(sem, at)
    eng.nop(nofuse=True)


class Scope:

    def __init__(self, nc, stack, tag):
        self.nc, self.stack, self.tag = nc, stack, tag

    def sb(self, name, shape, dt=F32):
        return self.stack.enter_context(self.nc.sbuf_tensor(f"{self.tag}_{name}", shape, dt))

    def psum(self, name, cols=512):
        return self.stack.enter_context(self.nc.psum_tensor(f"{self.tag}_{name}", [P, cols], F32))

    def sem(self, name):
        return self.stack.enter_context(self.nc.semaphore(f"{self.tag}_{name}"))


def rows(ap2, n):
    return ap2.partition_broadcast(P)


def local_attention(nc, x_in, consts, w, x_out, B, S, H):
    DH = D // H
    NT = S // P
    SW = S + 2
    TRIPS = NT * B // 2
    scale = DH ** -0.5
    with ExitStack() as stack:
        m = Scope(nc, stack, "la")
        ident = m.sb("ident", [P, P])
        mhalf = m.sb("mhalf", [P, 1])
        wp = m.sb("wp", [P, KD, D]); wq = m.sb("wq", [P, KD, D]); wkv = m.sb("wkv", [P, KD, 2 * D]); wo = m.sb("wo", [P, KD, D])
        bp = m.sb("bp", [P, KD])
        bq = m.sb("bq", [P, D]); bk = m.sb("bk", [P, D]); bv = m.sb("bv", [P, D]); bo = m.sb("bo", [P, D])
        xpT = m.sb("xpT", [P, KD, B * SW])
        x = m.sb("x", [P, 2, D]); z = m.sb("z", [P, 2, D]); zT = m.sb("zT", [P, 2, KD, P])
        st = m.sb("st", [P, 2, 6]); mv = m.sb("mv", [P, 2, 2]); ve = m.sb("ve", [P, 2, 1]); rstd = m.sb("rstd", [P, 2, 1])
        win = m.sb("win", [P, 2, KD, P + 2])
        q = m.sb("q", [P, 2, D]); kb = m.sb("kb", [P, 2, D]); qk = m.sb("qk", [P, 3, D])
        sc = m.sb("sc", [P, 3, H]); mx = m.sb("mx", [P, H]); ex = m.sb("ex", [P, 3, H]); sm = m.sb("sm", [P, H])
        av = m.sb("av", [P, 3, D]); o = m.sb("o", [P, 2, D]); oT = m.sb("oT", [P, 2, KD, P]); y = m.sb("y", [P, 2, D])
        ps_t = [m.psum(f"ps_t{i}") for i in range(2)]
        ps_q = m.psum("ps_q")
        ps_kv = [m.psum(f"ps_kv{i}") for i in range(3)]
        ps_o = [m.psum(f"ps_o{i}") for i in range(2)]
        loaded = m.sem("loaded"); x_loaded = [m.sem(f"x_loaded{i}") for i in range(2)]
        var_ready = m.sem("var_ready"); rstd_ready = m.sem("rstd_ready"); z_ready = m.sem("z_ready")
        zT_psum = m.sem("zT_psum"); zT_ready = m.sem("zT_ready"); xp_psum = m.sem("xp_psum"); xp_ready = m.sem("xp_ready")
        halo_ready = m.sem("halo_ready"); win_ready = m.sem("win_ready"); qkv_psum = m.sem("qkv_psum"); kv_used = m.sem("kv_used")
        dve_chain = m.sem("dve_chain"); act_chain = m.sem("act_chain")
        scored = m.sem("scored"); exp_ready = m.sem("exp_ready"); o_ready = m.sem("o_ready"); oT_psum = m.sem("oT_psum")
        oT_ready = m.sem("oT_ready"); proj_psum = m.sem("proj_psum"); y_ready = m.sem("y_ready"); stored = [m.sem(f"stored{i}") for i in range(2)]
        x2_loaded = [m.sem(f"x2_loaded{i}") for i in range(2)]
        LOADS = 11
        xr = x_in.rearrange("b s d -> (b s) d")
        block = stack.enter_context(nc.Block())

        @block.sync
        def _(sp):
            for dst, src in ((ident[:], consts["ident"]), (mhalf[:], consts["mhalf"]),
                             (wp[:], w["WpT"].rearrange("(k p) n -> p k n", p=P)),
                             (wq[:], w["WqT"].rearrange("(k p) n -> p k n", p=P)),
                             (wkv[:], w["WkvT"].rearrange("(k p) n -> p k n", p=P)),
                             (wo[:], w["WoT"].rearrange("(k p) n -> p k n", p=P)),
                             (bp[:], w["bp"]), (bq[:], w["bq"].partition_broadcast(P)), (bk[:], w["bk"].partition_broadcast(P)),
                             (bv[:], w["bv"].partition_broadcast(P)), (bo[:], w["bo"].partition_broadcast(P))):
                sp.dma_start(dst, src).then_inc(loaded, 16)
            with sp.Fori(0, TRIPS) as i:
                for u in range(2):
                    sp.wait_ge(z_ready, i * 2)
                    sp.dma_start(x[:, u, :], xr[bass.ds(i * (2 * P) + u * P, P), :]).then_inc(x_loaded[u], 16)
            sp.wait_ge(xp_ready, KD * NT * B)
            with sp.Fori(0, TRIPS) as i:
                for u in range(2):
                    sp.wait_ge(y_ready, i * 2)
                    sp.dma_start(x[:, u, :], xr[bass.ds(i * (2 * P) + u * P, P), :]).then_inc(x2_loaded[u], 16)
                for u in range(2):
                    sp.wait_ge(y_ready, i * 2 + u + 1)
                    sp.dma_start(x_out[bass.ds(i * (2 * P) + u * P, P), :], y[:, u, :]).then_inc(stored[u], 16)
            for u in range(2):
                sp.wait_ge(stored[u], 16 * TRIPS)

        @block.gpsimd
        def _(pool):
            pool.wait_ge(loaded, 16 * LOADS)
            with pool.Fori(0, TRIPS) as i:
                for u in range(2):
                    pool.wait_ge(var_ready, i * 2 + u + 1)
                    nc.gpsimd.tensor_tensor(rstd[:, u, :], ve[:, u, :], mhalf[:], ALU.pow).then_inc(rstd_ready, 1)

        @block.vector
        def _(dve):
            c = Chain(dve, dve_chain)
            dve.wait_ge(loaded, 16 * LOADS)
            with dve.Fori(0, TRIPS) as i:
                c.enter(i, 4)
                for u in range(2):
                    dve.wait_ge(x_loaded[u], i * 16 + 16)
                    c.link(nc.vector.bn_stats(st[:, u, :], x[:, u, :]), apart=True)
                    c.link(nc.vector.bn_aggr(mv[:, u, :], st[:, u, :]))
                    nc.vector.tensor_scalar(ve[:, u, :], mv[:, u, 1:2], LN_EPS, None, ALU.add).then_inc(var_ready, 1)
                    dve.wait_ge(rstd_ready, i * 2 + u + 1)
                    dve.wait_ge(zT_psum, i * 2)
                    nc.vector.tensor_scalar(z[:, u, :], x[:, u, :], mv[:, u, 0:1], rstd[:, u, :], ALU.subtract, ALU.mult).then_inc(z_ready, 1)
                c.leave(TRIPS)
            with dve.Fori(0, TRIPS) as i:
                c.enter(i, 40)
                for u in range(2):
                    dve.wait_ge(qkv_psum, i * 2 + u + 1)
                    c.link(nc.vector.tensor_tensor(q[:, u, :], ps_q[:, 0:D], bq[:], ALU.add))
                    c.link(nc.vector.tensor_scalar(q[:, u, :], q[:, u, :], scale, None, ALU.mult))
                    for n in range(3):
                        c.link(nc.vector.tensor_tensor(kb[:, u, :], ps_kv[n][:, 0:D], bk[:], ALU.add))
                        c.link(nc.vector.tensor_tensor(qk[:, n, :], kb[:, u, :], q[:, u, :], ALU.mult))
                        c.link(nc.vector.tensor_reduce(sc[:, n, :], qk[:, n, :].rearrange("p (h d) -> p h d", d=DH), AX, ALU.add))
                    c.link(nc.vector.tensor_tensor(mx[:], sc[:, 0, :], sc[:, 1, :], ALU.max))
                    c.link(nc.vector.tensor_tensor(mx[:], mx[:], sc[:, 2, :], ALU.max))
                    nc.vector.tensor_tensor(sc[:], sc[:], mx[:].unsqueeze(1).to_broadcast([P, 3, H]), ALU.subtract).then_inc(scored, 1)
                    dve.wait_ge(exp_ready, i * 2 + u + 1)
                    c.link(nc.vector.tensor_tensor(sm[:], ex[:, 0, :], ex[:, 1, :], ALU.add))
                    c.link(nc.vector.tensor_tensor(sm[:], sm[:], ex[:, 2, :], ALU.add))
                    c.link(nc.vector.reciprocal(sm[:], sm[:]))
                    c.link(nc.vector.tensor_tensor(ex[:], ex[:], sm[:].unsqueeze(1).to_broadcast([P, 3, H]), ALU.mult))
                    for n in range(3):
                        ins = nc.vector.tensor_tensor(av[:, n, :].rearrange("p (h d) -> p h d", d=DH),
                                                      ps_kv[n][:, D:2 * D].rearrange("p (h d) -> p h d", d=DH),
                                                      ex[:, n, :].unsqueeze(2).to_broadcast([P, H, DH]), ALU.mult)
                        if n < 2:
                            continue
                        ins.then_inc(kv_used, 1)
                    dve.wait_ge(kv_used, i * 2 + u + 1)
                    c.link(nc.vector.tensor_tensor(o[:, u, :], av[:, 0, :], av[:, 1, :], ALU.add))
                    c.link(nc.vector.tensor_tensor(o[:, u, :], o[:, u, :], av[:, 2, :], ALU.add))
                    nc.vector.tensor_tensor(o[:, u, :], o[:, u, :], bv[:], ALU.add).then_inc(o_ready, 1)
                    dve.wait_ge(proj_psum, i * 2 + u + 1)
                    dve.wait_ge(x2_loaded[u], i * 16 + 16)
                    dve.wait_ge(stored[u], i * 16)
                    c.link(nc.vector.tensor_tensor(y[:, u, :], ps_o[u][:, 0:D], bo[:], ALU.add))
                    nc.vector.tensor_tensor(y[:, u, :], y[:, u, :], x[:, u, :], ALU.add).then_inc(y_ready, 1)
                c.leave(TRIPS)

        @block.scalar
        def _(act):
            act.wait_ge(loaded, 16 * LOADS)
            with act.Fori(0, B) as b:
                with act.Fori(0, NT // 2) as i:
                    for u in range(2):
                        n = b * NT + i * 2 + u
                        act.wait_ge(zT_psum, n + 1)
                        nc.scalar.copy(zT[:, u], ps_t[u][:, 0:D].rearrange("p (k t) -> p k t", k=KD)).then_inc(zT_ready, 1)
                        act.wait_ge(xp_psum, n + 1)
                        for k in range(KD):
                            nc.scalar.activation(xpT[:, k, bass.ds(b * SW + i * (2 * P) + (u * P + 1), P)],
                                                 ps_o[u][:, k * P:(k + 1) * P], ACT.Identity, bias=bp[:, k:k + 1]).then_inc(xp_ready, 1)
            act.wait_ge(xp_ready, KD * NT * B)
            by_batch = xpT[:].rearrange("p k (b s) -> p k b s", b=B)
            nc.scalar.copy(by_batch[:, :, :, 0:1], by_batch[:, :, :, S:S + 1]).then_inc(halo_ready, 1)
            nc.scalar.copy(by_batch[:, :, :, S + 1:S + 2], by_batch[:, :, :, 1:2]).then_inc(halo_ready, 1)
            act.wait_ge(halo_ready, 2)
            with act.Fori(0, B) as b:
                with act.Fori(0, NT // 2) as i:
                    t = b * (NT // 2) + i
                    for u in range(2):
                        n = t * 2 + u
                        if u == 0:
                            act.wait_ge(qkv_psum, t * 2)
                        nc.scalar.copy(win[:, u], xpT[:, :, bass.ds(b * SW + i * (2 * P) + u * P, P + 2)]).then_inc(win_ready, 1)
                    for u in range(2):
                        n = t * 2 + u
                        act.wait_ge(scored, n + 1)
                        nc.scalar.activation(ex[:], sc[:], ACT.Exp).then_inc(exp_ready, 1)
                        act.wait_ge(oT_psum, n + 1)
                        nc.scalar.copy(oT[:, u], ps_t[u][:, 0:D].rearrange("p (k t) -> p k t", k=KD)).then_inc(oT_ready, 1)

        @block.tensor
        def _(pe):
            pe.wait_ge(loaded, 16 * LOADS)
            with pe.Fori(0, TRIPS) as t:
                for u in range(2):
                    n = t * 2 + u
                    pe.wait_ge(z_ready, n + 1)
                    for k in range(KD):
                        ins = nc.tensor.transpose(ps_t[u][:, k * P:(k + 1) * P], z[:, u, k * P:(k + 1) * P], ident[:])
                    ins.then_inc(zT_psum, 1)
                    pe.wait_ge(zT_ready, n + 1)
                    pe.wait_ge(xp_ready, t * (2 * KD))
                    for k2 in range(KD):
                        for k in range(KD):
                            ins = nc.tensor.matmul(ps_o[u][:, k2 * P:(k2 + 1) * P], wp[:, k, k2 * P:(k2 + 1) * P], zT[:, u, k, :],
                                                   start=(k == 0), stop=(k == KD - 1))
                    ins.then_inc(xp_psum, 1)
            pe.wait_ge(xp_ready, KD * NT * B)
            with pe.Fori(0, TRIPS) as t:
                for u in range(2):
                    n = t * 2 + u
                    pe.wait_ge(win_ready, n + 1)
                    pe.wait_ge(kv_used, n)
                    for k in range(KD):
                        nc.tensor.matmul(ps_q[:, 0:D], win[:, u, k, 1:P + 1], wq[:, k, :], start=(k == 0), stop=(k == KD - 1))
                    for j in range(3):
                        for k in range(KD):
                            ins = nc.tensor.matmul(ps_kv[j][:], win[:, u, k, j:j + P], wkv[:, k, :], start=(k == 0), stop=(k == KD - 1))
                    ins.then_inc(qkv_psum, 1)
                    pe.wait_ge(o_ready, n + 1)
                    for k in range(KD):
                        ins = nc.tensor.transpose(ps_t[u][:, k * P:(k + 1) * P], o[:, u, k * P:(k + 1) * P], ident[:])
                    ins.then_inc(oT_psum, 1)
                    pe.wait_ge(oT_ready, n + 1)
                    pe.wait_ge(y_ready, t * 2)
                    for k in range(KD):
                        ins = nc.tensor.matmul(ps_o[u][:, 0:D], oT[:, u, k, :], wo[:, k, :], start=(k == 0), stop=(k == KD - 1))
                    ins.then_inc(proj_psum, 1)


def mixture_of_experts(nc, x_in, consts, w, x_out, T, E, F):
    TT = 512
    ST = TT // P
    TRIPS = T // TT
    FB = F // P
    UPS = 3
    with ExitStack() as stack:
        m = Scope(nc, stack, "moe")
        ident = m.sb("ident", [P, P]); mhalf = m.sb("mhalf", [P, 1]); iota = m.sb("iota", [P, E])
        up = m.sb("up", [P, E, KD, F]); down = m.sb("down", [P, E, FB, D])
        rw = m.sb("rw", [P, KD, E]); rb = m.sb("rb", [P, E])
        acc = m.sb("acc", [P, ST, D]); z = m.sb("z", [P, ST, D]); zT = m.sb("zT", [P, KD, TT])
        st = m.sb("st", [P, ST, 6]); mv = m.sb("mv", [P, ST, 2]); ve = m.sb("ve", [P, ST]); rstd = m.sb("rstd", [P, ST])
        lg = m.sb("lg", [P, ST, E]); top = m.sb("top", [P, ST, E]); ti = m.sb("ti", [P, ST, E], U32); tf = m.sb("tf", [P, ST, 2])
        lm = m.sb("lm", [P, ST, E]); pe_ = m.sb("pexp", [P, ST, E]); sm = m.sb("sm", [P, ST]); hot = m.sb("hot", [P, 2, ST, E])
        comb = m.sb("comb", [P, ST, E])
        hT = [m.sb(f"hT{i}", [P, FB, TT]) for i in range(2)]
        ps_t = m.psum("ps_t")
        ps_up = [m.psum(f"ps_up{i}") for i in range(UPS)]
        ps_dn = [m.psum(f"ps_dn{i}") for i in range(4)]
        loaded = m.sem("loaded"); w_loaded = [m.sem(f"w_loaded{e}") for e in range(E)]
        x_loaded = m.sem("x_loaded"); var_ready = m.sem("var_ready"); rstd_ready = m.sem("rstd_ready"); z_ready = m.sem("z_ready")
        zT_psum = m.sem("zT_psum"); zT_ready = m.sem("zT_ready"); logit_psum = m.sem("logit_psum"); shifted = m.sem("shifted")
        exp_ready = m.sem("exp_ready"); chain = m.sem("chain"); up_psum = m.sem("up_psum"); h_ready = m.sem("h_ready")
        down_psum = m.sem("down_psum"); added = m.sem("added"); stored = m.sem("stored")
        LOADS = 5
        block = stack.enter_context(nc.Block())

        @block.sync
        def _(sp):
            for dst, src in ((ident[:], consts["ident"]), (mhalf[:], consts["mhalf"]), (iota[:], consts["iota8"].partition_broadcast(P)),
                             (rw[:], w["router_w"].rearrange("(k p) n -> p k n", p=P)), (rb[:], w["router_b"].partition_broadcast(P))):
                sp.dma_start(dst, src).then_inc(loaded, 16)
            for e in range(E):
                sp.dma_start(up[:, e], w["upT"][e].rearrange("(k p) f -> p k f", p=P)).then_inc(w_loaded[e], 16)
                sp.dma_start(down[:, e], w["downT"][e].rearrange("(k p) f -> p k f", p=P)).then_inc(w_loaded[e], 16)
            with sp.Fori(0, TRIPS) as i:
                sp.wait_ge(stored, i * 16)
                sp.dma_start(acc[:], x_in[bass.ds(i * TT, TT), :].rearrange("(s p) d -> p s d", p=P)).then_inc(x_loaded, 16)
                sp.wait_ge(added, (i + 1) * (E * ST))
                sp.dma_start(x_out[bass.ds(i * TT, TT), :].rearrange("(s p) d -> p s d", p=P), acc[:]).then_inc(stored, 16)
            sp.wait_ge(stored, 16 * TRIPS)

        @block.gpsimd
        def _(pool):
            pool.wait_ge(loaded, 16 * LOADS)
            with pool.Fori(0, TRIPS) as i:
                pool.wait_ge(var_ready, i + 1)
                nc.gpsimd.tensor_tensor(rstd[:], ve[:], mhalf[:].to_broadcast([P, ST]), ALU.pow).then_inc(rstd_ready, 1)

        @block.vector
        def _(dve):
            c = Chain(dve, chain)
            dve.wait_ge(loaded, 16 * LOADS)
            with dve.Fori(0, TRIPS) as i:
                c.enter(i, 13 + 2 * ST)
                dve.wait_ge(x_loaded, i * 16 + 16)
                for s in range(ST):
                    ins = nc.vector.bn_stats(st[:, s, :], acc[:, s, :])
                c.link(ins, apart=True)
                for s in range(ST):
                    ins = nc.vector.bn_aggr(mv[:, s, :], st[:, s, :])
                c.link(ins)
                nc.vector.tensor_scalar(ve[:], mv[:, :, 1], LN_EPS, None, ALU.add).then_inc(var_ready, 1)
                dve.wait_ge(rstd_ready, i + 1)
                for s in range(ST):
                    nc.vector.tensor_scalar(z[:, s, :], acc[:, s, :], mv[:, s, 0:1], rstd[:, s:s + 1], ALU.subtract, ALU.mult).then_inc(z_ready, 1)
                dve.wait_ge(logit_psum, i + 1)
                c.link(nc.vector.tensor_tensor(lg[:], ps_t[:, 0:ST * E].rearrange("p (s e) -> p s e", e=E),
                                               rb[:].unsqueeze(1).to_broadcast([P, ST, E]), ALU.add))
                c.link(nc.vector.tensor_reduce(sm[:], lg[:], AX, ALU.max))
                nc.vector.tensor_tensor(lm[:], lg[:], sm[:].unsqueeze(2).to_broadcast([P, ST, E]), ALU.subtract).then_inc(shifted, 1)
                dve.wait_ge(exp_ready, i + 1)
                c.link(nc.vector.tensor_reduce(sm[:], pe_[:], AX, ALU.add))
                c.link(nc.vector.reciprocal(sm[:], sm[:]))
                c.link(nc.vector.tensor_tensor(pe_[:], pe_[:], sm[:].unsqueeze(2).to_broadcast([P, ST, E]), ALU.mult), apart=True)
                for s in range(ST):
                    c.link(nc.vector.max(top[:, s, :], pe_[:, s, :]), apart=True)
                    c.link(nc.vector.max_index(ti[:, s, :], top[:, s, :], pe_[:, s, :]), apart=True)
                c.link(nc.vector.tensor_copy(tf[:], ti[:, :, 0:2]))
                for r in range(2):
                    c.link(nc.vector.tensor_tensor(hot[:, r], iota[:].unsqueeze(1).to_broadcast([P, ST, E]),
                                                   tf[:, :, r:r + 1].to_broadcast([P, ST, E]), ALU.is_equal))
                    c.link(nc.vector.tensor_tensor(hot[:, r], hot[:, r], top[:, :, r:r + 1].to_broadcast([P, ST, E]), ALU.mult))
                c.link(nc.vector.tensor_tensor(comb[:], hot[:, 0], hot[:, 1], ALU.add))
                for e in range(E):
                    for s in range(ST):
                        dve.wait_ge(down_psum, i * (E * ST) + (e * ST + s + 1))
                        if e > 0:
                            dve.wait_ge(added, i * (E * ST) + ((e - 1) * ST + s + 1))
                        nc.vector.scalar_tensor_tensor(acc[:, s, :], ps_dn[s][:, 0:D], comb[:, s, e:e + 1], acc[:, s, :],
                                                       ALU.mult, ALU.add).then_inc(added, 1)
                c.leave(TRIPS)

        @block.scalar
        def _(act):
            with act.Fori(0, TRIPS) as i:
                for k in range(KD):
                    act.wait_ge(zT_psum, i * KD + (k + 1))
                    nc.scalar.copy(zT[:, k, :], ps_t[:]).then_inc(zT_ready, 1)
                act.wait_ge(shifted, i + 1)
                nc.scalar.activation(pe_[:], lm[:], ACT.Exp).then_inc(exp_ready, 1)
                for e in range(E):
                    if e >= 2:
                        act.wait_ge(down_psum, i * (E * ST) + (e - 1) * ST)
                    for f in range(FB):
                        act.wait_ge(up_psum, i * (E * FB) + (e * FB + f + 1))
                        nc.scalar.activation(hT[e % 2][:, f, :], ps_up[(e * FB + f) % UPS][:], ACT.Gelu).then_inc(h_ready, 1)

        @block.tensor
        def _(pe):
            pe.wait_ge(loaded, 16 * LOADS)
            for e in range(E):
                pe.wait_ge(w_loaded[e], 32)

            def up_products(i, e):
                for f in range(FB):
                    n = e * FB + f
                    pe.wait_ge(h_ready, i * (E * FB) + max(n - UPS + 1, 0))
                    for k in range(KD):
                        ins = nc.tensor.matmul(ps_up[n % UPS][:], up[:, e, k, f * P:(f + 1) * P], zT[:, k, :],
                                               start=(k == 0), stop=(k == KD - 1))
                    ins.then_inc(up_psum, 1)

            def down_products(i, e):
                pe.wait_ge(h_ready, i * (E * FB) + (e + 1) * FB)
                for s in range(ST):
                    pe.wait_ge(added, i * (E * ST) + max((e - 1) * ST + s + 1, 0))
                    for f in range(FB):
                        ins = nc.tensor.matmul(ps_dn[s][:, 0:D], hT[e % 2][:, f, s * P:(s + 1) * P], down[:, e, f, :],
                                               start=(f == 0), stop=(f == FB - 1))
                    ins.then_inc(down_psum, 1)

            with pe.Fori(0, TRIPS) as i:
                for k in range(KD):
                    if k == 0:
                        pe.wait_ge(shifted, i)
                    else:
                        pe.wait_ge(zT_ready, i * KD + k)
                    for s in range(ST):
                        pe.wait_ge(z_ready, i * ST + (s + 1))
                        ins = nc.tensor.transpose(ps_t[:, s * P:(s + 1) * P], z[:, s, k * P:(k + 1) * P], ident[:])
                    ins.then_inc(zT_psum, 1)
                pe.wait_ge(zT_ready, (i + 1) * KD)
                for s in range(ST):
                    for k in range(KD):
                        ins = nc.tensor.matmul(ps_t[:, s * E:(s + 1) * E], zT[:, k, s * P:(s + 1) * P], rw[:, k, :],
                                               start=(k == 0), stop=(k == KD - 1))
                ins.then_inc(logit_psum, 1)
                for e in range(E):
                    up_products(i, e)
                    if e > 0:
                        down_products(i, e - 1)
                down_products(i, E - 1)


C = 32
HG = 4


def delta_consts():
    row = np.arange(P)
    b, s = row // C, row % C
    t = np.arange(C)
    same = b[:, None] == b[None, :]
    upto = same & (s[:, None] <= s[None, :])
    first_half = same & (s[:, None] < C // 2)
    cum = -(upto.astype(np.float32) - first_half.astype(np.float32))
    nb = P // C
    ends = np.zeros((P, 2, nb), np.float32)
    for j in range(nb):
        ends[(b == j) & (s < C // 2), 0, j] = -1.0
        ends[(b == j) & (s >= C // 2), 1, j] = -1.0
    strict_T = (s[:, None] < t[None, :]).astype(np.float32)
    upto_T = (s[:, None] <= t[None, :]).astype(np.float32)
    strict = (t[None, :] < s[:, None]).astype(np.float32)
    mask = np.stack([strict_T, strict_T, upto_T, strict], axis=1)
    eye = (s[:, None] == t[None, :]).astype(np.float32)
    return {"cum": cum.astype(np.float32), "ends": ends.reshape(P, 2 * nb), "mask": mask.reshape(P, 4 * C), "eye": eye}


def delta_attention(nc, x_in, consts, w, x_out, B, S, H, DH):
    DI = H * DH
    NHP = H // 2
    NCH = S // C
    NG = H // HG
    GW = HG * DH
    with ExitStack() as stack:
        m = Scope(nc, stack, "da")
        ident = m.sb("ident", [P, P]); mhalf = m.sb("mhalf", [P, 1])
        cum = m.sb("cum", [P, P]); ends = m.sb("ends", [P, 2 * B]); mask = m.sb("mask", [P, 4 * C]); eye = m.sb("eye", [P, C])
        wx = m.sb("wx", [P, KD, 5, DI]); wbg = m.sb("wbg", [P, KD, 2 * H]); wo = m.sb("wo", [P, NHP, D])
        ba = m.sb("ba", [P, 2, DI]); bbg = m.sb("bbg", [P, 2 * H]); lnw = m.sb("lnw", [P, D]); lnb = m.sb("lnb", [P, D])
        x = m.sb("x", [P, D]); z = m.sb("z", [P, D]); xz = m.sb("xz", [P, D]); xn = m.sb("xn", [P, D]); xnT = m.sb("xnT", [P, KD, P])
        st = m.sb("st", [P, 2, 6]); mv = m.sb("mv", [P, 2, 2]); ve = m.sb("ve", [P, 2]); rstd = m.sb("rstd", [P, 2])
        e = m.sb("e", [P, 2, DI])
        sp = m.sb("sp", [P, 2, DI])
        eG = m.sb("eG", [P, 2, DI]); eGn = m.sb("eGn", [P, 2, DI])
        k = m.sb("k", [P, DI]); v = m.sb("v", [P, DI]); q = m.sb("q", [P, DI]); tmp = m.sb("tmp", [P, DI])
        ss = m.sb("ss", [P, H]); ssm = m.sb("ssm", [P, H]); kinv = m.sb("kinv", [P, H])
        bg = m.sb("bg", [P, 2 * H]); bge = m.sb("bge", [P, 2 * H]); sig = m.sb("sig", [P, 2 * H]); nsig = m.sb("nsig", [P, 2 * H])
        Kb = m.sb("Kb", [P, 2, DI]); Km = m.sb("Km", [P, 2, DI]); Qp0 = m.sb("Qp0", [P, DI])
        Kprev, Qp, bv, o, oT = e[:, 0], (Qp0, q), sp[:, 1], eG[:, 0], eG[:, 1].rearrange("p (h t) -> p h t", t=P)
        FS = m.sb("FS", [P, NHP, 3, P]); FR = m.sb("FR", [P, NHP, 2, P]); FK = m.sb("FK", [P, 2, NHP, P])
        M = m.sb("M", [P, 2, NHP, B, DH])
        fac = m.sb("fac", [P, 2, NHP, 2, B]); prev_end = m.sb("prev_end", [P, 2, NHP, B]); decay = m.sb("decay", [P, 2, NHP, B])
        gm = m.sb("gm", [P, 2, 2, 2, HG // 2, 4 * C]); db = m.sb("db", [P, 2, 2, 2, HG // 2, 2, C]); dbT = m.sb("dbT", [P, 2, 2, HG // 2, C]); nn = m.sb("nn", [P, 2, 2, HG // 2, C]); TT = m.sb("TT", [P, 2, 2, 2, HG // 2, C])
        W = m.sb("W", [P, 2, 2, HG // 2, DH]); U = m.sb("U", [P, 2, 2, HG // 2, B, DH]); r = m.sb("r", [P, 2, HG // 2, DH]); y = m.sb("y", [P, D])
        pair = [m.psum(f"pair{i}", 1024) for i in range(4)]
        names = ("loaded x_loaded var_ready rstd_ready z_ready xn_ready xT_psum xT_ready proj_psum a_ready k_ready sq_ready ss_ready kinv_ready "
                 "e_ready sp_ready bg_ready bge_ready sig_ready q_ready v_ready g_ready fac_ready kb_ready kprev_ready km_ready bv_ready qp_ready "
                 "krb_ready krm_ready ft_psum ft_act ft_dve chain act_chain state_scaled gram_psum mask_done gram_ready dbl_psum y_ready w_psum w_ready part_psum "
                 "u_psum u_ready pu_psum wr_ready ds_psum s_updated ur_psum ur_ready o_psum o_ready dr_psum r_updated oT_psum oT_ready "
                 "out_psum out_ready stored xz_ready").split()
        (loaded, x_loaded, var_ready, rstd_ready, z_ready, xn_ready, xT_psum, xT_ready, proj_psum, a_ready, k_ready, sq_ready, ss_ready, kinv_ready,
         e_ready, sp_ready, bg_ready, bge_ready, sig_ready, q_ready, v_ready, g_ready, fac_ready, kb_ready, kprev_ready, km_ready, bv_ready, qp_ready,
         krb_ready, krm_ready, ft_psum, ft_act, ft_dve, chain, act_chain, state_scaled, gram_psum, mask_done, gram_ready, dbl_psum, y_ready, w_psum, w_ready, part_psum,
         u_psum, u_ready, pu_psum, wr_ready, ds_psum, s_updated, ur_psum, ur_ready, o_psum, o_ready, dr_psum, r_updated, oT_psum, oT_ready,
         out_psum, out_ready, stored, xz_ready) = [m.sem(n) for n in names]

        per_head = lambda a: a.rearrange("p (h d) -> p h d", d=DH)
        over_head = lambda a, n=H: a.unsqueeze(2).to_broadcast([P, n, DH])
        LEVELS = 5
        HJ = HG // 2
        JW = HJ * DH
        gram_ps = pair[0][:].rearrange("p (q c) -> p q c", q=2)[:, :, 0:HJ * 4 * C].rearrange("p q (j c) -> p q j c", j=HJ)
        power_ps = [pair[1][:, rec * 512:rec * 512 + HG * 2 * C].rearrange("p (q j s c) -> p q j s c", q=2, j=HJ, s=2) for rec in range(2)]
        wu_ps = pair[2][:].rearrange("p (q k j e) -> p q k j e", q=2, k=4, j=HJ)
        po_ps = pair[3][:].rearrange("p (q k j e) -> p q k j e", q=2, k=4, j=HJ)
        by_head = lambda a: a.rearrange("p (j q e) -> p q j e", q=2, e=DH)

        ORDER = (("G", 0), "W0", "V0", ("G", 1), ("D", 0, 0), "U0", ("D", 0, 1), ("D", 1, 0), "W1", "I0", ("D", 1, 1), "S0",
                 ("D", 2, 0), ("D", 2, 1), "U1", ("D", 3, 0), "I1", ("D", 3, 1), "S1", ("D", 4, 0), ("D", 4, 1))
        gram_at = lambda i, g, rec: i * (2 * NG) + (2 * g + rec + 1)
        dbl_at = lambda i, g, lvl, rec: i * (10 * NG) + (10 * g + 2 * lvl + rec + 1)
        y_at = lambda i, g, lvl, rec: i * (10 * NG) + (10 * g + 2 * lvl + rec + 1)
        once = lambda i, g: i * NG + (g + 1)
        LOADS = 18
        block = stack.enter_context(nc.Block())
        chunk_rows = lambda a, i, b: a[bass.ds(i * C + b * S, C), :]

        @block.sync
        def _(sp_):
            rows_ = lambda a: a.partition_broadcast(P)
            loads = [(ident[:], consts["ident"]), (mhalf[:], consts["mhalf"]), (cum[:], consts["cum"]), (ends[:], consts["ends"]),
                     (mask[:], consts["mask"]), (eye[:], consts["eye"]),
                     (wbg[:], w["WbgT"].rearrange("(k p) n -> p k n", p=P)), (wo[:], w["WoT"].rearrange("(k p) n -> p k n", p=P)),
                     (ba[:, 0], rows_(w["ba"])), (ba[:, 1], rows_(w["baR"])), (bbg[:], rows_(w["bbg"])), (lnw[:], rows_(w["ln_w"])), (lnb[:], rows_(w["ln_b"]))]
            loads += [(wx[:, :, j], w[n].rearrange("(k p) n -> p k n", p=P)) for j, n in enumerate(("WaT", "WaRT", "WkT", "WqT", "WvT"))]
            assert len(loads) == LOADS
            for dst, src in loads:
                sp_.dma_start(dst, src).then_inc(loaded, 16)
            with sp_.Fori(0, NCH) as i:
                sp_.wait_ge(xz_ready, i)
                for b in range(B):
                    sp_.dma_start(x[b * C:(b + 1) * C, :], chunk_rows(x_in, i, b)).then_inc(x_loaded, 16)
                sp_.wait_ge(out_ready, i + 1)
                for b in range(B):
                    sp_.dma_start(chunk_rows(x_out, i, b), y[b * C:(b + 1) * C, :]).then_inc(stored, 16)
            sp_.wait_ge(stored, 16 * B * NCH)

        @block.gpsimd
        def _(pool):
            pool.wait_ge(loaded, 16 * LOADS)
            with pool.Fori(0, NCH) as i:
                for n in range(2):
                    pool.wait_ge(var_ready, i * 2 + (n + 1))
                    nc.gpsimd.tensor_tensor(rstd[:, n:n + 1], ve[:, n:n + 1], mhalf[:], ALU.pow).then_inc(rstd_ready, 1)
                pool.wait_ge(z_ready, i + 1)
                pool.wait_ge(out_ready, i)
                nc.gpsimd.tensor_tensor(xz[:], x[:], z[:], ALU.add).then_inc(xz_ready, 1)
                pool.wait_ge(ss_ready, i + 1)
                nc.gpsimd.tensor_tensor(kinv[:], ssm[:], mhalf[:].to_broadcast([P, H]), ALU.pow).then_inc(kinv_ready, 1)
                pool.wait_ge(v_ready, i + 1)
                pool.wait_ge(sig_ready, i * 2 + 2)
                pool.wait_ge(fac_ready, i * 2 + 2)
                nc.gpsimd.tensor_tensor(per_head(bv), per_head(v[:]), over_head(sig[:, 0:H]), ALU.mult).then_inc(bv_ready, 1)
                pool.wait_ge(q_ready, i + 1)
                for rec in range(2):
                    pool.wait_ge(g_ready, i * 4 + 2 * rec + 1)
                    pool.wait_ge(qp_ready, i * 2 + rec)
                    nc.gpsimd.tensor_tensor(Qp[rec][:], q[:], eG[:, rec], ALU.mult).then_inc(qp_ready, 1)

        @block.vector
        def _(dve):
            c = Chain(dve, chain)
            c.link(nc.vector.memset(M[:].rearrange("p a b c d -> p (a b c d)"), 0.0))
            c.link(nc.vector.memset(U[:].rearrange("p a b c d e -> p (a b c d e)"), 0.0))
            c.link(nc.vector.memset(prev_end[:].rearrange("p a b c -> p (a b c)"), 1.0))
            dve.wait_ge(loaded, 16 * LOADS)

            flat = lambda a: a.rearrange("p q j c -> p (q j c)")

            def gram_mask(i, g, rec):
                lo = 0 if rec == 0 else C
                dve.wait_ge(gram_psum, gram_at(i, g, rec))
                for q_ in range(2):
                    ins = nc.vector.tensor_tensor(gm[:, rec, g % 2, q_, :, lo:3 * C], gram_ps[:, q_, :, lo:3 * C],
                                                  mask[:, lo:3 * C].unsqueeze(1).to_broadcast([P, HJ, 3 * C - lo]), ALU.mult)
                ins.then_inc(mask_done, 1)
                dve.wait_ge(mask_done, gram_at(i, g, rec))
                c.link(nc.vector.transpose(nn[:, rec], gm[:, rec, g % 2, :, :, C:2 * C]))
                nc.vector.tensor_tensor(db[:, rec, 0, :, :, 1, :], nn[:, rec], eye[:].unsqueeze(1).unsqueeze(1).to_broadcast([P, 2, HJ, C]), ALU.add).then_inc(gram_ready, 1)

            def powers(i, g, lvl, rec):
                dve.wait_ge(dbl_psum, dbl_at(i, g, lvl, rec))
                out = power_ps[rec]
                if lvl > 0:
                    last = lvl == LEVELS - 1
                    ins = nc.vector.tensor_tensor(nn[:, rec] if last else db[:, rec, lvl % 2, :, :, 1, :], db[:, rec, (lvl - 1) % 2, :, :, 1, :], out[:, :, :, 1, :], ALU.add)
                    if last:
                        c.link(ins)
                        nc.vector.transpose(TT[:, rec, g % 2], nn[:, rec]).then_inc(y_ready, 1)
                        return
                nc.vector.tensor_copy(db[:, rec, lvl % 2, :, :, 0, :], out[:, :, :, 0, :])
                nc.vector.transpose(dbT[:, rec], out[:, :, :, 0, :]).then_inc(y_ready, 1)

            def add_bv(i, g):
                dve.wait_ge(w_psum, once(i, g))
                nc.vector.tensor_tensor(W[:, 0], wu_ps[:, :, 0], by_head(bv[:, g * GW:(g + 1) * GW]), ALU.add).then_inc(w_ready, 1)

            def clipped(i, g):
                dve.wait_ge(pu_psum, once(i, g))
                gamma = sig[:, H + g * HG:H + (g + 1) * HG].rearrange("p (j q) -> p q j", q=2).unsqueeze(3).to_broadcast([P, 2, HJ, DH])
                c.link(nc.vector.tensor_tensor(r[:], by_head(v[:, g * GW:(g + 1) * GW]), po_ps[:, :, 0], ALU.subtract))
                c.link(nc.vector.tensor_scalar(r[:], r[:], 1.0, -1.0, ALU.min, ALU.max))
                c.link(nc.vector.tensor_tensor(r[:], r[:], gamma, ALU.mult))
                nc.vector.tensor_tensor(W[:, 1], wu_ps[:, :, 1], r[:], ALU.add).then_inc(wr_ready, 1)

            def update(i, g, rec):
                dve.wait_ge((ds_psum, dr_psum)[rec], once(i, g))
                st_ = M[:, rec, 2 * g:2 * g + 2].rearrange("p a b c -> p (a b c)")
                nc.vector.tensor_tensor(st_, pair[0][:, rec * 512:(rec + 1) * 512], st_, ALU.add).then_inc((s_updated, r_updated)[rec], 1)

            with dve.Fori(0, NCH) as i:
                c.enter(i, 43)
                dve.wait_ge(x_loaded, i * (16 * B) + 16 * B)
                for n, src in enumerate((x, z)):
                    c.link(nc.vector.bn_stats(st[:, n], src[:]), apart=True)
                    c.link(nc.vector.bn_aggr(mv[:, n], st[:, n]))
                    nc.vector.tensor_scalar(ve[:, n:n + 1], mv[:, n, 1:2], LN_EPS, None, ALU.add).then_inc(var_ready, 1)
                    dve.wait_ge(rstd_ready, i * 2 + (n + 1))
                    if n == 0:
                        dve.wait_ge(xz_ready, i)
                        nc.vector.tensor_scalar(z[:], x[:], mv[:, 0, 0:1], rstd[:, 0:1], ALU.subtract, ALU.mult).then_inc(z_ready, 1)
                        dve.wait_ge(z_ready, i + 1)
                    else:
                        c.link(nc.vector.tensor_scalar(xn[:], z[:], mv[:, 1, 0:1], rstd[:, 1:2], ALU.subtract, ALU.mult))
                c.link(nc.vector.tensor_tensor(xn[:], xn[:], lnw[:], ALU.mult))
                nc.vector.tensor_tensor(xn[:], xn[:], lnb[:], ALU.add).then_inc(xn_ready, 1)
                for rec in range(2):
                    dve.wait_ge(proj_psum, i * 9 + (rec + 1))
                    nc.vector.tensor_tensor(sp[:, rec], pair[rec][:], ba[:, rec], ALU.add).then_inc(a_ready, 1)
                dve.wait_ge(sq_ready, i + 1)
                c.link(nc.vector.tensor_reduce(ss[:], per_head(tmp[:]), AX, ALU.add))
                nc.vector.tensor_scalar(ssm[:], ss[:], 1e-24, None, ALU.max).then_inc(ss_ready, 1)
                dve.wait_ge(proj_psum, i * 9 + 4)
                nc.vector.tensor_tensor(bg[:], pair[3][:, 256:256 + 2 * H], bbg[:], ALU.add).then_inc(bg_ready, 1)
                dve.wait_ge(bge_ready, i + 1)
                c.link(nc.vector.tensor_scalar(bge[:], bge[:], 1.0, None, ALU.add))
                nc.vector.reciprocal(sig[:], bge[:]).then_inc(sig_ready, 1)
                dve.wait_ge(sig_ready, i * 2 + 1)
                nc.vector.tensor_scalar(nsig[:], sig[:], -1.0, None, ALU.mult).then_inc(sig_ready, 1)
                dve.wait_ge(kinv_ready, i + 1)
                dve.wait_ge(sig_ready, i * 2 + 2)
                c.link(nc.vector.tensor_tensor(per_head(k[:]), per_head(k[:]), over_head(kinv[:]), ALU.mult))
                for rec in range(2):
                    dve.wait_ge(g_ready, i * 4 + 2 * rec + 1)
                    c.link(nc.vector.tensor_tensor(tmp[:], eG[:, rec], k[:], ALU.mult))
                    nc.vector.tensor_tensor(per_head(Kb[:, rec]), per_head(tmp[:]), over_head(nsig[:, rec * H:(rec + 1) * H]), ALU.mult).then_inc(kb_ready, 1)
                    if rec == 0:
                        c.link(nc.vector.scalar_tensor_tensor(Kprev, e[:, 0], 1.0, tmp[:], ALU.add, ALU.mult))
                    dve.wait_ge(g_ready, i * 4 + 2 * rec + 2)
                    nc.vector.tensor_tensor(Km[:, rec], eGn[:, rec], k[:], ALU.mult).then_inc(km_ready, 1)
                dve.wait_ge(fac_ready, i * 2 + 2)
                c.link(nc.vector.tensor_tensor(decay[:], fac[:, :, :, 0, :], prev_end[:], ALU.mult))
                for rec in range(2):
                    st_ = M[:, rec].rearrange("p a b c -> p (a b) c")
                    c.link(nc.vector.tensor_tensor(st_, st_, decay[:, rec].rearrange("p a b -> p (a b)").unsqueeze(2).to_broadcast([P, NHP * B, DH]), ALU.mult))
                nc.vector.tensor_copy(prev_end[:], fac[:, :, :, 1, :]).then_inc(state_scaled, 1)
                dve.wait_ge(ft_psum, i * 7 + 4)
                nc.vector.tensor_copy(FS[:, :, 2, :], pair[3][:].rearrange("p (h t) -> p h t", t=P)).then_inc(ft_dve, 1)
                dve.wait_ge(ft_psum, i * 7 + 7)
                nc.vector.tensor_copy(FR[:, :, 1, :], pair[2][:].rearrange("p (h t) -> p h t", t=P)).then_inc(ft_dve, 1)
                for slot in range(NG + 1):
                    g, s = slot, slot - 1
                    for what in ORDER:
                        if what[0] in "GD":
                            if g >= NG:
                                continue
                            if what[0] == "G":
                                gram_mask(i, g, what[1])
                            else:
                                powers(i, g, what[1], what[2])
                        elif s >= 0:
                            if what == "W0":
                                if s == 0:
                                    dve.wait_ge(bv_ready, i + 1)
                                add_bv(i, s)
                            elif what == "I0":
                                clipped(i, s)
                            elif what[0] == "S":
                                update(i, s, int(what[1]))
                dve.wait_ge(out_psum, i + 1)
                dve.wait_ge(stored, i * (16 * B))
                nc.vector.tensor_tensor(y[:], pair[1][:, 0:D], xz[:], ALU.add).then_inc(out_ready, 1)
                c.leave(NCH)

        @block.scalar
        def _(act):
            def copy_u(i, g, rec):
                act.wait_ge((u_psum, ur_psum)[rec], once(i, g))
                for b in range(B):
                    ins = nc.scalar.copy(U[b * C:(b + 1) * C, rec, :, :, b, :], wu_ps[b * C:(b + 1) * C, :, 2 + rec])
                ins.then_inc((u_ready, ur_ready)[rec], 1)

            act.wait_ge(loaded, 16 * LOADS)
            with act.Fori(0, NCH) as i:
                act.wait_ge(xT_psum, i + 1)
                nc.scalar.copy(xnT[:], pair[3][:, 0:D].rearrange("p (k t) -> p k t", k=KD)).then_inc(xT_ready, 1)
                act.wait_ge(proj_psum, i * 9 + 3)
                nc.scalar.copy(k[:], pair[2][:]).then_inc(k_ready, 1)
                nc.scalar.activation(tmp[:], pair[2][:], ACT.Square).then_inc(sq_ready, 1)
                act.wait_ge(bg_ready, i + 1)
                nc.scalar.activation(bge[:], bg[:], ACT.Exp, scale=-1.0).then_inc(bge_ready, 1)
                for rec in range(2):
                    act.wait_ge(a_ready, i * 2 + (rec + 1))
                    nc.scalar.activation(e[:, rec], sp[:, rec], ACT.Exp, scale=-1.0).then_inc(e_ready, 1)
                for rec in range(2):
                    act.wait_ge(e_ready, i * 2 + (rec + 1))
                    nc.scalar.activation(sp[:, rec], e[:, rec], ACT.Ln, bias=1.0).then_inc(sp_ready, 1)
                act.wait_ge(proj_psum, i * 9 + 5)
                nc.scalar.copy(q[:], pair[0][:]).then_inc(q_ready, 1)
                act.wait_ge(proj_psum, i * 9 + 6)
                nc.scalar.copy(v[:], pair[1][:]).then_inc(v_ready, 1)
                for rec in range(2):
                    act.wait_ge(proj_psum, i * 9 + (7 + rec))
                    nc.scalar.activation(eG[:, rec], pair[2 + rec][:], ACT.Exp).then_inc(g_ready, 1)
                    nc.scalar.activation(eGn[:, rec], pair[2 + rec][:], ACT.Exp, scale=-1.0).then_inc(g_ready, 1)
                act.wait_ge(proj_psum, i * 9 + 9)
                for rec in range(2):
                    nc.scalar.activation(fac[:, rec].rearrange("p a b c -> p (a b c)"), pair[0][:, rec * 512:rec * 512 + NHP * 2 * B], ACT.Exp).then_inc(fac_ready, 1)
                for n, dst in ((0, FS[:, :, 1, :]), (1, FS[:, :, 0, :]), (2, FK[:, 0]), (4, FR[:, :, 0, :]), (5, FK[:, 1])):
                    act.wait_ge(ft_psum, i * 7 + (n + 1))
                    nc.scalar.copy(dst, pair[n % 4][:].rearrange("p (h t) -> p h t", t=P)).then_inc(ft_act, 1)
                for s in range(NG):
                    copy_u(i, s, 0)
                    copy_u(i, s, 1)
                    act.wait_ge(o_psum, once(i, s))
                    nc.scalar.copy(by_head(o[:, s * GW:(s + 1) * GW]), po_ps[:, :, 1]).then_inc(o_ready, 1)
                act.wait_ge(oT_psum, i + 1)
                nc.scalar.copy(oT, pair[0][:].rearrange("p (h t) -> p h t", t=P)).then_inc(oT_ready, 1)

        @block.tensor
        def _(pe):
            mm = nc.tensor.matmul

            apart = lambda sem, at: wait_apart(pe, sem, at)

            heads = [(b, q_, j) for j in range(HJ) for q_ in range(2) for b in range(B)]
            rows_of = lambda b: slice(b * C, (b + 1) * C)
            feat = lambda q_: slice(DH * q_, DH * (q_ + 1))

            def gram(i, g, rec):
                F = (FS, FR)[rec]
                lo = 0 if rec == 0 else 1
                for b, q_, j in heads:
                    f, hp, rw = feat(q_), g * HJ + j, rows_of(b)
                    ins = mm(gram_ps[rw, q_, j, lo * C:3 * C], FK[f, rec, hp, rw], F[f, hp, lo - rec:3 - rec, rw], start=True, stop=True)
                ins.then_inc(gram_psum, 1)

            def double(i, g, lvl, rec):
                if lvl == 0:
                    apart(gram_ready, gram_at(i, g, rec))
                    apart(y_ready, i * (10 * NG) + 10 * g)
                else:
                    apart(y_ready, y_at(i, g, lvl - 1, rec))
                for b, q_, j in heads:
                    rw = rows_of(b)
                    out = power_ps[rec][rw, q_, j]
                    if lvl == 0:
                        ins = mm(out[:, 0, :], gm[rw, rec, g % 2, q_, j, C:2 * C], nn[rw, rec, q_, j], start=True, stop=True)
                    else:
                        lo = 1 if lvl == LEVELS - 1 else 0
                        ins = mm(out[:, lo:2, :], dbT[rw, rec, q_, j], db[rw, rec, (lvl - 1) % 2, q_, j, lo:2, :], start=True, stop=True)
                ins.then_inc(dbl_psum, 1)

            def state_w(i, g, rec):
                if rec == 0:
                    apart(ur_ready, i * NG + g)
                else:
                    apart(u_ready, once(i, g))
                F = (FS, FR)[rec]
                for b, q_, j in heads:
                    f, hp, rw = feat(q_), g * HJ + j, rows_of(b)
                    ins = mm(wu_ps[rw, q_, rec, j], F[f, hp, 1 - rec, rw], M[f, rec, hp, b, :], start=True, stop=True)
                if rec == 0:
                    ins.then_inc(w_psum, 1)

            def state_parts(i, g, rec):
                apart(o_ready, i * NG + g)
                for b, q_, j in heads:
                    f, hp, rw = feat(q_), g * HJ + j, rows_of(b)
                    mm(po_ps[rw, q_, 0, j], FS[f, hp, 0, rw], M[f, 0, hp, b, :], start=(j == 0), stop=False, skip_group_check=True)
                for b, q_, j in heads:
                    f, hp, rw = feat(q_), g * HJ + j, rows_of(b)
                    mm(po_ps[rw, q_, 1, j], FS[f, hp, 2, rw], M[f, 0, hp, b, :], start=False, stop=False, skip_group_check=True)
                    mm(po_ps[rw, q_, 1, j], FR[f, hp, 1, rw], M[f, 1, hp, b, :], start=False, stop=False, skip_group_check=True)

            def solve(i, g, rec):
                apart((w_ready, wr_ready)[rec], once(i, g))
                apart(y_ready, y_at(i, g, LEVELS - 1, rec))
                for b, q_, j in heads:
                    rw = rows_of(b)
                    ins = mm(wu_ps[rw, q_, 2 + rec, j], TT[rw, rec, g % 2, q_, j], W[rw, rec, q_, j], start=True, stop=True)
                ins.then_inc((u_psum, ur_psum)[rec], 1)

            def inner_parts(i, g, rec):
                apart((u_ready, ur_ready)[rec], once(i, g))
                for b, q_, j in heads:
                    rw = rows_of(b)
                    G = gm[rw, rec, g % 2, q_, j]
                    if rec == 0:
                        mm(po_ps[rw, q_, 0, j], G[:, 0:C], U[rw, 0, q_, j, b], start=False, stop=True, skip_group_check=True)
                    ins = mm(po_ps[rw, q_, 1, j], G[:, 2 * C:3 * C], U[rw, rec, q_, j, b], start=False, stop=(rec == 1), skip_group_check=True)
                ins.then_inc((pu_psum, o_psum)[rec], 1)

            def state_update(i, g, rec):
                for q_ in range(2):
                    for j in range(HJ):
                        col = (g * HG + 2 * j + q_) * DH
                        ins = mm(pair[0][feat(q_), rec * 512 + j * B * DH:rec * 512 + (j + 1) * B * DH], Km[:, rec, col:col + DH],
                                 U[:, rec, q_, j].rearrange("p b e -> p (b e)"), start=True, stop=True)
                ins.then_inc((ds_psum, dr_psum)[rec], 1)

            def project(out, j, n0):
                for half in range(2):
                    for kk in range(KD):
                        ins = mm(out[:, half * 512:(half + 1) * 512], xnT[:, kk, :], wx[:, kk, j, half * 512:(half + 1) * 512], start=(kk == 0), stop=(kk == KD - 1))
                ins.then_inc(proj_psum, 1)

            pe.wait_ge(loaded, 16 * LOADS)
            with pe.Fori(0, NCH) as i:
                pe.wait_ge(xn_ready, i + 1)
                pe.wait_ge(out_ready, i)
                for kk in range(KD):
                    ins = nc.tensor.transpose(pair[3][:, kk * P:(kk + 1) * P], xn[:, kk * P:(kk + 1) * P], ident[:])
                ins.then_inc(xT_psum, 1)
                pe.wait_ge(xT_ready, i + 1)
                project(pair[0], 0, 0)
                project(pair[1], 1, 0)
                project(pair[2], 2, 0)
                for kk in range(KD):
                    ins = mm(pair[3][:, 256:256 + 2 * H], xnT[:, kk, :], wbg[:, kk, :], start=(kk == 0), stop=(kk == KD - 1))
                ins.then_inc(proj_psum, 1)
                pe.wait_ge(a_ready, i * 2 + 1)
                project(pair[0], 3, 0)
                pe.wait_ge(a_ready, i * 2 + 2)
                project(pair[1], 4, 0)
                pe.wait_ge(sq_ready, i + 1)
                pe.wait_ge(bg_ready, i + 1)
                for rec in range(2):
                    pe.wait_ge(sp_ready, i * 2 + (rec + 1))
                    for half in range(2):
                        ins = mm(pair[2 + rec][:, half * 512:(half + 1) * 512], cum[:], sp[:, rec, half * 512:(half + 1) * 512], start=True, stop=True)
                    ins.then_inc(proj_psum, 1)
                pe.wait_ge(q_ready, i + 1)
                for rec in range(2):
                    for hp in range(NHP):
                        ins = mm(pair[0][:, rec * 512 + hp * 2 * B:rec * 512 + (hp + 1) * 2 * B], sp[:, rec, hp * P:(hp + 1) * P], ends[:], start=True, stop=True)
                ins.then_inc(proj_psum, 1)
                for n, (src, ready) in enumerate((
                        (Kb[:, 0], [(kb_ready, i * 2 + 1), (fac_ready, i * 2 + 2)]), (Kprev, [(km_ready, i * 2 + 1), (v_ready, i + 1)]),
                        (Km[:, 0], [(km_ready, i * 2 + 1), (g_ready, i * 4 + 2)]), (Qp[0], [(qp_ready, i * 2 + 1), (g_ready, i * 4 + 4)]),
                        (Kb[:, 1], [(kb_ready, i * 2 + 2), (ft_act, i * 5 + 1)]), (Km[:, 1], [(km_ready, i * 2 + 2), (ft_act, i * 5 + 2)]),
                        (Qp[1], [(qp_ready, i * 2 + 2), (ft_act, i * 5 + 3)]))):
                    for sem, at in ready:
                        pe.wait_ge(sem, at)
                    for hp in range(NHP):
                        ins = nc.tensor.transpose(pair[n % 4][:, hp * P:(hp + 1) * P], src[:, hp * P:(hp + 1) * P], ident[:])
                    ins.then_inc(ft_psum, 1)
                pe.wait_ge(ft_act, i * 5 + 5)
                pe.wait_ge(ft_dve, i * 2 + 2)
                apart(state_scaled, i + 1)
                for slot in range(NG + 1):
                    g, s = slot, slot - 1
                    for what in ORDER:
                        if what[0] in "GD":
                            if g >= NG:
                                continue
                            if what[0] == "D":
                                double(i, g, what[1], what[2])
                                continue
                            apart(*((r_updated, i * NG + max(s, 0)) if what[1] == 0 else (mask_done, gram_at(i, g, 0))))
                            gram(i, g, what[1])
                        elif s >= 0:
                            rec = int(what[1])
                            if what[0] == "S" and rec == 0:
                                apart(mask_done, gram_at(i, min(g, NG - 1), 1))
                            {"W": state_w, "V": state_parts, "U": solve, "I": inner_parts, "S": state_update}[what[0]](i, s, rec)
                pe.wait_ge(r_updated, (i + 1) * NG)
                pe.wait_ge(o_ready, (i + 1) * NG)
                for hp in range(NHP):
                    ins = nc.tensor.transpose(pair[0][:, hp * P:(hp + 1) * P], o[:, hp * P:(hp + 1) * P], ident[:])
                ins.then_inc(oT_psum, 1)
                pe.wait_ge(oT_ready, i + 1)
                for hp in range(NHP):
                    ins = mm(pair[1][:, 0:D], oT[:, hp, :], wo[:, hp, :], start=(hp == 0), stop=(hp == NHP - 1))
                ins.then_inc(out_psum, 1)


FP4_BLOCK = 16
FP4_MAX = 6.0
FP4_STEPS = ((5.0, 4), (3.5, 2), (2.5, 2), (1.75, 1), (1.25, 1), (0.75, 1), (0.25, 1))


def fp4_feed_forward(nc, x_in, consts, w, x_out, T, I):
    IC = -(-I // P)
    HI = I // 2
    NT = T // P
    TRIPS = NT // 2
    QLINKS = 12
    with ExitStack() as stack:
        m = Scope(nc, stack, "ff")
        ident = m.sb("ident", [P, P]); mhalf = m.sb("mhalf", [P, 1])
        guT = [m.sb(f"guT{j}", [P, KD, I]) for j in range(2)]
        downT = m.sb("downT", [P, IC, D])
        x = m.sb("x", [P, 2, D]); y = m.sb("y", [P, 2, D]); z = m.sb("z", [P, 2, D]); zqT = m.sb("zqT", [P, 2, KD, P])
        st = m.sb("st", [P, 2, 6]); mv = m.sb("mv", [P, 2, 2]); ve = m.sb("ve", [P, 2, 1]); rstd = m.sb("rstd", [P, 2, 1])
        raw = m.sb("raw", [P, 2, I]); mag = m.sb("mag", [P, 2, I]); sgn = m.sb("sgn", [P, 2, I])
        ratio = m.sb("ratio", [P, I]); level = m.sb("level", [P, I]); qz = m.sb("qz", [P, 2, D]); qh = m.sb("qh", [P, 2, I])
        amax = m.sb("amax", [P, I // FP4_BLOCK]); scl = m.sb("scl", [P, I // FP4_BLOCK]); inv = m.sb("inv", [P, I // FP4_BLOCK])
        silu = m.sb("silu", [P, 2, I]); hqT = m.sb("hqT", [P, 2, IC, P])
        ps_z = m.psum("ps_z"); ps_h = [m.psum(f"ps_h{i}") for i in range(2)]
        ps_g = [m.psum(f"ps_g{i}") for i in range(2)]; ps_u = [m.psum(f"ps_u{i}") for i in range(2)]; ps_y = m.psum("ps_y")
        loaded = m.sem("loaded"); w_loaded = [m.sem(f"w_loaded{i}") for i in range(2)]; w_signs = m.sem("w_signs"); w_quantised = m.sem("w_quantised")
        wT_psum = m.sem("wT_psum"); wT_ready = m.sem("wT_ready"); chain = m.sem("chain")
        x_loaded = [m.sem(f"x_loaded{i}") for i in range(2)]; var_ready = m.sem("var_ready"); rstd_ready = m.sem("rstd_ready")
        z_ready = m.sem("z_ready"); z_signs = m.sem("z_signs"); qz_ready = m.sem("qz_ready"); zT_psum = m.sem("zT_psum")
        zT_ready = m.sem("zT_ready"); gu_psum = m.sem("gu_psum"); silu_ready = m.sem("silu_ready"); h_ready = m.sem("h_ready")
        h_signs = m.sem("h_signs"); qh_ready = m.sem("qh_ready"); hT_psum = m.sem("hT_psum"); hT_ready = m.sem("hT_ready")
        y_psum = m.sem("y_psum"); y_ready = m.sem("y_ready"); stored = [m.sem(f"stored{i}") for i in range(2)]

        items = []
        for j, name in enumerate(("w_gate", "w_up")):
            for r in range(IC):
                n = min(P, I - r * P)
                items.append((w[name][r * P:r * P + n, :], n, D, [guT[j][:, k, r * P:r * P + n] for k in range(KD)]))
        for r in range(KD):
            items.append((w["w_down"][r * P:(r + 1) * P, :], P, I,
                          [downT[0:min(P, I - k * P), k, r * P:(r + 1) * P] for k in range(IC)]))

        block = stack.enter_context(nc.Block())

        @block.sync
        def _(sp):
            for dst, src in ((ident[:], consts["ident"]), (mhalf[:], consts["mhalf"])):
                sp.dma_start(dst, src).then_inc(loaded, 16)
            for n, (src, rows_, cols, _) in enumerate(items):
                if n >= 2:
                    sp.wait_ge(w_signs, n - 1)
                sp.dma_start(raw[0:rows_, n % 2, 0:cols], src).then_inc(w_loaded[n % 2], 16)
            with sp.Fori(0, TRIPS) as i:
                for u in range(2):
                    sp.wait_ge(y_ready, i * 2)
                    sp.dma_start(x[:, u, :], x_in[bass.ds(i * (2 * P) + u * P, P), :]).then_inc(x_loaded[u], 16)
                for u in range(2):
                    sp.wait_ge(y_ready, i * 2 + u + 1)
                    sp.dma_start(x_out[bass.ds(i * (2 * P) + u * P, P), :], y[:, u, :]).then_inc(stored[u], 16)
            for u in range(2):
                sp.wait_ge(stored[u], 16 * TRIPS)

        @block.gpsimd
        def _(pool):
            pool.wait_ge(loaded, 32)
            with pool.Fori(0, TRIPS) as i:
                for u in range(2):
                    pool.wait_ge(var_ready, i * 2 + u + 1)
                    nc.gpsimd.tensor_tensor(rstd[:, u, :], ve[:, u, :], mhalf[:], ALU.pow).then_inc(rstd_ready, 1)

        @block.vector
        def _(dve):
            c = Chain(dve, chain)

            def fp4(n, cols, magnitude, sign, out, done):
                nb = cols // FP4_BLOCK
                blocks = lambda a: a.rearrange("p (b e) -> p b e", e=FP4_BLOCK)
                per_block = lambda a: a[0:n, 0:nb].unsqueeze(2).to_broadcast([n, nb, FP4_BLOCK])
                r, l = ratio[0:n, 0:cols], level[0:n, 0:cols]
                c.link(nc.vector.tensor_reduce(amax[0:n, 0:nb], blocks(magnitude), AX, ALU.max))
                c.link(nc.vector.tensor_scalar(scl[0:n, 0:nb], amax[0:n, 0:nb], 1.0 / FP4_MAX, 1e-12, ALU.mult, ALU.max))
                c.link(nc.vector.reciprocal(inv[0:n, 0:nb], scl[0:n, 0:nb]))
                c.link(nc.vector.tensor_tensor(blocks(r), blocks(magnitude), per_block(inv), ALU.mult))
                c.link(nc.vector.tensor_scalar(l, r, FP4_STEPS[0][0], float(FP4_STEPS[0][1]), ALU.is_gt, ALU.mult))
                for at, halves in FP4_STEPS[1:]:
                    for _ in range(halves):
                        c.link(nc.vector.scalar_tensor_tensor(l, r, at, l, ALU.is_gt, ALU.add))
                c.link(nc.vector.scalar_tensor_tensor(blocks(l), blocks(l), 0.5, per_block(scl), ALU.mult, ALU.mult))
                nc.vector.tensor_tensor(out, l, sign, ALU.mult).then_inc(done, 1)

            QL = 6 + sum(h for _, h in FP4_STEPS[1:])
            for n, (_, rows_, cols, _) in enumerate(items):
                dve.wait_ge(w_signs, n + 1)
                if n >= 2:
                    dve.wait_ge(wT_psum, n - 1)
                fp4(rows_, cols, mag[0:rows_, n % 2, 0:cols], sgn[0:rows_, n % 2, 0:cols], qh[0:rows_, n % 2, 0:cols], w_quantised)
            with dve.Fori(0, TRIPS) as i:
                c.enter(i, 2 * (2 + 2 * QL))
                for u in range(2):
                    dve.wait_ge(x_loaded[u], i * 16 + 16)
                    c.link(nc.vector.bn_stats(st[:, u, :], x[:, u, :]), apart=True)
                    c.link(nc.vector.bn_aggr(mv[:, u, :], st[:, u, :]))
                    nc.vector.tensor_scalar(ve[:, u, :], mv[:, u, 1:2], LN_EPS, None, ALU.add).then_inc(var_ready, 1)
                    dve.wait_ge(rstd_ready, i * 2 + u + 1)
                    nc.vector.tensor_scalar(z[:, u, :], x[:, u, :], mv[:, u, 0:1], rstd[:, u, :], ALU.subtract, ALU.mult).then_inc(z_ready, 1)
                    dve.wait_ge(z_signs, i * 2 + u + 1)
                    fp4(P, D, mag[:, u, 0:D], sgn[:, u, 0:D], qz[:, u, :], qz_ready)
                for u in range(2):
                    dve.wait_ge(silu_ready, i * 2 + u + 1)
                    for j in range(2):
                        ins = nc.vector.tensor_tensor(raw[:, u, j * HI:(j + 1) * HI], silu[:, u, j * HI:(j + 1) * HI], ps_u[j][:, 0:HI], ALU.mult)
                        ins.then_inc(h_ready, 1)
                    dve.wait_ge(h_signs, i * 2 + u + 1)
                    fp4(P, I, mag[:, u, :], sgn[:, u, :], qh[:, u, :], qh_ready)
                    dve.wait_ge(y_psum, i * 2 + u + 1)
                    dve.wait_ge(stored[u], i * 16)
                    nc.vector.tensor_tensor(y[:, u, :], ps_y[:, 0:D], x[:, u, :], ALU.add).then_inc(y_ready, 1)
                c.leave(TRIPS)

        @block.scalar
        def _(act):
            for n, (_, rows_, cols, dst) in enumerate(items):
                act.wait_ge(w_loaded[n % 2], 16 * (n // 2 + 1))
                if n >= 2:
                    act.wait_ge(w_quantised, n - 1)
                nc.scalar.activation(mag[0:rows_, n % 2, 0:cols], raw[0:rows_, n % 2, 0:cols], ACT.Abs)
                nc.scalar.activation(sgn[0:rows_, n % 2, 0:cols], raw[0:rows_, n % 2, 0:cols], ACT.Sign).then_inc(w_signs, 1)
                act.wait_ge(wT_psum, n + 1)
                for k, d in enumerate(dst):
                    ins = nc.scalar.copy(d, ps_h[k // 4][0:d.shape[0], (k % 4) * P:(k % 4) * P + rows_])
                ins.then_inc(wT_ready, 1)
            with act.Fori(0, TRIPS) as i:
                for u in range(2):
                    act.wait_ge(z_ready, i * 2 + u + 1)
                    nc.scalar.activation(mag[:, u, 0:D], z[:, u, :], ACT.Abs)
                    nc.scalar.activation(sgn[:, u, 0:D], z[:, u, :], ACT.Sign).then_inc(z_signs, 1)
                    act.wait_ge(zT_psum, i * 2 + u + 1)
                    nc.scalar.copy(zqT[:, u], ps_z[:, 0:D].rearrange("p (k t) -> p k t", k=KD)).then_inc(zT_ready, 1)
                for u in range(2):
                    act.wait_ge(gu_psum, i * 2 + u + 1)
                    for j in range(2):
                        ins = nc.scalar.activation(silu[:, u, j * HI:(j + 1) * HI], ps_g[j][:, 0:HI], ACT.Silu)
                    ins.then_inc(silu_ready, 1)
                    act.wait_ge(h_ready, (i * 2 + u + 1) * 2)
                    nc.scalar.activation(mag[:, u, :], raw[:, u, :], ACT.Abs)
                    nc.scalar.activation(sgn[:, u, :], raw[:, u, :], ACT.Sign).then_inc(h_signs, 1)
                    act.wait_ge(hT_psum, i * 2 + u + 1)
                    nc.scalar.copy(hqT[:, u, 0:4, :], ps_h[0][:].rearrange("p (k t) -> p k t", k=4))
                    nc.scalar.copy(hqT[:, u, 4, :], ps_h[1][:, 0:P])
                    nc.scalar.copy(hqT[0:I - 5 * P, u, 5, :], ps_h[1][0:I - 5 * P, P:2 * P]).then_inc(hT_ready, 1)

        def gate_up(pe, i, u):
            pe.wait_ge(zT_ready, i * 2 + u + 1)
            pe.wait_ge(h_ready, (i * 2 + u) * 2)
            for j in range(2):
                for g, bank in ((0, ps_g[j]), (1, ps_u[j])):
                    for k in range(KD):
                        ins = nc.tensor.matmul(bank[:, 0:HI], zqT[:, u, k, :], guT[g][:, k, j * HI:(j + 1) * HI],
                                               start=(k == 0), stop=(k == KD - 1))
            ins.then_inc(gu_psum, 1)

        @block.tensor
        def _(pe):
            pe.wait_ge(loaded, 32)
            for n, (_, rows_, cols, dst) in enumerate(items):
                pe.wait_ge(w_quantised, n + 1)
                pe.wait_ge(wT_ready, n)
                for k in range(len(dst)):
                    width = min(P, cols - k * P)
                    ins = nc.tensor.transpose(ps_h[k // 4][0:width, (k % 4) * P:(k % 4) * P + rows_],
                                              qh[0:rows_, n % 2, k * P:k * P + width], ident[0:rows_, 0:rows_])
                ins.then_inc(wT_psum, 1)
            pe.wait_ge(wT_ready, len(items))
            with pe.Fori(0, TRIPS) as i:
                for u in range(2):
                    n = i * 2 + u
                    pe.wait_ge(qz_ready, n + 1)
                    pe.wait_ge(zT_ready, n)
                    for k in range(KD):
                        ins = nc.tensor.transpose(ps_z[:, k * P:(k + 1) * P], qz[:, u, k * P:(k + 1) * P], ident[:])
                    ins.then_inc(zT_psum, 1)
                    if u == 0:
                        gate_up(pe, i, u)
                for u in range(2):
                    if u == 1:
                        gate_up(pe, i, u)
                    pe.wait_ge(qh_ready, i * 2 + u + 1)
                    for k in range(IC):
                        width = min(P, I - k * P)
                        ins = nc.tensor.transpose(ps_h[k // 4][0:width, (k % 4) * P:(k % 4 + 1) * P], qh[:, u, k * P:k * P + width], ident[:])
                    ins.then_inc(hT_psum, 1)
                    pe.wait_ge(hT_ready, i * 2 + u + 1)
                    pe.wait_ge(y_ready, i * 2 + u)
                    for k in range(IC):
                        width = min(P, I - k * P)
                        ins = nc.tensor.matmul(ps_y[:, 0:D], hqT[0:width, u, k, :], downT[0:width, k, :], start=(k == 0), stop=(k == IC - 1))
                    ins.then_inc(y_psum, 1)


_OUT = (4, 1024, 256)


def build(nc, a, out):
    B, S, _ = _OUT
    T = B * S
    streams = [nc.dram_tensor(f"stream{i}", (T, D), F32).ap() for i in range(3)]
    consts = {n: a[n] for n in ("ident", "mhalf", "iota8", "cum", "ends", "mask", "eye")}
    local_attention(nc, a["x"], consts, {n: a["L0_" + n] for n in ("WpT", "WqT", "WkvT", "WoT", "bp", "bq", "bk", "bv", "bo")}, streams[0], B, S, 16)
    mixture_of_experts(nc, streams[0], consts, {n: a[n] for n in ("router_w", "router_b", "upT", "downT")}, streams[1], T, 8, 1024)
    delta_attention(nc, streams[1], consts, {n: a["L1_" + n] for n in ("WaT", "WaRT", "WkT", "WqT", "WvT", "WbgT", "WoT", "ba", "baR", "bbg", "ln_w", "ln_b")},
                    streams[2], B, S, 16, 64)
    fp4_feed_forward(nc, streams[2], consts, {n: a[n] for n in ("w_gate", "w_up", "w_down")}, out.rearrange("b s d -> (b s) d"), T, 704)


def kernel(**inputs):
    import concourse.bacc as _bacc
    from concourse.bass_utils import run_bass_kernel_spmd as _run

    g = {n: np.asarray(v) for n, v in inputs.items()}
    t = lambda n: g[n].T
    arrays = {
        "x": g["L0_attn_x"],
        "L0_WpT": t("L0_attn_Wp"), "L0_WqT": t("L0_attn_Wq"), "L0_WkvT": np.concatenate([t("L0_attn_Wk"), t("L0_attn_Wv")], axis=1), "L0_WoT": t("L0_attn_Wo"),
        "L0_bp": g["L0_attn_bp"].reshape(KD, P).T, "L0_bq": g["L0_attn_bq"], "L0_bk": g["L0_attn_bk"], "L0_bv": g["L0_attn_bv"], "L0_bo": g["L0_attn_bo"],
        "router_w": g["L0_ffn_router_w"], "router_b": g["L0_ffn_router_b"],
        "upT": g["L0_ffn_expert_up"].transpose(0, 2, 1), "downT": g["L0_ffn_expert_down"].transpose(0, 2, 1),
        "L1_WaT": t("L1_attn_Wa"), "L1_WaRT": t("L1_attn_WaR"), "L1_WkT": t("L1_attn_Wk"), "L1_WqT": t("L1_attn_Wq"), "L1_WvT": t("L1_attn_Wv"),
        "L1_WbgT": np.concatenate([t("L1_attn_Wb"), t("L1_attn_Wg")], axis=1), "L1_WoT": t("L1_attn_Wo"),
        "L1_ba": g["L1_attn_ba"], "L1_baR": g["L1_attn_baR"], "L1_bbg": np.concatenate([g["L1_attn_bb"], g["L1_attn_bg"]]),
        "L1_ln_w": g["L1_attn_ln_w"], "L1_ln_b": g["L1_attn_ln_b"],
        "w_gate": g["L1_ffn_w_gate"], "w_up": g["L1_ffn_w_up"], "w_down": g["L1_ffn_w_down"],
        "ident": np.eye(P, dtype=np.float32), "mhalf": np.full((P, 1), -0.5, np.float32), "iota8": np.arange(8, dtype=np.float32),
    }
    arrays.update(delta_consts())
    nc = _bacc.Bacc("TRN2", target_bir_lowering=False, num_devices=1)
    feeds, args = {}, {}
    for name, array in arrays.items():
        feeds[f"in_{name}"] = np.ascontiguousarray(array)
        args[name] = nc.dram_tensor(f"in_{name}", feeds[f"in_{name}"].shape, mybir.dt.from_np(feeds[f"in_{name}"].dtype), kind="ExternalInput").ap()
    out = nc.dram_tensor("out_0", _OUT, F32, kind="ExternalOutput").ap()
    build(nc, args, out)
    r = _run(nc, [feeds], core_ids=[0])
    return r.results[0]["out_0"]
```

```python
from contextlib import ExitStack

import numpy as np

import concourse.bass as bass
from concourse import mybir

ALU = mybir.AluOpType
ACT = mybir.ActivationFunctionType
F32 = mybir.dt.float32
BF16 = mybir.dt.bfloat16
U32 = mybir.dt.uint32
AX = mybir.AxisListType.X

P = 128
D = 256
KD = D // P
LN_EPS = 1e-5


class Chain:

    def __init__(self, eng, sem, per_trip=0):
        self.eng, self.sem, self.base, self.per_trip, self.n, self.trip = eng, sem, 0, per_trip, 0, None

    def enter(self, trip, per_trip):
        self.base += self.n
        self.n, self.trip, self.per_trip = 0, trip, per_trip

    def leave(self, trips):
        assert self.n == self.per_trip, (self.n, self.per_trip)
        self.base += trips * self.per_trip
        self.n, self.trip = 0, None

    def link(self, ins, apart=False):
        self.n += 1
        ins.then_inc(self.sem, 1)
        at = self.base + self.n
        at = at if self.trip is None else self.trip * self.per_trip + at
        if apart and self.trip is not None:
            wait_apart(self.eng, self.sem, at)
        else:
            self.eng.wait_ge(self.sem, at)


def wait_apart(eng, sem, at):
    eng.wait_ge(sem, at)
    eng.nop(nofuse=True)


class Scope:

    def __init__(self, nc, stack, tag):
        self.nc, self.stack, self.tag = nc, stack, tag

    def sb(self, name, shape, dt=F32):
        return self.stack.enter_context(self.nc.sbuf_tensor(f"{self.tag}_{name}", shape, dt))

    def psum(self, name, cols=512):
        return self.stack.enter_context(self.nc.psum_tensor(f"{self.tag}_{name}", [P, cols], F32))

    def sem(self, name):
        return self.stack.enter_context(self.nc.semaphore(f"{self.tag}_{name}"))


def rows(ap2, n):
    return ap2.partition_broadcast(P)


def local_attention(nc, x_in, consts, w, x_out, B, S, H):
    DH = D // H
    NT = S // P
    SW = S + 2
    TRIPS = NT * B // 2
    scale = DH ** -0.5
    with ExitStack() as stack:
        m = Scope(nc, stack, "la")
        ident = m.sb("ident", [P, P])
        mhalf = m.sb("mhalf", [P, 1])
        wp = m.sb("wp", [P, KD, D]); wq = m.sb("wq", [P, KD, D]); wkv = m.sb("wkv", [P, KD, 2 * D]); wo = m.sb("wo", [P, KD, D])
        bp = m.sb("bp", [P, KD])
        bq = m.sb("bq", [P, D]); bk = m.sb("bk", [P, D]); bv = m.sb("bv", [P, D]); bo = m.sb("bo", [P, D])
        xpT = m.sb("xpT", [P, KD, B * SW])
        x = m.sb("x", [P, 2, D]); z = m.sb("z", [P, 2, D]); zT = m.sb("zT", [P, 2, KD, P])
        st = m.sb("st", [P, 2, 6]); mv = m.sb("mv", [P, 2, 2]); ve = m.sb("ve", [P, 2, 1]); rstd = m.sb("rstd", [P, 2, 1])
        win = m.sb("win", [P, 2, KD, P + 2])
        q = m.sb("q", [P, 2, D]); kv = m.sb("kv", [P, 2, 3, 2 * D]); qraw = m.sb("qraw", [P, 2, D]); kb = m.sb("kb", [P, 3, D]); qk = m.sb("qk", [P, 3, D])
        sc = m.sb("sc", [P, 3, H]); mx = m.sb("mx", [P, H]); ex = m.sb("ex", [P, 3, H]); sm = m.sb("sm", [P, H])
        av = m.sb("av", [P, 3, D]); osum = m.sb("osum", [P, 2, D]); xb = m.sb("xb", [P, 2, D]); o = m.sb("o", [P, 2, D]); oT = m.sb("oT", [P, 2, KD, P]); y = m.sb("y", [P, 2, D])
        ps_t = [m.psum(f"ps_t{i}") for i in range(2)]
        ps_q = m.psum("ps_q")
        ps_kv = [m.psum(f"ps_kv{i}") for i in range(3)]
        ps_o = [m.psum(f"ps_o{i}") for i in range(2)]
        loaded = m.sem("loaded"); x_loaded = [m.sem(f"x_loaded{i}") for i in range(2)]
        var_ready = m.sem("var_ready"); rstd_ready = m.sem("rstd_ready"); z_ready = m.sem("z_ready")
        zT_psum = m.sem("zT_psum"); zT_ready = m.sem("zT_ready"); xp_psum = m.sem("xp_psum"); xp_ready = m.sem("xp_ready")
        halo_ready = m.sem("halo_ready"); win_ready = m.sem("win_ready"); qkv_psum = m.sem("qkv_psum"); kv_used = m.sem("kv_used")
        kv_copied = m.sem("kv_copied"); dve_chain = m.sem("dve_chain"); xb_ready = m.sem("xb_ready")
        scored = m.sem("scored"); exp_ready = m.sem("exp_ready"); o_ready = m.sem("o_ready"); oT_psum = m.sem("oT_psum")
        oT_ready = m.sem("oT_ready"); proj_psum = m.sem("proj_psum"); y_ready = m.sem("y_ready"); stored = [m.sem(f"stored{i}") for i in range(2)]
        x2_loaded = [m.sem(f"x2_loaded{i}") for i in range(2)]
        LOADS = 11
        xr = x_in.rearrange("b s d -> (b s) d")
        block = stack.enter_context(nc.Block())

        @block.sync
        def _(sp):
            for dst, src in ((ident[:], consts["ident"]), (mhalf[:], consts["mhalf"]),
                             (wp[:], w["WpT"].rearrange("(k p) n -> p k n", p=P)),
                             (wq[:], w["WqT"].rearrange("(k p) n -> p k n", p=P)),
                             (wkv[:], w["WkvT"].rearrange("(k p) n -> p k n", p=P)),
                             (wo[:], w["WoT"].rearrange("(k p) n -> p k n", p=P)),
                             (bp[:], w["bp"]), (bq[:], w["bq"].partition_broadcast(P)), (bk[:], w["bk"].partition_broadcast(P)),
                             (bv[:], w["bv"].partition_broadcast(P)), (bo[:], w["bo"].partition_broadcast(P))):
                sp.dma_start(dst, src).then_inc(loaded, 16)
            with sp.Fori(0, TRIPS) as i:
                for u in range(2):
                    sp.wait_ge(z_ready, i * 2)
                    sp.dma_start(x[:, u, :], xr[bass.ds(i * (2 * P) + u * P, P), :]).then_inc(x_loaded[u], 16)
            sp.wait_ge(xp_ready, KD * NT * B)
            with sp.Fori(0, TRIPS) as i:
                for u in range(2):
                    sp.wait_ge(y_ready, i * 2)
                    sp.dma_start(x[:, u, :], xr[bass.ds(i * (2 * P) + u * P, P), :]).then_inc(x2_loaded[u], 16)
                for u in range(2):
                    sp.wait_ge(y_ready, i * 2 + u + 1)
                    sp.dma_start(x_out[bass.ds(i * (2 * P) + u * P, P), :], y[:, u, :]).then_inc(stored[u], 16)
            for u in range(2):
                sp.wait_ge(stored[u], 16 * TRIPS)

        @block.gpsimd
        def _(pool):
            pool.wait_ge(loaded, 16 * LOADS)
            with pool.Fori(0, TRIPS) as i:
                for u in range(2):
                    pool.wait_ge(var_ready, i * 2 + u + 1)
                    nc.gpsimd.tensor_tensor(rstd[:, u, :], ve[:, u, :], mhalf[:], ALU.pow).then_inc(rstd_ready, 1)

        @block.vector
        def _(dve):
            c = Chain(dve, dve_chain)
            dve.wait_ge(loaded, 16 * LOADS)
            with dve.Fori(0, TRIPS) as i:
                c.enter(i, 4)
                for u in range(2):
                    dve.wait_ge(x_loaded[u], i * 16 + 16)
                    c.link(nc.vector.bn_stats(st[:, u, :], x[:, u, :]), apart=True)
                    c.link(nc.vector.bn_aggr(mv[:, u, :], st[:, u, :]))
                    nc.vector.tensor_scalar(ve[:, u, :], mv[:, u, 1:2], LN_EPS, None, ALU.add).then_inc(var_ready, 1)
                    dve.wait_ge(rstd_ready, i * 2 + u + 1)
                    dve.wait_ge(zT_psum, i * 2)
                    nc.vector.tensor_scalar(z[:, u, :], x[:, u, :], mv[:, u, 0:1], rstd[:, u, :], ALU.subtract, ALU.mult).then_inc(z_ready, 1)
                c.leave(TRIPS)
            with dve.Fori(0, TRIPS) as i:
                c.enter(i, 22)
                for u in range(2):
                    dve.wait_ge(kv_copied, i * 8 + (4 * u + 4))
                    nc.vector.tensor_tensor(q[:, u, :], qraw[:, u, :], bq[:], ALU.add)
                    c.link(nc.vector.tensor_tensor(kb[:], kv[:, u, :, 0:D], bk[:].unsqueeze(1).to_broadcast([P, 3, D]), ALU.add))
                    c.link(nc.vector.tensor_tensor(qk[:], kb[:], q[:, u, :].unsqueeze(1).to_broadcast([P, 3, D]), ALU.mult))
                    c.link(nc.vector.tensor_reduce(sc[:].rearrange("p n h -> p (n h)"), qk[:].rearrange("p n (h d) -> p (n h) d", d=DH), AX, ALU.add))
                    c.link(nc.vector.tensor_tensor(mx[:], sc[:, 0, :], sc[:, 1, :], ALU.max))
                    c.link(nc.vector.tensor_tensor(mx[:], mx[:], sc[:, 2, :], ALU.max))
                    nc.vector.tensor_tensor(sc[:], sc[:], mx[:].unsqueeze(1).to_broadcast([P, 3, H]), ALU.subtract).then_inc(scored, 1)
                    dve.wait_ge(x2_loaded[u], i * 16 + 16)
                    nc.vector.tensor_tensor(xb[:, u, :], x[:, u, :], bo[:], ALU.add).then_inc(xb_ready, 1)
                    dve.wait_ge(exp_ready, i * 2 + u + 1)
                    c.link(nc.vector.tensor_tensor(sm[:], ex[:, 0, :], ex[:, 1, :], ALU.add))
                    c.link(nc.vector.tensor_tensor(sm[:], sm[:], ex[:, 2, :], ALU.add))
                    c.link(nc.vector.reciprocal(sm[:], sm[:]))
                    c.link(nc.vector.tensor_tensor(ex[:], ex[:], sm[:].unsqueeze(1).to_broadcast([P, 3, H]), ALU.mult))
                    for n in range(3):
                        ins = nc.vector.tensor_tensor(av[:, n, :].rearrange("p (h d) -> p h d", d=DH),
                                                      kv[:, u, n, D:2 * D].rearrange("p (h d) -> p h d", d=DH),
                                                      ex[:, n, :].unsqueeze(2).to_broadcast([P, H, DH]), ALU.mult)
                    ins.then_inc(kv_used, 1)
                    dve.wait_ge(kv_used, i * 2 + u + 1)
                    c.link(nc.vector.tensor_tensor(osum[:, u, :], av[:, 0, :], av[:, 1, :], ALU.add))
                    c.link(nc.vector.tensor_tensor(osum[:, u, :], osum[:, u, :], av[:, 2, :], ALU.add))
                    nc.vector.tensor_tensor(o[:, u, :], osum[:, u, :], bv[:], ALU.add).then_inc(o_ready, 1)
                for u in range(2):
                    dve.wait_ge(proj_psum, i * 2 + u + 1)
                    dve.wait_ge(stored[u], i * 16)
                    nc.vector.tensor_tensor(y[:, u, :], ps_o[u][:, 0:D], xb[:, u, :], ALU.add).then_inc(y_ready, 1)
                c.leave(TRIPS)

        @block.scalar
        def _(act):
            act.wait_ge(loaded, 16 * LOADS)
            with act.Fori(0, B) as b:
                with act.Fori(0, NT // 2) as i:
                    for u in range(2):
                        n = b * NT + i * 2 + u
                        act.wait_ge(zT_psum, n + 1)
                        nc.scalar.copy(zT[:, u], ps_t[u][:, 0:D].rearrange("p (k t) -> p k t", k=KD)).then_inc(zT_ready, 1)
                        act.wait_ge(xp_psum, n + 1)
                        for k in range(KD):
                            nc.scalar.activation(xpT[:, k, bass.ds(b * SW + i * (2 * P) + (u * P + 1), P)],
                                                 ps_o[u][:, k * P:(k + 1) * P], ACT.Identity, bias=bp[:, k:k + 1]).then_inc(xp_ready, 1)
            act.wait_ge(xp_ready, KD * NT * B)
            by_batch = xpT[:].rearrange("p k (b s) -> p k b s", b=B)
            nc.scalar.copy(by_batch[:, :, :, 0:1], by_batch[:, :, :, S:S + 1]).then_inc(halo_ready, 1)
            nc.scalar.copy(by_batch[:, :, :, S + 1:S + 2], by_batch[:, :, :, 1:2]).then_inc(halo_ready, 1)
            act.wait_ge(halo_ready, 2)
            with act.Fori(0, B) as b:
                with act.Fori(0, NT // 2) as i:
                    t = b * (NT // 2) + i
                    for u in range(2):
                        if u == 0:
                            act.wait_ge(qkv_psum, t * 8)
                        nc.scalar.copy(win[:, u], xpT[:, :, bass.ds(b * SW + i * (2 * P) + u * P, P + 2)]).then_inc(win_ready, 1)
                    for u in range(2):
                        n = t * 2 + u
                        act.wait_ge(kv_used, t * 2)
                        for j in range(4):
                            act.wait_ge(qkv_psum, t * 8 + (4 * u + j + 1))
                            dst, src = (qraw[:, u, :], ps_q[:, 0:D]) if j == 0 else (kv[:, u, j - 1, :], ps_kv[j - 1][:])
                            nc.scalar.copy(dst, src).then_inc(kv_copied, 1)
                    for u in range(2):
                        n = t * 2 + u
                        act.wait_ge(scored, n + 1)
                        nc.scalar.activation(ex[:], sc[:], ACT.Exp, scale=scale).then_inc(exp_ready, 1)
                        act.wait_ge(oT_psum, n + 1)
                        nc.scalar.copy(oT[:, u], ps_t[u][:, 0:D].rearrange("p (k t) -> p k t", k=KD)).then_inc(oT_ready, 1)

        @block.tensor
        def _(pe):
            pe.wait_ge(loaded, 16 * LOADS)
            with pe.Fori(0, TRIPS) as t:
                for u in range(2):
                    n = t * 2 + u
                    pe.wait_ge(z_ready, n + 1)
                    for k in range(KD):
                        ins = nc.tensor.transpose(ps_t[u][:, k * P:(k + 1) * P], z[:, u, k * P:(k + 1) * P], ident[:])
                    ins.then_inc(zT_psum, 1)
                    pe.wait_ge(zT_ready, n + 1)
                    pe.wait_ge(xp_ready, t * (2 * KD))
                    for k2 in range(KD):
                        for k in range(KD):
                            ins = nc.tensor.matmul(ps_o[u][:, k2 * P:(k2 + 1) * P], wp[:, k, k2 * P:(k2 + 1) * P], zT[:, u, k, :],
                                                   start=(k == 0), stop=(k == KD - 1))
                    ins.then_inc(xp_psum, 1)
            pe.wait_ge(xp_ready, KD * NT * B)
            with pe.Fori(0, TRIPS) as t:
                for u in range(2):
                    n = t * 2 + u
                    pe.wait_ge(win_ready, n + 1)
                    for j in range(4):
                        pe.wait_ge(kv_copied, t * 8 + (j + 1 if u else 0))
                        for k in range(KD):
                            out, left, right = (ps_q[:, 0:D], win[:, u, k, 1:P + 1], wq[:, k, :]) if j == 0 else (ps_kv[j - 1][:], win[:, u, k, j - 1:j - 1 + P], wkv[:, k, :])
                            ins = nc.tensor.matmul(out, left, right, start=(k == 0), stop=(k == KD - 1))
                        ins.then_inc(qkv_psum, 1)
                for u in range(2):
                    n = t * 2 + u
                    pe.wait_ge(o_ready, n + 1)
                    for k in range(KD):
                        ins = nc.tensor.transpose(ps_t[u][:, k * P:(k + 1) * P], o[:, u, k * P:(k + 1) * P], ident[:])
                    ins.then_inc(oT_psum, 1)
                    pe.wait_ge(oT_ready, n + 1)
                    pe.wait_ge(y_ready, t * 2)
                    for k in range(KD):
                        ins = nc.tensor.matmul(ps_o[u][:, 0:D], oT[:, u, k, :], wo[:, k, :], start=(k == 0), stop=(k == KD - 1))
                    ins.then_inc(proj_psum, 1)


def mixture_of_experts(nc, x_in, consts, w, x_out, T, E, F):
    TT = 512
    ST = TT // P
    TRIPS = T // TT
    FB = F // P
    UPS = 3
    with ExitStack() as stack:
        m = Scope(nc, stack, "moe")
        ident = m.sb("ident", [P, P]); mhalf = m.sb("mhalf", [P, 1]); iota = m.sb("iota", [P, E])
        up = m.sb("up", [P, E, KD, F]); down = m.sb("down", [P, E, FB, D])
        rw = m.sb("rw", [P, KD, E]); rb = m.sb("rb", [P, E])
        acc = m.sb("acc", [P, ST, D]); z = m.sb("z", [P, ST, D]); zT = m.sb("zT", [P, KD, TT])
        st = m.sb("st", [P, ST, 6]); mv = m.sb("mv", [P, ST, 2]); ve = m.sb("ve", [P, ST]); rstd = m.sb("rstd", [P, ST])
        lg = m.sb("lg", [P, ST, E]); top = m.sb("top", [P, ST, E]); ti = m.sb("ti", [P, ST, E], U32); tf = m.sb("tf", [P, ST, 2])
        lm = m.sb("lm", [P, ST, E]); pe_ = m.sb("pexp", [P, ST, E]); sm = m.sb("sm", [P, ST]); hot = m.sb("hot", [P, 2, ST, E])
        comb = m.sb("comb", [P, ST, E])
        hT = [m.sb(f"hT{i}", [P, FB, TT]) for i in range(2)]
        ps_t = m.psum("ps_t")
        ps_up = [m.psum(f"ps_up{i}") for i in range(UPS)]
        ps_dn = [m.psum(f"ps_dn{i}") for i in range(4)]
        loaded = m.sem("loaded"); w_loaded = [m.sem(f"w_loaded{e}") for e in range(E)]
        x_loaded = m.sem("x_loaded"); var_ready = m.sem("var_ready"); rstd_ready = m.sem("rstd_ready"); z_ready = m.sem("z_ready")
        zT_psum = m.sem("zT_psum"); zT_ready = m.sem("zT_ready"); logit_psum = m.sem("logit_psum"); shifted = m.sem("shifted")
        exp_ready = m.sem("exp_ready"); chain = m.sem("chain"); up_psum = m.sem("up_psum"); h_ready = m.sem("h_ready")
        down_psum = m.sem("down_psum"); added = m.sem("added"); stored = m.sem("stored")
        LOADS = 5
        block = stack.enter_context(nc.Block())

        @block.sync
        def _(sp):
            for dst, src in ((ident[:], consts["ident"]), (mhalf[:], consts["mhalf"]), (iota[:], consts["iota8"].partition_broadcast(P)),
                             (rw[:], w["router_w"].rearrange("(k p) n -> p k n", p=P)), (rb[:], w["router_b"].partition_broadcast(P))):
                sp.dma_start(dst, src).then_inc(loaded, 16)
            for e in range(E):
                sp.dma_start(up[:, e], w["upT"][e].rearrange("(k p) f -> p k f", p=P)).then_inc(w_loaded[e], 16)
                sp.dma_start(down[:, e], w["downT"][e].rearrange("(k p) f -> p k f", p=P)).then_inc(w_loaded[e], 16)
            with sp.Fori(0, TRIPS) as i:
                sp.wait_ge(stored, i * 16)
                sp.dma_start(acc[:], x_in[bass.ds(i * TT, TT), :].rearrange("(s p) d -> p s d", p=P)).then_inc(x_loaded, 16)
                sp.wait_ge(added, (i + 1) * (E * ST))
                sp.dma_start(x_out[bass.ds(i * TT, TT), :].rearrange("(s p) d -> p s d", p=P), acc[:]).then_inc(stored, 16)
            sp.wait_ge(stored, 16 * TRIPS)

        @block.gpsimd
        def _(pool):
            pool.wait_ge(loaded, 16 * LOADS)
            with pool.Fori(0, TRIPS) as i:
                pool.wait_ge(var_ready, i + 1)
                nc.gpsimd.tensor_tensor(rstd[:], ve[:], mhalf[:].to_broadcast([P, ST]), ALU.pow).then_inc(rstd_ready, 1)

        @block.vector
        def _(dve):
            c = Chain(dve, chain)
            dve.wait_ge(loaded, 16 * LOADS)
            with dve.Fori(0, TRIPS) as i:
                c.enter(i, 13 + 2 * ST)
                dve.wait_ge(x_loaded, i * 16 + 16)
                for s in range(ST):
                    ins = nc.vector.bn_stats(st[:, s, :], acc[:, s, :])
                c.link(ins, apart=True)
                for s in range(ST):
                    ins = nc.vector.bn_aggr(mv[:, s, :], st[:, s, :])
                c.link(ins)
                nc.vector.tensor_scalar(ve[:], mv[:, :, 1], LN_EPS, None, ALU.add).then_inc(var_ready, 1)
                dve.wait_ge(rstd_ready, i + 1)
                for s in range(ST):
                    nc.vector.tensor_scalar(z[:, s, :], acc[:, s, :], mv[:, s, 0:1], rstd[:, s:s + 1], ALU.subtract, ALU.mult).then_inc(z_ready, 1)
                dve.wait_ge(logit_psum, i + 1)
                c.link(nc.vector.tensor_tensor(lg[:], ps_t[:, 0:ST * E].rearrange("p (s e) -> p s e", e=E),
                                               rb[:].unsqueeze(1).to_broadcast([P, ST, E]), ALU.add))
                c.link(nc.vector.tensor_reduce(sm[:], lg[:], AX, ALU.max))
                nc.vector.tensor_tensor(lm[:], lg[:], sm[:].unsqueeze(2).to_broadcast([P, ST, E]), ALU.subtract).then_inc(shifted, 1)
                dve.wait_ge(exp_ready, i + 1)
                c.link(nc.vector.tensor_reduce(sm[:], pe_[:], AX, ALU.add))
                c.link(nc.vector.reciprocal(sm[:], sm[:]))
                c.link(nc.vector.tensor_tensor(pe_[:], pe_[:], sm[:].unsqueeze(2).to_broadcast([P, ST, E]), ALU.mult), apart=True)
                for s in range(ST):
                    c.link(nc.vector.max(top[:, s, :], pe_[:, s, :]), apart=True)
                    c.link(nc.vector.max_index(ti[:, s, :], top[:, s, :], pe_[:, s, :]), apart=True)
                c.link(nc.vector.tensor_copy(tf[:], ti[:, :, 0:2]))
                for r in range(2):
                    c.link(nc.vector.tensor_tensor(hot[:, r], iota[:].unsqueeze(1).to_broadcast([P, ST, E]),
                                                   tf[:, :, r:r + 1].to_broadcast([P, ST, E]), ALU.is_equal))
                    c.link(nc.vector.tensor_tensor(hot[:, r], hot[:, r], top[:, :, r:r + 1].to_broadcast([P, ST, E]), ALU.mult))
                c.link(nc.vector.tensor_tensor(comb[:], hot[:, 0], hot[:, 1], ALU.add))
                for e in range(E):
                    for s in range(ST):
                        dve.wait_ge(down_psum, i * (E * ST) + (e * ST + s + 1))
                        if e > 0:
                            dve.wait_ge(added, i * (E * ST) + ((e - 1) * ST + s + 1))
                        nc.vector.scalar_tensor_tensor(acc[:, s, :], ps_dn[s][:, 0:D], comb[:, s, e:e + 1], acc[:, s, :],
                                                       ALU.mult, ALU.add).then_inc(added, 1)
                c.leave(TRIPS)

        @block.scalar
        def _(act):
            with act.Fori(0, TRIPS) as i:
                for k in range(KD):
                    act.wait_ge(zT_psum, i * KD + (k + 1))
                    nc.scalar.copy(zT[:, k, :], ps_t[:]).then_inc(zT_ready, 1)
                act.wait_ge(shifted, i + 1)
                nc.scalar.activation(pe_[:], lm[:], ACT.Exp).then_inc(exp_ready, 1)
                for e in range(E):
                    if e >= 2:
                        act.wait_ge(down_psum, i * (E * ST) + (e - 1) * ST)
                    for f in range(FB):
                        act.wait_ge(up_psum, i * (E * FB) + (e * FB + f + 1))
                        nc.scalar.activation(hT[e % 2][:, f, :], ps_up[(e * FB + f) % UPS][:], ACT.Gelu).then_inc(h_ready, 1)

        @block.tensor
        def _(pe):
            pe.wait_ge(loaded, 16 * LOADS)
            for e in range(E):
                pe.wait_ge(w_loaded[e], 32)

            def up_products(i, e):
                for f in range(FB):
                    n = e * FB + f
                    pe.wait_ge(h_ready, i * (E * FB) + max(n - UPS + 1, 0))
                    for k in range(KD):
                        ins = nc.tensor.matmul(ps_up[n % UPS][:], up[:, e, k, f * P:(f + 1) * P], zT[:, k, :],
                                               start=(k == 0), stop=(k == KD - 1))
                    ins.then_inc(up_psum, 1)

            def down_products(i, e):
                pe.wait_ge(h_ready, i * (E * FB) + (e + 1) * FB)
                for s in range(ST):
                    pe.wait_ge(added, i * (E * ST) + max((e - 1) * ST + s + 1, 0))
                    for f in range(FB):
                        ins = nc.tensor.matmul(ps_dn[s][:, 0:D], hT[e % 2][:, f, s * P:(s + 1) * P], down[:, e, f, :],
                                               start=(f == 0), stop=(f == FB - 1))
                    ins.then_inc(down_psum, 1)

            with pe.Fori(0, TRIPS) as i:
                for k in range(KD):
                    if k == 0:
                        pe.wait_ge(shifted, i)
                    else:
                        pe.wait_ge(zT_ready, i * KD + k)
                    for s in range(ST):
                        pe.wait_ge(z_ready, i * ST + (s + 1))
                        ins = nc.tensor.transpose(ps_t[:, s * P:(s + 1) * P], z[:, s, k * P:(k + 1) * P], ident[:])
                    ins.then_inc(zT_psum, 1)
                pe.wait_ge(zT_ready, (i + 1) * KD)
                for s in range(ST):
                    for k in range(KD):
                        ins = nc.tensor.matmul(ps_t[:, s * E:(s + 1) * E], zT[:, k, s * P:(s + 1) * P], rw[:, k, :],
                                               start=(k == 0), stop=(k == KD - 1))
                ins.then_inc(logit_psum, 1)
                for e in range(E):
                    up_products(i, e)
                    if e > 0:
                        down_products(i, e - 1)
                down_products(i, E - 1)


C = 32
HG = 4


def delta_consts():
    row = np.arange(P)
    b, s = row // C, row % C
    t = np.arange(C)
    same = b[:, None] == b[None, :]
    upto = same & (s[:, None] <= s[None, :])
    first_half = same & (s[:, None] < C // 2)
    cum = -(upto.astype(np.float32) - first_half.astype(np.float32))
    nb = P // C
    ends = np.zeros((P, 2, nb), np.float32)
    for j in range(nb):
        ends[(b == j) & (s < C // 2), 0, j] = -1.0
        ends[(b == j) & (s >= C // 2), 1, j] = -1.0
    strict_T = (s[:, None] < t[None, :]).astype(np.float32)
    upto_T = (s[:, None] <= t[None, :]).astype(np.float32)
    strict = (t[None, :] < s[:, None]).astype(np.float32)
    mask = np.stack([strict_T, strict_T, upto_T, strict], axis=1)
    eye = (s[:, None] == t[None, :]).astype(np.float32)
    return {"cum": cum.astype(np.float32), "ends": ends.reshape(P, 2 * nb), "mask": mask.reshape(P, 4 * C), "eye": eye}


def delta_attention(nc, x_in, consts, w, x_out, B, S, H, DH):
    DI = H * DH
    NHP = H // 2
    NCH = S // C
    NG = H // HG
    GW = HG * DH
    with ExitStack() as stack:
        m = Scope(nc, stack, "da")
        ident = m.sb("ident", [P, P]); mhalf = m.sb("mhalf", [P, 1])
        cum = m.sb("cum", [P, P]); ends = m.sb("ends", [P, 2 * B]); mask = m.sb("mask", [P, 4 * C]); eye = m.sb("eye", [P, C])
        wx = m.sb("wx", [P, KD, 5, DI]); wbg = m.sb("wbg", [P, KD, 2 * H]); wo = m.sb("wo", [P, NHP, D])
        ba = m.sb("ba", [P, 2, DI]); bbg = m.sb("bbg", [P, 2 * H]); lnw = m.sb("lnw", [P, D]); lnb = m.sb("lnb", [P, D])
        x = m.sb("x", [P, D]); z = m.sb("z", [P, D]); xz = m.sb("xz", [P, D]); xn = m.sb("xn", [P, D]); xnT = m.sb("xnT", [P, KD, P])
        st = m.sb("st", [P, 2, 6]); mv = m.sb("mv", [P, 2, 2]); ve = m.sb("ve", [P, 2]); rstd = m.sb("rstd", [P, 2])
        e = m.sb("e", [P, 2, DI])
        sp = m.sb("sp", [P, 2, DI])
        eG = m.sb("eG", [P, 2, DI]); eGn = m.sb("eGn", [P, 2, DI])
        k = m.sb("k", [P, DI]); v = m.sb("v", [P, DI]); q = m.sb("q", [P, DI]); tmp = m.sb("tmp", [P, DI])
        ss = m.sb("ss", [P, H]); ssm = m.sb("ssm", [P, H]); kinv = m.sb("kinv", [P, H])
        bg = m.sb("bg", [P, 2 * H]); bge = m.sb("bge", [P, 2 * H]); sig = m.sb("sig", [P, 2 * H]); nsig = m.sb("nsig", [P, 2 * H])
        Kb = m.sb("Kb", [P, 2, DI]); Km = m.sb("Km", [P, 2, DI]); Qp0 = m.sb("Qp0", [P, DI])
        Kprev, Qp, bv, o, oT = e[:, 0], (Qp0, q), sp[:, 1], eG[:, 0], eG[:, 1].rearrange("p (h t) -> p h t", t=P)
        FS = m.sb("FS", [P, NHP, 3, P]); FR = m.sb("FR", [P, NHP, 2, P]); FK = m.sb("FK", [P, 2, NHP, P])
        M = m.sb("M", [P, 2, NHP, B, DH])
        fac = m.sb("fac", [P, 2, NHP, 2, B]); prev_end = m.sb("prev_end", [P, 2, NHP, B]); decay = m.sb("decay", [P, 2, NHP, B])
        gm = m.sb("gm", [P, 2, 2, 2, HG // 2, 4 * C]); db = m.sb("db", [P, 2, 2, 2, HG // 2, 2, C]); dbT = m.sb("dbT", [P, 2, 2, HG // 2, C]); nn = m.sb("nn", [P, 2, 2, HG // 2, C]); TT = m.sb("TT", [P, 2, 2, 2, HG // 2, C])
        W = m.sb("W", [P, 2, 2, HG // 2, DH]); U = m.sb("U", [P, 2, 2, HG // 2, B, DH]); r = m.sb("r", [P, 2, HG // 2, DH]); y = m.sb("y", [P, D])
        pair = [m.psum(f"pair{i}", 1024) for i in range(4)]
        names = ("loaded x_loaded var_ready rstd_ready z_ready xn_ready xT_psum xT_ready proj_psum a_ready k_ready sq_ready ss_ready kinv_ready "
                 "e_ready sp_ready bg_ready bge_ready sig_ready q_ready v_ready g_ready fac_ready kb_ready kprev_ready km_ready bv_ready qp_ready "
                 "krb_ready krm_ready ft_psum ft_act ft_dve chain act_chain state_scaled decay_ready end_kept cleared gram_psum mask_done gram_ready dbl_psum y_ready w_psum w_ready part_psum "
                 "u_psum u_ready pu_psum wr_ready ds_psum s_updated ur_psum ur_ready o_psum o_ready dr_psum r_updated oT_psum oT_ready "
                 "out_psum out_ready stored xz_ready").split()
        (loaded, x_loaded, var_ready, rstd_ready, z_ready, xn_ready, xT_psum, xT_ready, proj_psum, a_ready, k_ready, sq_ready, ss_ready, kinv_ready,
         e_ready, sp_ready, bg_ready, bge_ready, sig_ready, q_ready, v_ready, g_ready, fac_ready, kb_ready, kprev_ready, km_ready, bv_ready, qp_ready,
         krb_ready, krm_ready, ft_psum, ft_act, ft_dve, chain, act_chain, state_scaled, decay_ready, end_kept, cleared, gram_psum, mask_done, gram_ready, dbl_psum, y_ready, w_psum, w_ready, part_psum,
         u_psum, u_ready, pu_psum, wr_ready, ds_psum, s_updated, ur_psum, ur_ready, o_psum, o_ready, dr_psum, r_updated, oT_psum, oT_ready,
         out_psum, out_ready, stored, xz_ready) = [m.sem(n) for n in names]

        per_head = lambda a: a.rearrange("p (h d) -> p h d", d=DH)
        over_head = lambda a, n=H: a.unsqueeze(2).to_broadcast([P, n, DH])
        LEVELS = 5
        HJ = HG // 2
        JW = HJ * DH
        gram_ps = pair[0][:].rearrange("p (q c) -> p q c", q=2)[:, :, 0:HJ * 4 * C].rearrange("p q (j c) -> p q j c", j=HJ)
        power_ps = [pair[1][:, rec * 512:rec * 512 + HG * 2 * C].rearrange("p (q j s c) -> p q j s c", q=2, j=HJ, s=2) for rec in range(2)]
        wu_ps = pair[2][:].rearrange("p (q k j e) -> p q k j e", q=2, k=4, j=HJ)
        po_ps = pair[3][:].rearrange("p (q k j e) -> p q k j e", q=2, k=4, j=HJ)
        by_head = lambda a: a.rearrange("p (j q e) -> p q j e", q=2, e=DH)

        ORDER = (("G", 0), "W0", "V0", ("G", 1), ("D", 0, 0), "U0", ("D", 0, 1), ("D", 1, 0), "W1", "I0", ("D", 1, 1), "S0",
                 ("D", 2, 0), ("D", 2, 1), "U1", ("D", 3, 0), "I1", ("D", 3, 1), "S1", ("D", 4, 0), ("D", 4, 1))
        LN_AT = (2, 8, 14)
        gram_at = lambda i, g, rec: i * (2 * NG) + (2 * g + rec + 1)
        dbl_at = lambda i, g, lvl, rec: i * (10 * NG) + (10 * g + 2 * lvl + rec + 1)
        y_at = lambda i, g, lvl, rec: i * (10 * NG) + (10 * g + 2 * lvl + rec + 1)
        once = lambda i, g: i * NG + (g + 1)
        LOADS = 18
        block = stack.enter_context(nc.Block())
        chunk_rows = lambda a, i, b: a[bass.ds(i * C + b * S, C), :]

        def every_chunk(eng, chunk):
            with eng.Fori(0, NCH - 1) as i:
                chunk(i, False)
            chunk(NCH - 1, True)

        @block.sync
        def _(sp_):
            rows_ = lambda a: a.partition_broadcast(P)
            loads = [(ident[:], consts["ident"]), (mhalf[:], consts["mhalf"]), (cum[:], consts["cum"]), (ends[:], consts["ends"]),
                     (mask[:], consts["mask"]), (eye[:], consts["eye"]),
                     (wbg[:], w["WbgT"].rearrange("(k p) n -> p k n", p=P)), (wo[:], w["WoT"].rearrange("(k p) n -> p k n", p=P)),
                     (ba[:, 0], rows_(w["ba"])), (ba[:, 1], rows_(w["baR"])), (bbg[:], rows_(w["bbg"])), (lnw[:], rows_(w["ln_w"])), (lnb[:], rows_(w["ln_b"]))]
            loads += [(wx[:, :, j], w[n].rearrange("(k p) n -> p k n", p=P)) for j, n in enumerate(("WaT", "WaRT", "WkT", "WqT", "WvT"))]
            assert len(loads) == LOADS
            for dst, src in loads:
                sp_.dma_start(dst, src).then_inc(loaded, 16)

            def load_x(i):
                for b in range(B):
                    sp_.dma_start(x[b * C:(b + 1) * C, :], chunk_rows(x_in, i, b)).then_inc(x_loaded, 16)

            def chunk(i, last):
                if not last:
                    sp_.wait_ge(xz_ready, i + 1)
                    load_x(i + 1)
                sp_.wait_ge(out_ready, i + 1)
                for b in range(B):
                    sp_.dma_start(chunk_rows(x_out, i, b), y[b * C:(b + 1) * C, :]).then_inc(stored, 16)

            load_x(0)
            every_chunk(sp_, chunk)
            sp_.wait_ge(stored, 16 * B * NCH)

        @block.gpsimd
        def _(pool):
            pool.wait_ge(loaded, 16 * LOADS)

            def norms(i):
                for n in range(2):
                    pool.wait_ge(var_ready, i * 2 + (n + 1))
                    nc.gpsimd.tensor_tensor(rstd[:, n:n + 1], ve[:, n:n + 1], mhalf[:], ALU.pow).then_inc(rstd_ready, 1)

            def chunk(i, last):
                pool.wait_ge(z_ready, i + 1)
                pool.wait_ge(out_ready, i)
                nc.gpsimd.tensor_tensor(xz[:], x[:], z[:], ALU.add).then_inc(xz_ready, 1)
                pool.wait_ge(ss_ready, i + 1)
                nc.gpsimd.tensor_tensor(kinv[:], ssm[:], mhalf[:].to_broadcast([P, H]), ALU.pow).then_inc(kinv_ready, 1)
                pool.wait_ge(v_ready, i + 1)
                pool.wait_ge(sig_ready, i * 2 + 2)
                pool.wait_ge(fac_ready, i * 2 + 2)
                nc.gpsimd.tensor_tensor(per_head(bv), per_head(v[:]), over_head(sig[:, 0:H]), ALU.mult).then_inc(bv_ready, 1)
                pool.wait_ge(q_ready, i + 1)
                for rec in range(2):
                    pool.wait_ge(g_ready, i * 4 + 2 * rec + 1)
                    pool.wait_ge(qp_ready, i * 2 + rec)
                    nc.gpsimd.tensor_tensor(Qp[rec][:], q[:], eG[:, rec], ALU.mult).then_inc(qp_ready, 1)
                nc.gpsimd.tensor_tensor(decay[:], fac[:, :, :, 0, :], prev_end[:], ALU.mult).then_inc(decay_ready, 1)
                pool.wait_ge(decay_ready, i + 1)
                pool.wait_ge(r_updated, i * NG)
                for rec in range(2):
                    st_ = M[:, rec].rearrange("p a b c -> p (a b) c")
                    nc.gpsimd.tensor_tensor(st_, st_, decay[:, rec].rearrange("p a b -> p (a b)").unsqueeze(2).to_broadcast([P, NHP * B, DH]), ALU.mult).then_inc(state_scaled, 1)
                nc.gpsimd.tensor_copy(prev_end[:], fac[:, :, :, 1, :]).then_inc(end_kept, 1)
                pool.wait_ge(end_kept, i + 1)
                if not last:
                    norms(i + 1)

            norms(0)
            pool.wait_ge(cleared, 1)
            every_chunk(pool, chunk)

        @block.vector
        def _(dve):
            c = Chain(dve, chain)
            c.link(nc.vector.memset(M[:].rearrange("p a b c d -> p (a b c d)"), 0.0))
            c.link(nc.vector.memset(U[:].rearrange("p a b c d e -> p (a b c d e)"), 0.0))
            nc.vector.memset(prev_end[:].rearrange("p a b c -> p (a b c)"), 1.0).then_inc(cleared, 1)
            dve.wait_ge(loaded, 16 * LOADS)

            flat = lambda a: a.rearrange("p q j c -> p (q j c)")

            def gram_mask(i, g, rec):
                lo = 0 if rec == 0 else C
                dve.wait_ge(gram_psum, gram_at(i, g, rec))
                for q_ in range(2):
                    ins = nc.vector.tensor_tensor(gm[:, rec, g % 2, q_, :, lo:3 * C], gram_ps[:, q_, :, lo:3 * C],
                                                  mask[:, lo:3 * C].unsqueeze(1).to_broadcast([P, HJ, 3 * C - lo]), ALU.mult)
                ins.then_inc(mask_done, 1)
                dve.wait_ge(mask_done, gram_at(i, g, rec))
                c.link(nc.vector.transpose(nn[:, rec], gm[:, rec, g % 2, :, :, C:2 * C]))
                nc.vector.tensor_tensor(db[:, rec, 0, :, :, 1, :], nn[:, rec], eye[:].unsqueeze(1).unsqueeze(1).to_broadcast([P, 2, HJ, C]), ALU.add).then_inc(gram_ready, 1)

            def powers(i, g, lvl, rec):
                dve.wait_ge(dbl_psum, dbl_at(i, g, lvl, rec))
                out = power_ps[rec]
                if lvl > 0:
                    last = lvl == LEVELS - 1
                    ins = nc.vector.tensor_tensor(nn[:, rec] if last else db[:, rec, lvl % 2, :, :, 1, :], db[:, rec, (lvl - 1) % 2, :, :, 1, :], out[:, :, :, 1, :], ALU.add)
                    if last:
                        c.link(ins)
                        nc.vector.transpose(TT[:, rec, g % 2], nn[:, rec]).then_inc(y_ready, 1)
                        return
                nc.vector.tensor_copy(db[:, rec, lvl % 2, :, :, 0, :], out[:, :, :, 0, :])
                nc.vector.transpose(dbT[:, rec], out[:, :, :, 0, :]).then_inc(y_ready, 1)

            def add_bv(i, g):
                dve.wait_ge(w_psum, once(i, g))
                nc.vector.tensor_tensor(W[:, 0], wu_ps[:, :, 0], by_head(bv[:, g * GW:(g + 1) * GW]), ALU.add).then_inc(w_ready, 1)

            def clipped(i, g):
                dve.wait_ge(pu_psum, once(i, g))
                gamma = sig[:, H + g * HG:H + (g + 1) * HG].rearrange("p (j q) -> p q j", q=2).unsqueeze(3).to_broadcast([P, 2, HJ, DH])
                c.link(nc.vector.tensor_tensor(r[:], by_head(v[:, g * GW:(g + 1) * GW]), po_ps[:, :, 0], ALU.subtract))
                c.link(nc.vector.tensor_scalar(r[:], r[:], 1.0, -1.0, ALU.min, ALU.max))
                c.link(nc.vector.tensor_tensor(r[:], r[:], gamma, ALU.mult))
                nc.vector.tensor_tensor(W[:, 1], wu_ps[:, :, 1], r[:], ALU.add).then_inc(wr_ready, 1)

            def update(i, g, rec):
                dve.wait_ge((ds_psum, dr_psum)[rec], once(i, g))
                st_ = M[:, rec, 2 * g:2 * g + 2].rearrange("p a b c -> p (a b c)")
                nc.vector.tensor_tensor(st_, pair[0][:, rec * 512:(rec + 1) * 512], st_, ALU.add).then_inc((s_updated, r_updated)[rec], 1)

            def layer_norms(i, step):
                def variance(n, src):
                    c.link(nc.vector.bn_stats(st[:, n], src[:]), apart=True)
                    c.link(nc.vector.bn_aggr(mv[:, n], st[:, n]))
                    nc.vector.tensor_scalar(ve[:, n:n + 1], mv[:, n, 1:2], LN_EPS, None, ALU.add).then_inc(var_ready, 1)

                if step == 0:
                    dve.wait_ge(x_loaded, i * (16 * B) + 16 * B)
                    variance(0, x)
                elif step == 1:
                    dve.wait_ge(rstd_ready, i * 2 + 1)
                    dve.wait_ge(xz_ready, i)
                    nc.vector.tensor_scalar(z[:], x[:], mv[:, 0, 0:1], rstd[:, 0:1], ALU.subtract, ALU.mult).then_inc(z_ready, 1)
                    dve.wait_ge(z_ready, i + 1)
                    variance(1, z)
                else:
                    dve.wait_ge(rstd_ready, i * 2 + 2)
                    dve.wait_ge(xT_psum, i)
                    c.link(nc.vector.tensor_scalar(xn[:], z[:], mv[:, 1, 0:1], rstd[:, 1:2], ALU.subtract, ALU.mult))
                    c.link(nc.vector.tensor_tensor(xn[:], xn[:], lnw[:], ALU.mult))
                    nc.vector.tensor_tensor(xn[:], xn[:], lnb[:], ALU.add).then_inc(xn_ready, 1)

            def chunk(i, last):
                for rec in range(2):
                    dve.wait_ge(proj_psum, i * 9 + (rec + 1))
                    nc.vector.tensor_tensor(sp[:, rec], pair[rec][:], ba[:, rec], ALU.add).then_inc(a_ready, 1)
                dve.wait_ge(sq_ready, i + 1)
                c.link(nc.vector.tensor_reduce(ss[:], per_head(tmp[:]), AX, ALU.add))
                nc.vector.tensor_scalar(ssm[:], ss[:], 1e-24, None, ALU.max).then_inc(ss_ready, 1)
                dve.wait_ge(proj_psum, i * 9 + 4)
                nc.vector.tensor_tensor(bg[:], pair[3][:, 256:256 + 2 * H], bbg[:], ALU.add).then_inc(bg_ready, 1)
                dve.wait_ge(bge_ready, i + 1)
                c.link(nc.vector.tensor_scalar(bge[:], bge[:], 1.0, None, ALU.add))
                nc.vector.reciprocal(sig[:], bge[:]).then_inc(sig_ready, 1)
                dve.wait_ge(sig_ready, i * 2 + 1)
                nc.vector.tensor_scalar(nsig[:], sig[:], -1.0, None, ALU.mult).then_inc(sig_ready, 1)
                dve.wait_ge(kinv_ready, i + 1)
                dve.wait_ge(sig_ready, i * 2 + 2)
                c.link(nc.vector.tensor_tensor(per_head(k[:]), per_head(k[:]), over_head(kinv[:]), ALU.mult))
                for rec in range(2):
                    dve.wait_ge(g_ready, i * 4 + 2 * rec + 1)
                    c.link(nc.vector.tensor_tensor(tmp[:], eG[:, rec], k[:], ALU.mult))
                    nc.vector.tensor_tensor(per_head(Kb[:, rec]), per_head(tmp[:]), over_head(nsig[:, rec * H:(rec + 1) * H]), ALU.mult).then_inc(kb_ready, 1)
                    if rec == 0:
                        c.link(nc.vector.scalar_tensor_tensor(Kprev, e[:, 0], 1.0, tmp[:], ALU.add, ALU.mult))
                    dve.wait_ge(g_ready, i * 4 + 2 * rec + 2)
                    nc.vector.tensor_tensor(Km[:, rec], eGn[:, rec], k[:], ALU.mult).then_inc(km_ready, 1)
                dve.wait_ge(ft_psum, i * 7 + 4)
                nc.vector.tensor_copy(FS[:, :, 2, :], pair[3][:].rearrange("p (h t) -> p h t", t=P)).then_inc(ft_dve, 1)
                dve.wait_ge(ft_psum, i * 7 + 7)
                nc.vector.tensor_copy(FR[:, :, 1, :], pair[2][:].rearrange("p (h t) -> p h t", t=P)).then_inc(ft_dve, 1)
                for slot in range(NG + 1):
                    g, s = slot, slot - 1
                    for at, what in enumerate(ORDER):
                        if slot == 2 and not last and at in LN_AT:
                            layer_norms(i + 1, LN_AT.index(at))
                        if what[0] in "GD":
                            if g >= NG:
                                continue
                            if what[0] == "G":
                                gram_mask(i, g, what[1])
                            else:
                                powers(i, g, what[1], what[2])
                        elif s >= 0:
                            if what == "W0":
                                if s == 0:
                                    dve.wait_ge(bv_ready, i + 1)
                                add_bv(i, s)
                            elif what == "I0":
                                clipped(i, s)
                            elif what[0] == "S":
                                update(i, s, int(what[1]))
                dve.wait_ge(out_psum, i + 1)
                dve.wait_ge(stored, i * (16 * B))
                nc.vector.tensor_tensor(y[:], pair[1][:, 0:D], xz[:], ALU.add).then_inc(out_ready, 1)

            for step in range(3):
                layer_norms(0, step)
            with dve.Fori(0, NCH - 1) as i:
                c.enter(i, 40)
                chunk(i, False)
                c.leave(NCH - 1)
            chunk(NCH - 1, True)

        @block.scalar
        def _(act):
            def copy_u(i, g, rec):
                act.wait_ge((u_psum, ur_psum)[rec], once(i, g))
                for b in range(B):
                    ins = nc.scalar.copy(U[b * C:(b + 1) * C, rec, :, :, b, :], wu_ps[b * C:(b + 1) * C, :, 2 + rec])
                ins.then_inc((u_ready, ur_ready)[rec], 1)

            def copy_xT(i):
                act.wait_ge(xT_psum, i + 1)
                nc.scalar.copy(xnT[:], pair[3][:, 0:D].rearrange("p (k t) -> p k t", k=KD)).then_inc(xT_ready, 1)

            def chunk(i, last):
                act.wait_ge(proj_psum, i * 9 + 3)
                nc.scalar.copy(k[:], pair[2][:]).then_inc(k_ready, 1)
                nc.scalar.activation(tmp[:], pair[2][:], ACT.Square).then_inc(sq_ready, 1)
                act.wait_ge(bg_ready, i + 1)
                nc.scalar.activation(bge[:], bg[:], ACT.Exp, scale=-1.0).then_inc(bge_ready, 1)
                for rec in range(2):
                    act.wait_ge(a_ready, i * 2 + (rec + 1))
                    nc.scalar.activation(e[:, rec], sp[:, rec], ACT.Exp, scale=-1.0).then_inc(e_ready, 1)
                for rec in range(2):
                    act.wait_ge(e_ready, i * 2 + (rec + 1))
                    nc.scalar.activation(sp[:, rec], e[:, rec], ACT.Ln, bias=1.0).then_inc(sp_ready, 1)
                act.wait_ge(proj_psum, i * 9 + 5)
                nc.scalar.copy(q[:], pair[0][:]).then_inc(q_ready, 1)
                act.wait_ge(proj_psum, i * 9 + 6)
                nc.scalar.copy(v[:], pair[1][:]).then_inc(v_ready, 1)
                for rec in range(2):
                    act.wait_ge(proj_psum, i * 9 + (7 + rec))
                    nc.scalar.activation(eG[:, rec], pair[2 + rec][:], ACT.Exp).then_inc(g_ready, 1)
                    nc.scalar.activation(eGn[:, rec], pair[2 + rec][:], ACT.Exp, scale=-1.0).then_inc(g_ready, 1)
                act.wait_ge(proj_psum, i * 9 + 9)
                for rec in range(2):
                    nc.scalar.activation(fac[:, rec].rearrange("p a b c -> p (a b c)"), pair[0][:, rec * 512:rec * 512 + NHP * 2 * B], ACT.Exp).then_inc(fac_ready, 1)
                for n, dst in ((0, FS[:, :, 1, :]), (1, FS[:, :, 0, :]), (2, FK[:, 0]), (4, FR[:, :, 0, :]), (5, FK[:, 1])):
                    act.wait_ge(ft_psum, i * 7 + (n + 1))
                    nc.scalar.copy(dst, pair[n % 4][:].rearrange("p (h t) -> p h t", t=P)).then_inc(ft_act, 1)
                for s in range(NG):
                    copy_u(i, s, 0)
                    copy_u(i, s, 1)
                    act.wait_ge(o_psum, once(i, s))
                    nc.scalar.copy(by_head(o[:, s * GW:(s + 1) * GW]), po_ps[:, :, 1]).then_inc(o_ready, 1)
                act.wait_ge(oT_psum, i + 1)
                nc.scalar.copy(oT, pair[0][:].rearrange("p (h t) -> p h t", t=P)).then_inc(oT_ready, 1)
                if not last:
                    copy_xT(i + 1)

            act.wait_ge(loaded, 16 * LOADS)
            copy_xT(0)
            every_chunk(act, chunk)

        @block.tensor
        def _(pe):
            mm = nc.tensor.matmul

            apart = lambda sem, at: wait_apart(pe, sem, at)

            heads = [(b, q_, j) for j in range(HJ) for q_ in range(2) for b in range(B)]
            rows_of = lambda b: slice(b * C, (b + 1) * C)
            feat = lambda q_: slice(DH * q_, DH * (q_ + 1))

            def gram(i, g, rec):
                F = (FS, FR)[rec]
                lo = 0 if rec == 0 else 1
                for b, q_, j in heads:
                    f, hp, rw = feat(q_), g * HJ + j, rows_of(b)
                    ins = mm(gram_ps[rw, q_, j, lo * C:3 * C], FK[f, rec, hp, rw], F[f, hp, lo - rec:3 - rec, rw], start=True, stop=True)
                ins.then_inc(gram_psum, 1)

            def double(i, g, lvl, rec):
                if lvl == 0:
                    apart(gram_ready, gram_at(i, g, rec))
                    apart(y_ready, i * (10 * NG) + 10 * g)
                else:
                    apart(y_ready, y_at(i, g, lvl - 1, rec))
                for b, q_, j in heads:
                    rw = rows_of(b)
                    out = power_ps[rec][rw, q_, j]
                    if lvl == 0:
                        ins = mm(out[:, 0, :], gm[rw, rec, g % 2, q_, j, C:2 * C], nn[rw, rec, q_, j], start=True, stop=True)
                    else:
                        lo = 1 if lvl == LEVELS - 1 else 0
                        ins = mm(out[:, lo:2, :], dbT[rw, rec, q_, j], db[rw, rec, (lvl - 1) % 2, q_, j, lo:2, :], start=True, stop=True)
                ins.then_inc(dbl_psum, 1)

            def state_w(i, g, rec):
                if rec == 0:
                    apart(ur_ready, i * NG + g)
                else:
                    apart(u_ready, once(i, g))
                F = (FS, FR)[rec]
                for b, q_, j in heads:
                    f, hp, rw = feat(q_), g * HJ + j, rows_of(b)
                    ins = mm(wu_ps[rw, q_, rec, j], F[f, hp, 1 - rec, rw], M[f, rec, hp, b, :], start=True, stop=True)
                if rec == 0:
                    ins.then_inc(w_psum, 1)

            def state_parts(i, g, rec):
                apart(o_ready, i * NG + g)
                for b, q_, j in heads:
                    f, hp, rw = feat(q_), g * HJ + j, rows_of(b)
                    mm(po_ps[rw, q_, 0, j], FS[f, hp, 0, rw], M[f, 0, hp, b, :], start=(j == 0), stop=False, skip_group_check=True)
                for b, q_, j in heads:
                    f, hp, rw = feat(q_), g * HJ + j, rows_of(b)
                    mm(po_ps[rw, q_, 1, j], FS[f, hp, 2, rw], M[f, 0, hp, b, :], start=False, stop=False, skip_group_check=True)
                    mm(po_ps[rw, q_, 1, j], FR[f, hp, 1, rw], M[f, 1, hp, b, :], start=False, stop=False, skip_group_check=True)

            def solve(i, g, rec):
                apart((w_ready, wr_ready)[rec], once(i, g))
                apart(y_ready, y_at(i, g, LEVELS - 1, rec))
                for b, q_, j in heads:
                    rw = rows_of(b)
                    ins = mm(wu_ps[rw, q_, 2 + rec, j], TT[rw, rec, g % 2, q_, j], W[rw, rec, q_, j], start=True, stop=True)
                ins.then_inc((u_psum, ur_psum)[rec], 1)

            def inner_parts(i, g, rec):
                apart((u_ready, ur_ready)[rec], once(i, g))
                for b, q_, j in heads:
                    rw = rows_of(b)
                    G = gm[rw, rec, g % 2, q_, j]
                    if rec == 0:
                        mm(po_ps[rw, q_, 0, j], G[:, 0:C], U[rw, 0, q_, j, b], start=False, stop=True, skip_group_check=True)
                    ins = mm(po_ps[rw, q_, 1, j], G[:, 2 * C:3 * C], U[rw, rec, q_, j, b], start=False, stop=(rec == 1), skip_group_check=True)
                ins.then_inc((pu_psum, o_psum)[rec], 1)

            def state_update(i, g, rec):
                for q_ in range(2):
                    for j in range(HJ):
                        col = (g * HG + 2 * j + q_) * DH
                        ins = mm(pair[0][feat(q_), rec * 512 + j * B * DH:rec * 512 + (j + 1) * B * DH], Km[:, rec, col:col + DH],
                                 U[:, rec, q_, j].rearrange("p b e -> p (b e)"), start=True, stop=True)
                ins.then_inc((ds_psum, dr_psum)[rec], 1)

            def project(out, j, n0):
                for half in range(2):
                    for kk in range(KD):
                        ins = mm(out[:, half * 512:(half + 1) * 512], xnT[:, kk, :], wx[:, kk, j, half * 512:(half + 1) * 512], start=(kk == 0), stop=(kk == KD - 1))
                ins.then_inc(proj_psum, 1)

            def transpose_x(i):
                pe.wait_ge(xn_ready, i + 1)
                for kk in range(KD):
                    ins = nc.tensor.transpose(pair[3][:, kk * P:(kk + 1) * P], xn[:, kk * P:(kk + 1) * P], ident[:])
                ins.then_inc(xT_psum, 1)

            def chunk(i, last):
                pe.wait_ge(xT_ready, i + 1)
                project(pair[0], 0, 0)
                pe.wait_ge(out_ready, i)
                project(pair[1], 1, 0)
                project(pair[2], 2, 0)
                for kk in range(KD):
                    ins = mm(pair[3][:, 256:256 + 2 * H], xnT[:, kk, :], wbg[:, kk, :], start=(kk == 0), stop=(kk == KD - 1))
                ins.then_inc(proj_psum, 1)
                pe.wait_ge(a_ready, i * 2 + 1)
                project(pair[0], 3, 0)
                pe.wait_ge(a_ready, i * 2 + 2)
                project(pair[1], 4, 0)
                pe.wait_ge(sq_ready, i + 1)
                pe.wait_ge(bg_ready, i + 1)
                for rec in range(2):
                    pe.wait_ge(sp_ready, i * 2 + (rec + 1))
                    for half in range(2):
                        ins = mm(pair[2 + rec][:, half * 512:(half + 1) * 512], cum[:], sp[:, rec, half * 512:(half + 1) * 512], start=True, stop=True)
                    ins.then_inc(proj_psum, 1)
                pe.wait_ge(q_ready, i + 1)
                for rec in range(2):
                    for hp in range(NHP):
                        ins = mm(pair[0][:, rec * 512 + hp * 2 * B:rec * 512 + (hp + 1) * 2 * B], sp[:, rec, hp * P:(hp + 1) * P], ends[:], start=True, stop=True)
                ins.then_inc(proj_psum, 1)
                for n, (src, ready) in enumerate((
                        (Kb[:, 0], [(kb_ready, i * 2 + 1), (fac_ready, i * 2 + 2)]), (Kprev, [(km_ready, i * 2 + 1), (v_ready, i + 1)]),
                        (Km[:, 0], [(km_ready, i * 2 + 1), (g_ready, i * 4 + 2)]), (Qp[0], [(qp_ready, i * 2 + 1), (g_ready, i * 4 + 4)]),
                        (Kb[:, 1], [(kb_ready, i * 2 + 2), (ft_act, i * 5 + 1)]), (Km[:, 1], [(km_ready, i * 2 + 2), (ft_act, i * 5 + 2)]),
                        (Qp[1], [(qp_ready, i * 2 + 2), (ft_act, i * 5 + 3)]))):
                    for sem, at in ready:
                        pe.wait_ge(sem, at)
                    for hp in range(NHP):
                        ins = nc.tensor.transpose(pair[n % 4][:, hp * P:(hp + 1) * P], src[:, hp * P:(hp + 1) * P], ident[:])
                    ins.then_inc(ft_psum, 1)
                pe.wait_ge(ft_act, i * 5 + 5)
                pe.wait_ge(ft_dve, i * 2 + 2)
                for slot in range(NG + 1):
                    g, s = slot, slot - 1
                    if slot == 1:
                        apart(state_scaled, i * 2 + 2)
                    for what in ORDER:
                        if what[0] in "GD":
                            if g >= NG:
                                continue
                            if what[0] == "D":
                                double(i, g, what[1], what[2])
                                continue
                            apart(*((r_updated, i * NG + max(s, 0)) if what[1] == 0 else (mask_done, gram_at(i, g, 0))))
                            gram(i, g, what[1])
                        elif s >= 0:
                            rec = int(what[1])
                            if what[0] == "S" and rec == 0:
                                apart(mask_done, gram_at(i, min(g, NG - 1), 1))
                            {"W": state_w, "V": state_parts, "U": solve, "I": inner_parts, "S": state_update}[what[0]](i, s, rec)
                pe.wait_ge(r_updated, (i + 1) * NG)
                pe.wait_ge(o_ready, (i + 1) * NG)
                for hp in range(NHP):
                    ins = nc.tensor.transpose(pair[0][:, hp * P:(hp + 1) * P], o[:, hp * P:(hp + 1) * P], ident[:])
                ins.then_inc(oT_psum, 1)
                if not last:
                    transpose_x(i + 1)
                pe.wait_ge(oT_ready, i + 1)
                for hp in range(NHP):
                    ins = mm(pair[1][:, 0:D], oT[:, hp, :], wo[:, hp, :], start=(hp == 0), stop=(hp == NHP - 1))
                ins.then_inc(out_psum, 1)

            pe.wait_ge(loaded, 16 * LOADS)
            transpose_x(0)
            every_chunk(pe, chunk)


FP4_BLOCK = 16
FP4_MAX = 6.0


def fp4_feed_forward(nc, x_in, consts, w, x_out, T, I):
    IC = -(-I // P)
    HI = I // 2
    NT = T // P
    UN = 4
    TRIPS = NT // UN
    with ExitStack() as stack:
        m = Scope(nc, stack, "ff")
        ident = m.sb("ident", [P, P]); mhalf = m.sb("mhalf", [P, 1])
        guT = [m.sb(f"guT{j}", [P, KD, I]) for j in range(2)]
        downT = m.sb("downT", [P, IC, D])
        x = m.sb("x", [P, UN, D]); y = m.sb("y", [P, UN, D]); z = m.sb("z", [P, UN, D]); zqT = m.sb("zqT", [P, UN, KD, P])
        st = m.sb("st", [P, UN, 6]); mv = m.sb("mv", [P, UN, 2]); ve = m.sb("ve", [P, UN, 1]); rstd = m.sb("rstd", [P, UN, 1])
        raw = m.sb("raw", [P, UN, I]); mag = m.sb("mag", [P, UN, I]); sgn = m.sb("sgn", [P, UN, I])
        ratio = m.sb("ratio", [P, I]); level = m.sb("level", [P, I]); above = m.sb("above", [P, I]); qz = m.sb("qz", [P, UN, D]); qh = m.sb("qh", [P, UN, I])
        amax = m.sb("amax", [P, I // FP4_BLOCK]); scl = m.sb("scl", [P, I // FP4_BLOCK]); inv = m.sb("inv", [P, I // FP4_BLOCK])
        silu = m.sb("silu", [P, UN, I]); hqT = m.sb("hqT", [P, UN, IC, P])
        ps_z = m.psum("ps_z"); ps_h = [m.psum(f"ps_h{i}") for i in range(2)]
        ps_g = [m.psum(f"ps_g{i}") for i in range(2)]; ps_u = [m.psum(f"ps_u{i}") for i in range(2)]; ps_y = m.psum("ps_y")
        loaded = m.sem("loaded"); w_loaded = [m.sem(f"w_loaded{i}") for i in range(2)]; w_signs = m.sem("w_signs"); w_quantised = m.sem("w_quantised")
        wT_psum = m.sem("wT_psum"); wT_ready = m.sem("wT_ready"); chain = m.sem("chain")
        x_loaded = [m.sem(f"x_loaded{i}") for i in range(UN)]; var_ready = m.sem("var_ready"); rstd_ready = m.sem("rstd_ready")
        z_ready = m.sem("z_ready"); z_signs = m.sem("z_signs"); qz_ready = m.sem("qz_ready"); zT_psum = m.sem("zT_psum")
        zT_ready = m.sem("zT_ready"); gu_psum = m.sem("gu_psum"); silu_ready = m.sem("silu_ready"); h_ready = m.sem("h_ready")
        h_signs = m.sem("h_signs"); qh_ready = m.sem("qh_ready"); hT_psum = m.sem("hT_psum"); hT_ready = m.sem("hT_ready")
        y_psum = m.sem("y_psum"); y_ready = m.sem("y_ready"); stored = [m.sem(f"stored{i}") for i in range(UN)]

        items = []
        for j, name in enumerate(("w_gate", "w_up")):
            for r in range(IC):
                n = min(P, I - r * P)
                items.append((w[name][r * P:r * P + n, :], n, D, [guT[j][:, k, r * P:r * P + n] for k in range(KD)]))
        for r in range(KD):
            items.append((w["w_down"][r * P:(r + 1) * P, :], P, I,
                          [downT[0:min(P, I - k * P), k, r * P:(r + 1) * P] for k in range(IC)]))

        block = stack.enter_context(nc.Block())

        @block.sync
        def _(sp):
            for dst, src in ((ident[:], consts["ident"]), (mhalf[:], consts["mhalf"])):
                sp.dma_start(dst, src).then_inc(loaded, 16)
            for n, (src, rows_, cols, _) in enumerate(items):
                if n >= 2:
                    sp.wait_ge(w_signs, n - 1)
                sp.dma_start(raw[0:rows_, n % 2, 0:cols], src).then_inc(w_loaded[n % 2], 16)

            def load_x(i, u):
                sp.dma_start(x[:, u, :], x_in[bass.ds(i * (UN * P) + u * P, P), :]).then_inc(x_loaded[u], 16)

            def store_y(i, u):
                sp.wait_ge(y_ready, i * UN + (u + 1))
                sp.dma_start(x_out[bass.ds(i * (UN * P) + u * P, P), :], y[:, u, :]).then_inc(stored[u], 16)

            for u in range(UN):
                load_x(0, u)
            with sp.Fori(0, TRIPS - 1) as i:
                for u in range(UN):
                    store_y(i, u)
                    load_x(i + 1, u)
            for u in range(UN):
                store_y(TRIPS - 1, u)
            for u in range(UN):
                sp.wait_ge(stored[u], 16 * TRIPS)

        @block.gpsimd
        def _(pool):
            pool.wait_ge(loaded, 32)
            with pool.Fori(0, TRIPS) as i:
                for u in range(UN):
                    pool.wait_ge(var_ready, i * UN + (u + 1))
                    nc.gpsimd.tensor_tensor(rstd[:, u, :], ve[:, u, :], mhalf[:], ALU.pow).then_inc(rstd_ready, 1)

        @block.vector
        def _(dve):
            c = Chain(dve, chain)

            def fp4(n, cols, magnitude, sign, out, done):
                nb = cols // FP4_BLOCK
                blocks = lambda a: a.rearrange("p (b e) -> p b e", e=FP4_BLOCK)
                per_block = lambda a: a[0:n, 0:nb].unsqueeze(2).to_broadcast([n, nb, FP4_BLOCK])
                r, l, a = ratio[0:n, 0:cols], level[0:n, 0:cols], above[0:n, 0:cols]
                c.link(nc.vector.tensor_reduce(amax[0:n, 0:nb], blocks(magnitude), AX, ALU.max))
                c.link(nc.vector.tensor_scalar(scl[0:n, 0:nb], amax[0:n, 0:nb], 1.0 / FP4_MAX, 1e-12, ALU.mult, ALU.max))
                c.link(nc.vector.reciprocal(inv[0:n, 0:nb], scl[0:n, 0:nb]))
                c.link(nc.vector.tensor_tensor(blocks(r), blocks(magnitude), per_block(inv), ALU.mult))
                nc.vector.tensor_scalar(a, r, 0.25, None, ALU.is_gt)
                c.link(nc.vector.tensor_scalar(l, r, 5.0, 2.0, ALU.is_gt, ALU.mult))
                for at in (3.5, 2.5):
                    c.link(nc.vector.scalar_tensor_tensor(l, r, at, l, ALU.is_gt, ALU.add))
                c.link(nc.vector.scalar_tensor_tensor(l, l, 2.0, a, ALU.mult, ALU.add))
                for at in (1.75, 1.25, 0.75):
                    c.link(nc.vector.scalar_tensor_tensor(l, r, at, l, ALU.is_gt, ALU.add))
                c.link(nc.vector.scalar_tensor_tensor(blocks(l), blocks(l), 0.5, per_block(scl), ALU.mult, ALU.mult))
                nc.vector.tensor_tensor(out, l, sign, ALU.mult).then_inc(done, 1)

            QL = 12
            for n, (_, rows_, cols, _) in enumerate(items):
                dve.wait_ge(w_signs, n + 1)
                if n >= 2:
                    dve.wait_ge(wT_psum, n - 1)
                fp4(rows_, cols, mag[0:rows_, n % 2, 0:cols], sgn[0:rows_, n % 2, 0:cols], qh[0:rows_, n % 2, 0:cols], w_quantised)

            def norm(i):
                for u in range(UN):
                    dve.wait_ge(x_loaded[u], i * 16 + 16)
                    ins = nc.vector.bn_stats(st[:, u, :], x[:, u, :])
                c.link(ins, apart=True)
                for u in range(UN):
                    ins = nc.vector.bn_aggr(mv[:, u, :], st[:, u, :])
                c.link(ins)
                for u in range(UN):
                    nc.vector.tensor_scalar(ve[:, u, :], mv[:, u, 1:2], LN_EPS, None, ALU.add).then_inc(var_ready, 1)
                for u in range(UN):
                    dve.wait_ge(rstd_ready, i * UN + (u + 1))
                    nc.vector.tensor_scalar(z[:, u, :], x[:, u, :], mv[:, u, 0:1], rstd[:, u, :], ALU.subtract, ALU.mult).then_inc(z_ready, 1)

            def round_z(i, u):
                dve.wait_ge(z_signs, i * UN + (u + 1))
                fp4(P, D, mag[:, u, 0:D], sgn[:, u, 0:D], qz[:, u, :], qz_ready)

            def hidden(i, u):
                dve.wait_ge(silu_ready, i * UN + (u + 1))
                for j in range(2):
                    nc.vector.tensor_tensor(raw[:, u, j * HI:(j + 1) * HI], silu[:, u, j * HI:(j + 1) * HI], ps_u[j][:, 0:HI], ALU.mult).then_inc(h_ready, 1)

            def round_h(i, u):
                dve.wait_ge(h_signs, i * UN + (u + 1))
                fp4(P, I, mag[:, u, :], sgn[:, u, :], qh[:, u, :], qh_ready)

            def result(i, u):
                dve.wait_ge(y_psum, i * UN + (u + 1))
                dve.wait_ge(stored[u], i * 16)
                nc.vector.tensor_tensor(y[:, u, :], ps_y[:, 0:D], x[:, u, :], ALU.add).then_inc(y_ready, 1)

            with dve.Fori(0, TRIPS) as i:
                c.enter(i, 2 + 2 * UN * QL)
                norm(i)
                for step, u in ((round_z, 0), (round_z, 1), (hidden, 0), (round_z, 2), (round_h, 0), (hidden, 1), (round_z, 3), (round_h, 1),
                                (result, 0), (hidden, 2), (round_h, 2), (result, 1), (hidden, 3), (round_h, 3), (result, 2), (result, 3)):
                    step(i, u)
                c.leave(TRIPS)

        @block.scalar
        def _(act):
            for n, (_, rows_, cols, dst) in enumerate(items):
                act.wait_ge(w_loaded[n % 2], 16 * (n // 2 + 1))
                if n >= 2:
                    act.wait_ge(w_quantised, n - 1)
                nc.scalar.activation(mag[0:rows_, n % 2, 0:cols], raw[0:rows_, n % 2, 0:cols], ACT.Abs)
                nc.scalar.activation(sgn[0:rows_, n % 2, 0:cols], raw[0:rows_, n % 2, 0:cols], ACT.Sign).then_inc(w_signs, 1)
                act.wait_ge(wT_psum, n + 1)
                for k, d in enumerate(dst):
                    ins = nc.scalar.copy(d, ps_h[k // 4][0:d.shape[0], (k % 4) * P:(k % 4) * P + rows_])
                ins.then_inc(wT_ready, 1)

            def signs_z(i, u):
                act.wait_ge(z_ready, i * UN + (u + 1))
                nc.scalar.activation(mag[:, u, 0:D], z[:, u, :], ACT.Abs)
                nc.scalar.activation(sgn[:, u, 0:D], z[:, u, :], ACT.Sign).then_inc(z_signs, 1)

            def copy_zT(i, u):
                act.wait_ge(zT_psum, i * UN + (u + 1))
                nc.scalar.copy(zqT[:, u], ps_z[:, 0:D].rearrange("p (k t) -> p k t", k=KD)).then_inc(zT_ready, 1)

            def silus(i, u):
                act.wait_ge(gu_psum, i * UN + (u + 1))
                for j in range(2):
                    ins = nc.scalar.activation(silu[:, u, j * HI:(j + 1) * HI], ps_g[j][:, 0:HI], ACT.Silu)
                ins.then_inc(silu_ready, 1)

            def signs_h(i, u):
                act.wait_ge(h_ready, (i * UN + (u + 1)) * 2)
                nc.scalar.activation(mag[:, u, :], raw[:, u, :], ACT.Abs)
                nc.scalar.activation(sgn[:, u, :], raw[:, u, :], ACT.Sign).then_inc(h_signs, 1)

            def copy_hT(i, u):
                act.wait_ge(hT_psum, i * UN + (u + 1))
                nc.scalar.copy(hqT[:, u, 0:4, :], ps_h[0][:].rearrange("p (k t) -> p k t", k=4))
                nc.scalar.copy(hqT[:, u, 4, :], ps_h[1][:, 0:P])
                nc.scalar.copy(hqT[0:I - 5 * P, u, 5, :], ps_h[1][0:I - 5 * P, P:2 * P]).then_inc(hT_ready, 1)

            with act.Fori(0, TRIPS) as i:
                for u in range(UN):
                    signs_z(i, u)
                for step, u in ((copy_zT, 0), (copy_zT, 1), (silus, 0), (signs_h, 0), (copy_zT, 2), (silus, 1), (signs_h, 1), (copy_hT, 0),
                                (silus, 2), (copy_zT, 3), (signs_h, 2), (copy_hT, 1), (silus, 3), (signs_h, 3), (copy_hT, 2), (copy_hT, 3)):
                    step(i, u)

        @block.tensor
        def _(pe):
            pe.wait_ge(loaded, 32)
            for n, (_, rows_, cols, dst) in enumerate(items):
                pe.wait_ge(w_quantised, n + 1)
                pe.wait_ge(wT_ready, n)
                for k in range(len(dst)):
                    width = min(P, cols - k * P)
                    ins = nc.tensor.transpose(ps_h[k // 4][0:width, (k % 4) * P:(k % 4) * P + rows_],
                                              qh[0:rows_, n % 2, k * P:k * P + width], ident[0:rows_, 0:rows_])
                ins.then_inc(wT_psum, 1)
            pe.wait_ge(wT_ready, len(items))

            def transpose_z(i, u):
                pe.wait_ge(qz_ready, i * UN + (u + 1))
                pe.wait_ge(zT_ready, i * UN + u)
                for k in range(KD):
                    ins = nc.tensor.transpose(ps_z[:, k * P:(k + 1) * P], qz[:, u, k * P:(k + 1) * P], ident[:])
                ins.then_inc(zT_psum, 1)

            def gate_up(i, u):
                pe.wait_ge(zT_ready, i * UN + (u + 1))
                pe.wait_ge(h_ready, (i * UN + u) * 2)
                for j in range(2):
                    for g, bank in ((0, ps_g[j]), (1, ps_u[j])):
                        for k in range(KD):
                            ins = nc.tensor.matmul(bank[:, 0:HI], zqT[:, u, k, :], guT[g][:, k, j * HI:(j + 1) * HI],
                                                   start=(k == 0), stop=(k == KD - 1))
                ins.then_inc(gu_psum, 1)

            def transpose_h(i, u):
                pe.wait_ge(qh_ready, i * UN + (u + 1))
                for k in range(IC):
                    width = min(P, I - k * P)
                    ins = nc.tensor.transpose(ps_h[k // 4][0:width, (k % 4) * P:(k % 4 + 1) * P], qh[:, u, k * P:k * P + width], ident[:])
                ins.then_inc(hT_psum, 1)

            def down(i, u):
                pe.wait_ge(hT_ready, i * UN + (u + 1))
                pe.wait_ge(y_ready, i * UN + u)
                for k in range(IC):
                    width = min(P, I - k * P)
                    ins = nc.tensor.matmul(ps_y[:, 0:D], hqT[0:width, u, k, :], downT[0:width, k, :], start=(k == 0), stop=(k == IC - 1))
                ins.then_inc(y_psum, 1)

            with pe.Fori(0, TRIPS) as i:
                for step, u in ((transpose_z, 0), (gate_up, 0), (transpose_z, 1), (gate_up, 1), (transpose_z, 2), (transpose_h, 0), (down, 0),
                                (gate_up, 2), (transpose_z, 3), (transpose_h, 1), (down, 1), (gate_up, 3),
                                (transpose_h, 2), (down, 2), (transpose_h, 3), (down, 3)):
                    step(i, u)


_OUT = (4, 1024, 256)


def build(nc, a, out):
    B, S, _ = _OUT
    T = B * S
    streams = [nc.dram_tensor(f"stream{i}", (T, D), F32).ap() for i in range(3)]
    consts = {n: a[n] for n in ("ident", "mhalf", "iota8", "cum", "ends", "mask", "eye")}
    local_attention(nc, a["x"], consts, {n: a["L0_" + n] for n in ("WpT", "WqT", "WkvT", "WoT", "bp", "bq", "bk", "bv", "bo")}, streams[0], B, S, 16)
    mixture_of_experts(nc, streams[0], consts, {n: a[n] for n in ("router_w", "router_b", "upT", "downT")}, streams[1], T, 8, 1024)
    delta_attention(nc, streams[1], consts, {n: a["L1_" + n] for n in ("WaT", "WaRT", "WkT", "WqT", "WvT", "WbgT", "WoT", "ba", "baR", "bbg", "ln_w", "ln_b")},
                    streams[2], B, S, 16, 64)
    fp4_feed_forward(nc, streams[2], consts, {n: a[n] for n in ("w_gate", "w_up", "w_down")}, out.rearrange("b s d -> (b s) d"), T, 704)


def kernel(**inputs):
    import concourse.bacc as _bacc
    from concourse.bass_utils import run_bass_kernel_spmd as _run

    g = {n: np.asarray(v) for n, v in inputs.items()}
    t = lambda n: g[n].T
    arrays = {
        "x": g["L0_attn_x"],
        "L0_WpT": t("L0_attn_Wp"), "L0_WqT": t("L0_attn_Wq"), "L0_WkvT": np.concatenate([t("L0_attn_Wk"), t("L0_attn_Wv")], axis=1), "L0_WoT": t("L0_attn_Wo"),
        "L0_bp": g["L0_attn_bp"].reshape(KD, P).T, "L0_bq": g["L0_attn_bq"], "L0_bk": g["L0_attn_bk"], "L0_bv": g["L0_attn_bv"], "L0_bo": g["L0_attn_bo"],
        "router_w": g["L0_ffn_router_w"], "router_b": g["L0_ffn_router_b"],
        "upT": g["L0_ffn_expert_up"].transpose(0, 2, 1), "downT": g["L0_ffn_expert_down"].transpose(0, 2, 1),
        "L1_WaT": t("L1_attn_Wa"), "L1_WaRT": t("L1_attn_WaR"), "L1_WkT": t("L1_attn_Wk"), "L1_WqT": t("L1_attn_Wq"), "L1_WvT": t("L1_attn_Wv"),
        "L1_WbgT": np.concatenate([t("L1_attn_Wb"), t("L1_attn_Wg")], axis=1), "L1_WoT": t("L1_attn_Wo"),
        "L1_ba": g["L1_attn_ba"], "L1_baR": g["L1_attn_baR"], "L1_bbg": np.concatenate([g["L1_attn_bb"], g["L1_attn_bg"]]),
        "L1_ln_w": g["L1_attn_ln_w"], "L1_ln_b": g["L1_attn_ln_b"],
        "w_gate": g["L1_ffn_w_gate"], "w_up": g["L1_ffn_w_up"], "w_down": g["L1_ffn_w_down"],
        "ident": np.eye(P, dtype=np.float32), "mhalf": np.full((P, 1), -0.5, np.float32), "iota8": np.arange(8, dtype=np.float32),
    }
    arrays.update(delta_consts())
    nc = _bacc.Bacc("TRN2", target_bir_lowering=False, num_devices=1)
    feeds, args = {}, {}
    for name, array in arrays.items():
        feeds[f"in_{name}"] = np.ascontiguousarray(array)
        args[name] = nc.dram_tensor(f"in_{name}", feeds[f"in_{name}"].shape, mybir.dt.from_np(feeds[f"in_{name}"].dtype), kind="ExternalInput").ap()
    out = nc.dram_tensor("out_0", _OUT, F32, kind="ExternalOutput").ap()
    build(nc, args, out)
    r = _run(nc, [feeds], core_ids=[0])
    return r.results[0]["out_0"]
```

```python
from contextlib import ExitStack

import numpy as np

import concourse.bass as bass
from concourse import mybir

ALU = mybir.AluOpType
ACT = mybir.ActivationFunctionType
F32 = mybir.dt.float32
BF16 = mybir.dt.bfloat16
U32 = mybir.dt.uint32
AX = mybir.AxisListType.X

P = 128
D = 256
KD = D // P
LN_EPS = 1e-5


class Chain:

    def __init__(self, eng, sem, per_trip=0):
        self.eng, self.sem, self.base, self.per_trip, self.n, self.trip = eng, sem, 0, per_trip, 0, None

    def enter(self, trip, per_trip):
        self.base += self.n
        self.n, self.trip, self.per_trip = 0, trip, per_trip

    def leave(self, trips):
        assert self.n == self.per_trip, (self.n, self.per_trip)
        self.base += trips * self.per_trip
        self.n, self.trip = 0, None

    def link(self, ins, apart=False):
        self.n += 1
        ins.then_inc(self.sem, 1)
        at = self.base + self.n
        at = at if self.trip is None else self.trip * self.per_trip + at
        if apart and self.trip is not None:
            wait_apart(self.eng, self.sem, at)
        else:
            self.eng.wait_ge(self.sem, at)


def wait_apart(eng, sem, at):
    eng.wait_ge(sem, at)
    eng.nop(nofuse=True)


class Scope:

    def __init__(self, nc, stack, tag):
        self.nc, self.stack, self.tag = nc, stack, tag

    def sb(self, name, shape, dt=F32):
        return self.stack.enter_context(self.nc.sbuf_tensor(f"{self.tag}_{name}", shape, dt))

    def psum(self, name, cols=512):
        return self.stack.enter_context(self.nc.psum_tensor(f"{self.tag}_{name}", [P, cols], F32))

    def sem(self, name):
        return self.stack.enter_context(self.nc.semaphore(f"{self.tag}_{name}"))


def rows(ap2, n):
    return ap2.partition_broadcast(P)


def local_attention(nc, x_in, consts, w, x_out, B, S, H):
    DH = D // H
    NT = S // P
    SW = S + 2
    TRIPS = NT * B // 2
    UN = 4
    TRIPS2 = NT * B // UN
    scale = DH ** -0.5
    with ExitStack() as stack:
        m = Scope(nc, stack, "la")
        ident = m.sb("ident", [P, P])
        mhalf = m.sb("mhalf", [P, 1])
        wp = m.sb("wp", [P, KD, D]); wq = m.sb("wq", [P, KD, D]); wkv = m.sb("wkv", [P, KD, 2 * D]); wo = m.sb("wo", [P, KD, D])
        bp = m.sb("bp", [P, KD])
        bq = m.sb("bq", [P, D]); bk = m.sb("bk", [P, D]); bv = m.sb("bv", [P, D]); bo = m.sb("bo", [P, D])
        xpT = m.sb("xpT", [P, KD, B * SW])
        x = m.sb("x", [P, UN, D]); z = m.sb("z", [P, 2, D]); zT = m.sb("zT", [P, 2, KD, P])
        st = m.sb("st", [P, 2, 6]); mv = m.sb("mv", [P, 2, 2]); ve = m.sb("ve", [P, 2, 1]); rstd = m.sb("rstd", [P, 2, 1])
        win = m.sb("win", [P, UN, KD, P + 2])
        q = m.sb("q", [P, UN, D]); kv = m.sb("kv", [P, UN, 3, 2 * D]); qraw = m.sb("qraw", [P, UN, D]); kb = m.sb("kb", [P, 3, D]); qk = m.sb("qk", [P, 3, D])
        sc = m.sb("sc", [P, 3, H]); mx = m.sb("mx", [P, H]); ex = m.sb("ex", [P, 3, H]); sm = m.sb("sm", [P, H])
        av = m.sb("av", [P, 3, D]); osum = m.sb("osum", [P, UN, D]); xb = m.sb("xb", [P, UN, D]); o = m.sb("o", [P, UN, D]); oT = m.sb("oT", [P, UN, KD, P]); y = m.sb("y", [P, UN, D])
        ps_t = [m.psum(f"ps_t{i}") for i in range(2)]
        ps_q = m.psum("ps_q")
        ps_kv = [m.psum(f"ps_kv{i}") for i in range(3)]
        ps_o = [m.psum(f"ps_o{i}") for i in range(2)]
        loaded = m.sem("loaded"); x_loaded = [m.sem(f"x_loaded{i}") for i in range(2)]
        var_ready = m.sem("var_ready"); rstd_ready = m.sem("rstd_ready"); z_ready = m.sem("z_ready")
        zT_psum = m.sem("zT_psum"); zT_ready = m.sem("zT_ready"); xp_psum = m.sem("xp_psum"); xp_ready = m.sem("xp_ready")
        halo_ready = m.sem("halo_ready"); win_ready = m.sem("win_ready"); qkv_psum = m.sem("qkv_psum"); kv_used = m.sem("kv_used")
        kv_copied = m.sem("kv_copied"); dve_chain = m.sem("dve_chain"); xb_ready = m.sem("xb_ready")
        scored = m.sem("scored"); exp_ready = m.sem("exp_ready"); o_ready = m.sem("o_ready"); oT_psum = m.sem("oT_psum")
        oT_ready = m.sem("oT_ready"); proj_psum = m.sem("proj_psum"); y_ready = m.sem("y_ready"); stored = [m.sem(f"stored{i}") for i in range(UN)]
        x2_loaded = [m.sem(f"x2_loaded{i}") for i in range(UN)]
        LOADS = 11
        xr = x_in.rearrange("b s d -> (b s) d")
        block = stack.enter_context(nc.Block())

        @block.sync
        def _(sp):
            for dst, src in ((ident[:], consts["ident"]), (mhalf[:], consts["mhalf"]),
                             (wp[:], w["WpT"].rearrange("(k p) n -> p k n", p=P)),
                             (wq[:], w["WqT"].rearrange("(k p) n -> p k n", p=P)),
                             (wkv[:], w["WkvT"].rearrange("(k p) n -> p k n", p=P)),
                             (wo[:], w["WoT"].rearrange("(k p) n -> p k n", p=P)),
                             (bp[:], w["bp"]), (bq[:], w["bq"].partition_broadcast(P)), (bk[:], w["bk"].partition_broadcast(P)),
                             (bv[:], w["bv"].partition_broadcast(P)), (bo[:], w["bo"].partition_broadcast(P))):
                sp.dma_start(dst, src).then_inc(loaded, 16)
            with sp.Fori(0, TRIPS) as i:
                for u in range(2):
                    sp.wait_ge(z_ready, i * 2)
                    sp.dma_start(x[:, u, :], xr[bass.ds(i * (2 * P) + u * P, P), :]).then_inc(x_loaded[u], 16)
            sp.wait_ge(xp_ready, KD * NT * B)
            with sp.Fori(0, TRIPS2) as i:
                for u in range(UN):
                    sp.wait_ge(xb_ready, i * UN)
                    sp.dma_start(x[:, u, :], xr[bass.ds(i * (UN * P) + u * P, P), :]).then_inc(x2_loaded[u], 16)
                for u in range(UN):
                    sp.wait_ge(y_ready, i * UN + u + 1)
                    sp.dma_start(x_out[bass.ds(i * (UN * P) + u * P, P), :], y[:, u, :]).then_inc(stored[u], 16)
            for u in range(UN):
                sp.wait_ge(stored[u], 16 * TRIPS2)

        @block.gpsimd
        def _(pool):
            pool.wait_ge(loaded, 16 * LOADS)
            with pool.Fori(0, TRIPS) as i:
                for u in range(2):
                    pool.wait_ge(var_ready, i * 2 + u + 1)
                    nc.gpsimd.tensor_tensor(rstd[:, u, :], ve[:, u, :], mhalf[:], ALU.pow).then_inc(rstd_ready, 1)

        @block.vector
        def _(dve):
            c = Chain(dve, dve_chain)
            dve.wait_ge(loaded, 16 * LOADS)
            with dve.Fori(0, TRIPS) as i:
                c.enter(i, 4)
                for u in range(2):
                    dve.wait_ge(x_loaded[u], i * 16 + 16)
                    c.link(nc.vector.bn_stats(st[:, u, :], x[:, u, :]), apart=True)
                    c.link(nc.vector.bn_aggr(mv[:, u, :], st[:, u, :]))
                    nc.vector.tensor_scalar(ve[:, u, :], mv[:, u, 1:2], LN_EPS, None, ALU.add).then_inc(var_ready, 1)
                    dve.wait_ge(rstd_ready, i * 2 + u + 1)
                    dve.wait_ge(zT_psum, i * 2)
                    nc.vector.tensor_scalar(z[:, u, :], x[:, u, :], mv[:, u, 0:1], rstd[:, u, :], ALU.subtract, ALU.mult).then_inc(z_ready, 1)
                c.leave(TRIPS)
            def attend(i, u):
                dve.wait_ge(kv_copied, (i * (4 * UN)) + (4 * u + 4))
                nc.vector.tensor_tensor(q[:, u, :], qraw[:, u, :], bq[:], ALU.add)
                c.link(nc.vector.tensor_tensor(kb[:], kv[:, u, :, 0:D], bk[:].unsqueeze(1).to_broadcast([P, 3, D]), ALU.add))
                c.link(nc.vector.tensor_tensor(qk[:], kb[:], q[:, u, :].unsqueeze(1).to_broadcast([P, 3, D]), ALU.mult))
                c.link(nc.vector.tensor_reduce(sc[:].rearrange("p n h -> p (n h)"), qk[:].rearrange("p n (h d) -> p (n h) d", d=DH), AX, ALU.add))
                c.link(nc.vector.tensor_tensor(mx[:], sc[:, 0, :], sc[:, 1, :], ALU.max))
                c.link(nc.vector.tensor_tensor(mx[:], mx[:], sc[:, 2, :], ALU.max))
                nc.vector.tensor_tensor(sc[:], sc[:], mx[:].unsqueeze(1).to_broadcast([P, 3, H]), ALU.subtract).then_inc(scored, 1)
                dve.wait_ge(x2_loaded[u], i * 16 + 16)
                nc.vector.tensor_tensor(xb[:, u, :], x[:, u, :], bo[:], ALU.add).then_inc(xb_ready, 1)
                dve.wait_ge(exp_ready, i * UN + (u + 1))
                c.link(nc.vector.tensor_tensor(sm[:], ex[:, 0, :], ex[:, 1, :], ALU.add))
                c.link(nc.vector.tensor_tensor(sm[:], sm[:], ex[:, 2, :], ALU.add))
                c.link(nc.vector.reciprocal(sm[:], sm[:]))
                c.link(nc.vector.tensor_tensor(ex[:], ex[:], sm[:].unsqueeze(1).to_broadcast([P, 3, H]), ALU.mult))
                for n in range(3):
                    ins = nc.vector.tensor_tensor(av[:, n, :].rearrange("p (h d) -> p h d", d=DH),
                                                  kv[:, u, n, D:2 * D].rearrange("p (h d) -> p h d", d=DH),
                                                  ex[:, n, :].unsqueeze(2).to_broadcast([P, H, DH]), ALU.mult)
                ins.then_inc(kv_used, 1)
                dve.wait_ge(kv_used, i * UN + (u + 1))
                c.link(nc.vector.tensor_tensor(osum[:, u, :], av[:, 0, :], av[:, 1, :], ALU.add))
                c.link(nc.vector.tensor_tensor(osum[:, u, :], osum[:, u, :], av[:, 2, :], ALU.add))
                nc.vector.tensor_tensor(o[:, u, :], osum[:, u, :], bv[:], ALU.add).then_inc(o_ready, 1)

            def result(i, u):
                dve.wait_ge(proj_psum, i * UN + (u + 1))
                dve.wait_ge(stored[u], i * 16)
                nc.vector.tensor_tensor(y[:, u, :], ps_o[u % 2][:, 0:D], xb[:, u, :], ALU.add).then_inc(y_ready, 1)

            with dve.Fori(0, TRIPS2) as i:
                c.enter(i, 11 * UN)
                for step, u in ((attend, 0), (attend, 1), (result, 0), (attend, 2), (result, 1), (attend, 3), (result, 2), (result, 3)):
                    step(i, u)
                c.leave(TRIPS2)

        @block.scalar
        def _(act):
            act.wait_ge(loaded, 16 * LOADS)
            with act.Fori(0, B) as b:
                with act.Fori(0, NT // 2) as i:
                    for u in range(2):
                        n = b * NT + i * 2 + u
                        act.wait_ge(zT_psum, n + 1)
                        nc.scalar.copy(zT[:, u], ps_t[u][:, 0:D].rearrange("p (k t) -> p k t", k=KD)).then_inc(zT_ready, 1)
                        act.wait_ge(xp_psum, n + 1)
                        for k in range(KD):
                            nc.scalar.activation(xpT[:, k, bass.ds(b * SW + i * (2 * P) + (u * P + 1), P)],
                                                 ps_o[u][:, k * P:(k + 1) * P], ACT.Identity, bias=bp[:, k:k + 1]).then_inc(xp_ready, 1)
            act.wait_ge(xp_ready, KD * NT * B)
            by_batch = xpT[:].rearrange("p k (b s) -> p k b s", b=B)
            nc.scalar.copy(by_batch[:, :, :, 0:1], by_batch[:, :, :, S:S + 1]).then_inc(halo_ready, 1)
            nc.scalar.copy(by_batch[:, :, :, S + 1:S + 2], by_batch[:, :, :, 1:2]).then_inc(halo_ready, 1)
            act.wait_ge(halo_ready, 2)

            def copy_qkv(t, u):
                act.wait_ge(kv_used, t * UN)
                for j in range(4):
                    act.wait_ge(qkv_psum, t * (4 * UN) + (4 * u + j + 1))
                    dst, src = (qraw[:, u, :], ps_q[:, 0:D]) if j == 0 else (kv[:, u, j - 1, :], ps_kv[j - 1][:])
                    nc.scalar.copy(dst, src).then_inc(kv_copied, 1)

            def exps(t, u):
                act.wait_ge(scored, t * UN + (u + 1))
                nc.scalar.activation(ex[:], sc[:], ACT.Exp, scale=scale).then_inc(exp_ready, 1)

            def copy_oT(t, u):
                act.wait_ge(oT_psum, t * UN + (u + 1))
                nc.scalar.copy(oT[:, u], ps_t[u % 2][:, 0:D].rearrange("p (k t) -> p k t", k=KD)).then_inc(oT_ready, 1)

            with act.Fori(0, B) as b:
                with act.Fori(0, NT // UN) as i:
                    t = b * (NT // UN) + i
                    act.wait_ge(qkv_psum, t * (4 * UN))
                    for u in range(UN):
                        nc.scalar.copy(win[:, u], xpT[:, :, bass.ds(b * SW + i * (UN * P) + u * P, P + 2)]).then_inc(win_ready, 1)
                    for step, u in ((copy_qkv, 0), (copy_qkv, 1), (exps, 0), (copy_oT, 0), (exps, 1), (copy_qkv, 2), (copy_oT, 1),
                                    (exps, 2), (copy_qkv, 3), (copy_oT, 2), (exps, 3), (copy_oT, 3)):
                        step(t, u)

        @block.tensor
        def _(pe):
            pe.wait_ge(loaded, 16 * LOADS)
            with pe.Fori(0, TRIPS) as t:
                for u in range(2):
                    n = t * 2 + u
                    pe.wait_ge(z_ready, n + 1)
                    for k in range(KD):
                        ins = nc.tensor.transpose(ps_t[u][:, k * P:(k + 1) * P], z[:, u, k * P:(k + 1) * P], ident[:])
                    ins.then_inc(zT_psum, 1)
                    pe.wait_ge(zT_ready, n + 1)
                    pe.wait_ge(xp_ready, t * (2 * KD))
                    for k2 in range(KD):
                        for k in range(KD):
                            ins = nc.tensor.matmul(ps_o[u][:, k2 * P:(k2 + 1) * P], wp[:, k, k2 * P:(k2 + 1) * P], zT[:, u, k, :],
                                                   start=(k == 0), stop=(k == KD - 1))
                    ins.then_inc(xp_psum, 1)
            pe.wait_ge(xp_ready, KD * NT * B)

            def products(t, u):
                pe.wait_ge(win_ready, t * UN + (u + 1))
                for j in range(4):
                    pe.wait_ge(kv_copied, t * (4 * UN) + (4 * (u - 1) + j + 1 if u else 0))
                    for k in range(KD):
                        out, left, right = (ps_q[:, 0:D], win[:, u, k, 1:P + 1], wq[:, k, :]) if j == 0 else (ps_kv[j - 1][:], win[:, u, k, j - 1:j - 1 + P], wkv[:, k, :])
                        ins = nc.tensor.matmul(out, left, right, start=(k == 0), stop=(k == KD - 1))
                    ins.then_inc(qkv_psum, 1)

            def output(t, u):
                pe.wait_ge(o_ready, t * UN + (u + 1))
                for k in range(KD):
                    ins = nc.tensor.transpose(ps_t[u % 2][:, k * P:(k + 1) * P], o[:, u, k * P:(k + 1) * P], ident[:])
                ins.then_inc(oT_psum, 1)
                pe.wait_ge(oT_ready, t * UN + (u + 1))
                pe.wait_ge(y_ready, t * UN + max(u - 1, 0))
                for k in range(KD):
                    ins = nc.tensor.matmul(ps_o[u % 2][:, 0:D], oT[:, u, k, :], wo[:, k, :], start=(k == 0), stop=(k == KD - 1))
                ins.then_inc(proj_psum, 1)

            with pe.Fori(0, TRIPS2) as t:
                for step, u in ((products, 0), (products, 1), (output, 0), (products, 2), (output, 1), (products, 3), (output, 2), (output, 3)):
                    step(t, u)


def mixture_of_experts(nc, x_in, consts, w, x_out, T, E, F):
    TT = 512
    ST = TT // P
    TRIPS = T // TT
    FB = F // P
    UPS = 3
    with ExitStack() as stack:
        m = Scope(nc, stack, "moe")
        ident = m.sb("ident", [P, P]); mhalf = m.sb("mhalf", [P, 1]); iota = m.sb("iota", [P, E])
        up = m.sb("up", [P, E, KD, F]); down = m.sb("down", [P, E, FB, D])
        rw = m.sb("rw", [P, KD, E]); rb = m.sb("rb", [P, E])
        acc = m.sb("acc", [P, 2, ST, D]); z = m.sb("z", [P, ST, D]); zT = m.sb("zT", [P, 2, KD, TT])
        st = m.sb("st", [P, ST, 6]); mv = m.sb("mv", [P, ST, 2]); ve = m.sb("ve", [P, ST]); rstd = m.sb("rstd", [P, ST])
        lg = m.sb("lg", [P, ST, E]); top = m.sb("top", [P, ST, E]); ti = m.sb("ti", [P, ST, E], U32); tf = m.sb("tf", [P, ST, 2])
        lm = m.sb("lm", [P, ST, E]); pe_ = m.sb("pexp", [P, ST, E]); sm = m.sb("sm", [P, ST]); hot = m.sb("hot", [P, 2, ST, E])
        comb = m.sb("comb", [P, 2, ST, E])
        hT = [m.sb(f"hT{i}", [P, FB, TT]) for i in range(2)]
        ps_t = m.psum("ps_t")
        ps_up = [m.psum(f"ps_up{i}") for i in range(UPS)]
        ps_dn = [m.psum(f"ps_dn{i}") for i in range(4)]
        loaded = m.sem("loaded"); w_loaded = [m.sem(f"w_loaded{e}") for e in range(E)]
        x_loaded = [m.sem(f"x_loaded{b}") for b in range(2)]; var_ready = m.sem("var_ready"); rstd_ready = m.sem("rstd_ready"); z_ready = m.sem("z_ready")
        zT_psum = m.sem("zT_psum"); zT_ready = m.sem("zT_ready"); logit_psum = m.sem("logit_psum"); shifted = m.sem("shifted")
        exp_ready = m.sem("exp_ready"); chain = m.sem("chain"); up_psum = m.sem("up_psum"); h_ready = m.sem("h_ready")
        down_psum = m.sem("down_psum"); added = m.sem("added"); stored = [m.sem(f"stored{b}") for b in range(2)]
        LOADS = 5
        NORM_AT, TRANSPOSE_AT, LOGITS_AT, WEIGHTS_AT = 1, 2, 4, 5

        def every_tile(eng, tile):
            with eng.Fori(0, TRIPS // 2 - 1) as i:
                tile(i * 2, 0, i, False)
                tile(i * 2 + 1, 1, i, False)
            tile(TRIPS - 2, 0, TRIPS // 2 - 1, False)
            tile(TRIPS - 1, 1, TRIPS // 2 - 1, True)

        block = stack.enter_context(nc.Block())

        @block.sync
        def _(sp):
            for dst, src in ((ident[:], consts["ident"]), (mhalf[:], consts["mhalf"]), (iota[:], consts["iota8"].partition_broadcast(P)),
                             (rw[:], w["router_w"].rearrange("(k p) n -> p k n", p=P)), (rb[:], w["router_b"].partition_broadcast(P))):
                sp.dma_start(dst, src).then_inc(loaded, 16)
            def load_x(i, b):
                sp.dma_start(acc[:, b], x_in[bass.ds(i * TT, TT), :].rearrange("(s p) d -> p s d", p=P)).then_inc(x_loaded[b], 16)

            load_x(0, 0)
            for e in range(E):
                sp.dma_start(up[:, e], w["upT"][e].rearrange("(k p) f -> p k f", p=P)).then_inc(w_loaded[e], 16)
                sp.dma_start(down[:, e], w["downT"][e].rearrange("(k p) f -> p k f", p=P)).then_inc(w_loaded[e], 16)

            def tile(i, b, trip, last):
                if not last:
                    sp.wait_ge(stored[1 - b], (trip + b) * 16)
                    load_x(i + 1, 1 - b)
                sp.wait_ge(added, (i + 1) * (E * ST))
                sp.dma_start(x_out[bass.ds(i * TT, TT), :].rearrange("(s p) d -> p s d", p=P), acc[:, b]).then_inc(stored[b], 16)

            every_tile(sp, tile)
            for b in range(2):
                sp.wait_ge(stored[b], 16 * (TRIPS // 2))

        @block.gpsimd
        def _(pool):
            pool.wait_ge(loaded, 16 * LOADS)
            with pool.Fori(0, TRIPS) as i:
                pool.wait_ge(var_ready, i + 1)
                nc.gpsimd.tensor_tensor(rstd[:], ve[:], mhalf[:].to_broadcast([P, ST]), ALU.pow).then_inc(rstd_ready, 1)

        @block.vector
        def _(dve):
            c = Chain(dve, chain)
            dve.wait_ge(loaded, 16 * LOADS)

            def norm(i, b, trip):
                dve.wait_ge(x_loaded[b], trip * 16 + 16)
                for s in range(ST):
                    ins = nc.vector.bn_stats(st[:, s, :], acc[:, b, s, :])
                c.link(ins, apart=True)
                for s in range(ST):
                    ins = nc.vector.bn_aggr(mv[:, s, :], st[:, s, :])
                c.link(ins)
                nc.vector.tensor_scalar(ve[:], mv[:, :, 1], LN_EPS, None, ALU.add).then_inc(var_ready, 1)
                dve.wait_ge(rstd_ready, i + 1)
                for s in range(ST):
                    nc.vector.tensor_scalar(z[:, s, :], acc[:, b, s, :], mv[:, s, 0:1], rstd[:, s:s + 1], ALU.subtract, ALU.mult).then_inc(z_ready, 1)

            def shift(i):
                dve.wait_ge(logit_psum, i + 1)
                c.link(nc.vector.tensor_tensor(lg[:], ps_t[:, 0:ST * E].rearrange("p (s e) -> p s e", e=E),
                                               rb[:].unsqueeze(1).to_broadcast([P, ST, E]), ALU.add))
                c.link(nc.vector.tensor_reduce(sm[:], lg[:], AX, ALU.max))
                nc.vector.tensor_tensor(lm[:], lg[:], sm[:].unsqueeze(2).to_broadcast([P, ST, E]), ALU.subtract).then_inc(shifted, 1)

            def weights(i, b):
                dve.wait_ge(exp_ready, i + 1)
                c.link(nc.vector.tensor_reduce(sm[:], pe_[:], AX, ALU.add))
                c.link(nc.vector.reciprocal(sm[:], sm[:]))
                c.link(nc.vector.tensor_tensor(pe_[:], pe_[:], sm[:].unsqueeze(2).to_broadcast([P, ST, E]), ALU.mult), apart=True)
                for s in range(ST):
                    c.link(nc.vector.max(top[:, s, :], pe_[:, s, :]), apart=True)
                    c.link(nc.vector.max_index(ti[:, s, :], top[:, s, :], pe_[:, s, :]), apart=True)
                c.link(nc.vector.tensor_copy(tf[:], ti[:, :, 0:2]))
                for r in range(2):
                    c.link(nc.vector.tensor_tensor(hot[:, r], iota[:].unsqueeze(1).to_broadcast([P, ST, E]),
                                                   tf[:, :, r:r + 1].to_broadcast([P, ST, E]), ALU.is_equal))
                    c.link(nc.vector.tensor_tensor(hot[:, r], hot[:, r], top[:, :, r:r + 1].to_broadcast([P, ST, E]), ALU.mult))
                c.link(nc.vector.tensor_tensor(comb[:, b], hot[:, 0], hot[:, 1], ALU.add))

            def tile(i, b, trip, last):
                for e in range(E):
                    if not last:
                        if e == NORM_AT:
                            norm(i + 1, 1 - b, trip + b)
                        elif e == LOGITS_AT:
                            shift(i + 1)
                        elif e == WEIGHTS_AT:
                            weights(i + 1, 1 - b)
                    for s in range(ST):
                        dve.wait_ge(down_psum, i * (E * ST) + (e * ST + s + 1))
                        if e > 0:
                            dve.wait_ge(added, i * (E * ST) + ((e - 1) * ST + s + 1))
                        nc.vector.scalar_tensor_tensor(acc[:, b, s, :], ps_dn[s][:, 0:D], comb[:, b, s, e:e + 1], acc[:, b, s, :],
                                                       ALU.mult, ALU.add).then_inc(added, 1)

            norm(0, 0, 0)
            shift(0)
            weights(0, 0)
            with dve.Fori(0, TRIPS // 2 - 1) as i:
                c.enter(i, 2 * (13 + 2 * ST))
                tile(i * 2, 0, i, False)
                tile(i * 2 + 1, 1, i, False)
                c.leave(TRIPS // 2 - 1)
            tile(TRIPS - 2, 0, TRIPS // 2 - 1, False)
            tile(TRIPS - 1, 1, TRIPS // 2 - 1, True)

        @block.scalar
        def _(act):

            def copy_zT(i, b):
                for k in range(KD):
                    act.wait_ge(zT_psum, i * KD + (k + 1))
                    nc.scalar.copy(zT[:, b, k, :], ps_t[:]).then_inc(zT_ready, 1)

            def exps(i):
                act.wait_ge(shifted, i + 1)
                nc.scalar.activation(pe_[:], lm[:], ACT.Exp).then_inc(exp_ready, 1)

            def tile(i, b, trip, last):
                for e in range(E):
                    if e >= 2:
                        act.wait_ge(down_psum, i * (E * ST) + (e - 1) * ST)
                    if not last and e == TRANSPOSE_AT:
                        copy_zT(i + 1, 1 - b)
                    elif not last and e == WEIGHTS_AT:
                        exps(i + 1)
                    for f in range(FB):
                        act.wait_ge(up_psum, i * (E * FB) + (e * FB + f + 1))
                        nc.scalar.activation(hT[e % 2][:, f, :], ps_up[(e * FB + f) % UPS][:], ACT.Gelu).then_inc(h_ready, 1)

            copy_zT(0, 0)
            exps(0)
            every_tile(act, tile)

        @block.tensor
        def _(pe):
            pe.wait_ge(loaded, 16 * LOADS)
            def up_products(i, b, e):
                pe.wait_ge(w_loaded[e], 32)
                for f in range(FB):
                    n = e * FB + f
                    pe.wait_ge(h_ready, i * (E * FB) + max(n - UPS + 1, 0))
                    for k in range(KD):
                        ins = nc.tensor.matmul(ps_up[n % UPS][:], up[:, e, k, f * P:(f + 1) * P], zT[:, b, k, :],
                                               start=(k == 0), stop=(k == KD - 1))
                    ins.then_inc(up_psum, 1)

            def down_products(i, e):
                pe.wait_ge(h_ready, i * (E * FB) + (e + 1) * FB)
                for s in range(ST):
                    pe.wait_ge(added, i * (E * ST) + max((e - 1) * ST + s + 1, 0))
                    for f in range(FB):
                        ins = nc.tensor.matmul(ps_dn[s][:, 0:D], hT[e % 2][:, f, s * P:(s + 1) * P], down[:, e, f, :],
                                               start=(f == 0), stop=(f == FB - 1))
                    ins.then_inc(down_psum, 1)

            def transposes(i):
                pe.wait_ge(shifted, i)
                for k in range(KD):
                    if k > 0:
                        pe.wait_ge(zT_ready, i * KD + k)
                    for s in range(ST):
                        pe.wait_ge(z_ready, i * ST + (s + 1))
                        ins = nc.tensor.transpose(ps_t[:, s * P:(s + 1) * P], z[:, s, k * P:(k + 1) * P], ident[:])
                    ins.then_inc(zT_psum, 1)

            def logits(i, b):
                pe.wait_ge(zT_ready, (i + 1) * KD)
                for s in range(ST):
                    for k in range(KD):
                        ins = nc.tensor.matmul(ps_t[:, s * E:(s + 1) * E], zT[:, b, k, s * P:(s + 1) * P], rw[:, k, :],
                                               start=(k == 0), stop=(k == KD - 1))
                ins.then_inc(logit_psum, 1)

            def tile(i, b, trip, last):
                for e in range(E):
                    if not last and e == TRANSPOSE_AT:
                        transposes(i + 1)
                    elif not last and e == LOGITS_AT:
                        logits(i + 1, 1 - b)
                    up_products(i, b, e)
                    if e > 0:
                        down_products(i, e - 1)
                down_products(i, E - 1)

            transposes(0)
            logits(0, 0)
            every_tile(pe, tile)


C = 32
HG = 4


def delta_consts():
    row = np.arange(P)
    b, s = row // C, row % C
    t = np.arange(C)
    same = b[:, None] == b[None, :]
    upto = same & (s[:, None] <= s[None, :])
    first_half = same & (s[:, None] < C // 2)
    cum = -(upto.astype(np.float32) - first_half.astype(np.float32))
    nb = P // C
    ends = np.zeros((P, 2, nb), np.float32)
    for j in range(nb):
        ends[(b == j) & (s < C // 2), 0, j] = -1.0
        ends[(b == j) & (s >= C // 2), 1, j] = -1.0
    strict_T = (s[:, None] < t[None, :]).astype(np.float32)
    upto_T = (s[:, None] <= t[None, :]).astype(np.float32)
    strict = (t[None, :] < s[:, None]).astype(np.float32)
    mask = np.stack([strict_T, strict_T, upto_T, strict], axis=1)
    eye = (s[:, None] == t[None, :]).astype(np.float32)
    return {"cum": cum.astype(np.float32), "ends": ends.reshape(P, 2 * nb), "mask": mask.reshape(P, 4 * C), "eye": eye}


def delta_attention(nc, x_in, consts, w, x_out, B, S, H, DH):
    DI = H * DH
    NHP = H // 2
    NCH = S // C
    NG = H // HG
    GW = HG * DH
    with ExitStack() as stack:
        m = Scope(nc, stack, "da")
        ident = m.sb("ident", [P, P]); mhalf = m.sb("mhalf", [P, 1])
        cum = m.sb("cum", [P, P]); ends = m.sb("ends", [P, 2 * B]); mask = m.sb("mask", [P, 4 * C]); eye = m.sb("eye", [P, C])
        wx = m.sb("wx", [P, KD, 5, DI]); wbg = m.sb("wbg", [P, KD, 2 * H]); wo = m.sb("wo", [P, NHP, D])
        ba = m.sb("ba", [P, 2, DI]); bbg = m.sb("bbg", [P, 2 * H]); lnw = m.sb("lnw", [P, D]); lnb = m.sb("lnb", [P, D])
        x = m.sb("x", [P, D]); z = m.sb("z", [P, D]); xz = m.sb("xz", [P, D]); xn = m.sb("xn", [P, D]); xnT = m.sb("xnT", [P, KD, P])
        st = m.sb("st", [P, 2, 6]); mv = m.sb("mv", [P, 2, 2]); ve = m.sb("ve", [P, 2]); rstd = m.sb("rstd", [P, 2])
        e = m.sb("e", [P, 2, DI])
        sp = m.sb("sp", [P, 2, DI])
        eG = m.sb("eG", [P, 2, DI]); eGn = m.sb("eGn", [P, 2, DI])
        k = m.sb("k", [P, DI]); v = m.sb("v", [P, DI]); q = m.sb("q", [P, DI]); tmp = m.sb("tmp", [P, DI])
        ss = m.sb("ss", [P, H]); ssm = m.sb("ssm", [P, H]); kinv = m.sb("kinv", [P, H])
        bg = m.sb("bg", [P, 2 * H]); bge = m.sb("bge", [P, 2 * H]); sig = m.sb("sig", [P, 2 * H]); nsig = m.sb("nsig", [P, 2 * H])
        Kb = m.sb("Kb", [P, 2, DI]); Km = m.sb("Km", [P, 2, DI]); Qp0 = m.sb("Qp0", [P, DI])
        Kprev, Qp, bv, o, oT = e[:, 0], (Qp0, q), sp[:, 1], eG[:, 0], eG[:, 1].rearrange("p (h t) -> p h t", t=P)
        FS = m.sb("FS", [P, NHP, 3, P]); FR = m.sb("FR", [P, NHP, 2, P]); FK = m.sb("FK", [P, 2, NHP, P])
        M = m.sb("M", [P, 2, NHP, B, DH])
        fac = m.sb("fac", [P, 2, NHP, 2, B]); prev_end = m.sb("prev_end", [P, 2, NHP, B]); decay = m.sb("decay", [P, 2, NHP, B])
        gm = m.sb("gm", [P, 2, 2, 2, HG // 2, 4 * C]); db = m.sb("db", [P, 2, 2, 2, HG // 2, 2, C]); dbT = m.sb("dbT", [P, 2, 2, HG // 2, C]); nn = m.sb("nn", [P, 2, 2, HG // 2, C]); TT = m.sb("TT", [P, 2, 2, 2, HG // 2, C])
        W = m.sb("W", [P, 2, 2, HG // 2, DH]); U = m.sb("U", [P, 2, 2, HG // 2, B, DH]); r = m.sb("r", [P, 2, HG // 2, DH]); y = m.sb("y", [P, D])
        pair = [m.psum(f"pair{i}", 1024) for i in range(4)]
        names = ("loaded x_loaded var_ready rstd_ready z_ready xn_ready xT_psum xT_ready proj_psum a_ready k_ready sq_ready ss_ready kinv_ready "
                 "e_ready sp_ready bg_ready bge_ready sig_ready q_ready v_ready g_ready fac_ready kb_ready kprev_ready km_ready bv_ready qp_ready "
                 "krb_ready krm_ready ft_psum ft_act chain act_chain state_scaled decay_ready end_kept cleared gram_psum mask_done gram_ready dbl_psum y_ready w_psum w_ready part_psum "
                 "u_psum u_ready pu_psum wr_ready ds_psum s_updated ur_psum ur_ready o_psum o_ready dr_psum r_updated oT_psum oT_ready "
                 "out_psum out_ready stored xz_ready").split()
        (loaded, x_loaded, var_ready, rstd_ready, z_ready, xn_ready, xT_psum, xT_ready, proj_psum, a_ready, k_ready, sq_ready, ss_ready, kinv_ready,
         e_ready, sp_ready, bg_ready, bge_ready, sig_ready, q_ready, v_ready, g_ready, fac_ready, kb_ready, kprev_ready, km_ready, bv_ready, qp_ready,
         krb_ready, krm_ready, ft_psum, ft_act, chain, act_chain, state_scaled, decay_ready, end_kept, cleared, gram_psum, mask_done, gram_ready, dbl_psum, y_ready, w_psum, w_ready, part_psum,
         u_psum, u_ready, pu_psum, wr_ready, ds_psum, s_updated, ur_psum, ur_ready, o_psum, o_ready, dr_psum, r_updated, oT_psum, oT_ready,
         out_psum, out_ready, stored, xz_ready) = [m.sem(n) for n in names]

        per_head = lambda a: a.rearrange("p (h d) -> p h d", d=DH)
        over_head = lambda a, n=H: a.unsqueeze(2).to_broadcast([P, n, DH])
        LEVELS = 5
        HJ = HG // 2
        JW = HJ * DH
        gram_ps = pair[0][:].rearrange("p (q c) -> p q c", q=2)[:, :, 0:HJ * 4 * C].rearrange("p q (j c) -> p q j c", j=HJ)
        power_ps = [pair[1][:, rec * 512:rec * 512 + HG * 2 * C].rearrange("p (q j s c) -> p q j s c", q=2, j=HJ, s=2) for rec in range(2)]
        wu_ps = pair[2][:].rearrange("p (q k j e) -> p q k j e", q=2, k=4, j=HJ)
        po_ps = pair[3][:].rearrange("p (q k j e) -> p q k j e", q=2, k=4, j=HJ)
        by_head = lambda a: a.rearrange("p (j q e) -> p q j e", q=2, e=DH)

        ORDER = (("G", 0), "W0", "V0", ("G", 1), ("D", 0, 0), "U0", ("D", 0, 1), ("D", 1, 0), "W1", "I0", ("D", 1, 1), "S0",
                 ("D", 2, 0), ("D", 2, 1), "U1", ("D", 3, 0), "I1", ("D", 3, 1), "S1", ("D", 4, 0), ("D", 4, 1))
        LN_AT = (2, 8, 14)
        gram_at = lambda i, g, rec: i * (2 * NG) + (2 * g + rec + 1)
        dbl_at = lambda i, g, lvl, rec: i * (10 * NG) + (10 * g + 2 * lvl + rec + 1)
        y_at = lambda i, g, lvl, rec: i * (10 * NG) + (10 * g + 2 * lvl + rec + 1)
        once = lambda i, g: i * NG + (g + 1)
        LOADS = 18
        block = stack.enter_context(nc.Block())
        chunk_rows = lambda a, i, b: a[bass.ds(i * C + b * S, C), :]

        def every_chunk(eng, chunk):
            with eng.Fori(0, NCH - 1) as i:
                chunk(i, False)
            chunk(NCH - 1, True)

        @block.sync
        def _(sp_):
            rows_ = lambda a: a.partition_broadcast(P)
            loads = [(ident[:], consts["ident"]), (mhalf[:], consts["mhalf"]), (cum[:], consts["cum"]), (ends[:], consts["ends"]),
                     (mask[:], consts["mask"]), (eye[:], consts["eye"]),
                     (wbg[:], w["WbgT"].rearrange("(k p) n -> p k n", p=P)), (wo[:], w["WoT"].rearrange("(k p) n -> p k n", p=P)),
                     (ba[:, 0], rows_(w["ba"])), (ba[:, 1], rows_(w["baR"])), (bbg[:], rows_(w["bbg"])), (lnw[:], rows_(w["ln_w"])), (lnb[:], rows_(w["ln_b"]))]
            loads += [(wx[:, :, j], w[n].rearrange("(k p) n -> p k n", p=P)) for j, n in enumerate(("WaT", "WaRT", "WkT", "WqT", "WvT"))]
            assert len(loads) == LOADS
            for dst, src in loads:
                sp_.dma_start(dst, src).then_inc(loaded, 16)

            def load_x(i):
                for b in range(B):
                    sp_.dma_start(x[b * C:(b + 1) * C, :], chunk_rows(x_in, i, b)).then_inc(x_loaded, 16)

            def chunk(i, last):
                if not last:
                    sp_.wait_ge(xz_ready, i + 1)
                    load_x(i + 1)
                sp_.wait_ge(out_ready, i + 1)
                for b in range(B):
                    sp_.dma_start(chunk_rows(x_out, i, b), y[b * C:(b + 1) * C, :]).then_inc(stored, 16)

            load_x(0)
            every_chunk(sp_, chunk)
            sp_.wait_ge(stored, 16 * B * NCH)

        @block.gpsimd
        def _(pool):
            pool.wait_ge(loaded, 16 * LOADS)

            def norms(i):
                for n in range(2):
                    pool.wait_ge(var_ready, i * 2 + (n + 1))
                    nc.gpsimd.tensor_tensor(rstd[:, n:n + 1], ve[:, n:n + 1], mhalf[:], ALU.pow).then_inc(rstd_ready, 1)

            def chunk(i, last):
                pool.wait_ge(z_ready, i + 1)
                pool.wait_ge(out_ready, i)
                nc.gpsimd.tensor_tensor(xz[:], x[:], z[:], ALU.add).then_inc(xz_ready, 1)
                pool.wait_ge(ss_ready, i + 1)
                nc.gpsimd.tensor_tensor(kinv[:], ssm[:], mhalf[:].to_broadcast([P, H]), ALU.pow).then_inc(kinv_ready, 1)
                pool.wait_ge(v_ready, i + 1)
                pool.wait_ge(sig_ready, i * 2 + 2)
                pool.wait_ge(fac_ready, i * 2 + 2)
                nc.gpsimd.tensor_tensor(per_head(bv), per_head(v[:]), over_head(sig[:, 0:H]), ALU.mult).then_inc(bv_ready, 1)
                pool.wait_ge(q_ready, i + 1)
                for rec in range(2):
                    pool.wait_ge(g_ready, i * 4 + 2 * rec + 1)
                    pool.wait_ge(qp_ready, i * 2 + rec)
                    nc.gpsimd.tensor_tensor(Qp[rec][:], q[:], eG[:, rec], ALU.mult).then_inc(qp_ready, 1)
                nc.gpsimd.tensor_tensor(decay[:], fac[:, :, :, 0, :], prev_end[:], ALU.mult).then_inc(decay_ready, 1)
                pool.wait_ge(decay_ready, i + 1)
                pool.wait_ge(r_updated, i * NG)
                for rec in range(2):
                    st_ = M[:, rec].rearrange("p a b c -> p (a b) c")
                    nc.gpsimd.tensor_tensor(st_, st_, decay[:, rec].rearrange("p a b -> p (a b)").unsqueeze(2).to_broadcast([P, NHP * B, DH]), ALU.mult).then_inc(state_scaled, 1)
                nc.gpsimd.tensor_copy(prev_end[:], fac[:, :, :, 1, :]).then_inc(end_kept, 1)
                pool.wait_ge(end_kept, i + 1)
                if not last:
                    norms(i + 1)

            norms(0)
            pool.wait_ge(cleared, 1)
            every_chunk(pool, chunk)

        @block.vector
        def _(dve):
            c = Chain(dve, chain)
            c.link(nc.vector.memset(M[:].rearrange("p a b c d -> p (a b c d)"), 0.0))
            c.link(nc.vector.memset(U[:].rearrange("p a b c d e -> p (a b c d e)"), 0.0))
            nc.vector.memset(prev_end[:].rearrange("p a b c -> p (a b c)"), 1.0).then_inc(cleared, 1)
            dve.wait_ge(loaded, 16 * LOADS)

            flat = lambda a: a.rearrange("p q j c -> p (q j c)")

            def gram_mask(i, g, rec):
                lo = 0 if rec == 0 else C
                dve.wait_ge(gram_psum, gram_at(i, g, rec))
                for q_ in range(2):
                    ins = nc.vector.tensor_tensor(gm[:, rec, g % 2, q_, :, lo:3 * C], gram_ps[:, q_, :, lo:3 * C],
                                                  mask[:, lo:3 * C].unsqueeze(1).to_broadcast([P, HJ, 3 * C - lo]), ALU.mult)
                ins.then_inc(mask_done, 1)
                dve.wait_ge(mask_done, gram_at(i, g, rec))
                c.link(nc.vector.transpose(nn[:, rec], gm[:, rec, g % 2, :, :, C:2 * C]))
                nc.vector.tensor_tensor(db[:, rec, 0, :, :, 1, :], nn[:, rec], eye[:].unsqueeze(1).unsqueeze(1).to_broadcast([P, 2, HJ, C]), ALU.add).then_inc(gram_ready, 1)

            def powers(i, g, lvl, rec):
                dve.wait_ge(dbl_psum, dbl_at(i, g, lvl, rec))
                out = power_ps[rec]
                if lvl > 0:
                    last = lvl == LEVELS - 1
                    ins = nc.vector.tensor_tensor(nn[:, rec] if last else db[:, rec, lvl % 2, :, :, 1, :], db[:, rec, (lvl - 1) % 2, :, :, 1, :], out[:, :, :, 1, :], ALU.add)
                    if last:
                        c.link(ins)
                        nc.vector.transpose(TT[:, rec, g % 2], nn[:, rec]).then_inc(y_ready, 1)
                        return
                nc.vector.tensor_copy(db[:, rec, lvl % 2, :, :, 0, :], out[:, :, :, 0, :])
                nc.vector.transpose(dbT[:, rec], out[:, :, :, 0, :]).then_inc(y_ready, 1)

            def add_bv(i, g):
                dve.wait_ge(w_psum, once(i, g))
                nc.vector.tensor_tensor(W[:, 0], wu_ps[:, :, 0], by_head(bv[:, g * GW:(g + 1) * GW]), ALU.add).then_inc(w_ready, 1)

            def clipped(i, g):
                dve.wait_ge(pu_psum, once(i, g))
                gamma = sig[:, H + g * HG:H + (g + 1) * HG].rearrange("p (j q) -> p q j", q=2).unsqueeze(3).to_broadcast([P, 2, HJ, DH])
                c.link(nc.vector.tensor_tensor(r[:], by_head(v[:, g * GW:(g + 1) * GW]), po_ps[:, :, 0], ALU.subtract))
                c.link(nc.vector.tensor_scalar(r[:], r[:], 1.0, -1.0, ALU.min, ALU.max))
                c.link(nc.vector.tensor_tensor(r[:], r[:], gamma, ALU.mult))
                nc.vector.tensor_tensor(W[:, 1], wu_ps[:, :, 1], r[:], ALU.add).then_inc(wr_ready, 1)

            def update(i, g, rec):
                dve.wait_ge((ds_psum, dr_psum)[rec], once(i, g))
                st_ = M[:, rec, 2 * g:2 * g + 2].rearrange("p a b c -> p (a b c)")
                nc.vector.tensor_tensor(st_, pair[0][:, rec * 512:(rec + 1) * 512], st_, ALU.add).then_inc((s_updated, r_updated)[rec], 1)

            def layer_norms(i, step):
                def variance(n, src):
                    c.link(nc.vector.bn_stats(st[:, n], src[:]), apart=True)
                    c.link(nc.vector.bn_aggr(mv[:, n], st[:, n]))
                    nc.vector.tensor_scalar(ve[:, n:n + 1], mv[:, n, 1:2], LN_EPS, None, ALU.add).then_inc(var_ready, 1)

                if step == 0:
                    dve.wait_ge(x_loaded, i * (16 * B) + 16 * B)
                    variance(0, x)
                elif step == 1:
                    dve.wait_ge(rstd_ready, i * 2 + 1)
                    dve.wait_ge(xz_ready, i)
                    nc.vector.tensor_scalar(z[:], x[:], mv[:, 0, 0:1], rstd[:, 0:1], ALU.subtract, ALU.mult).then_inc(z_ready, 1)
                    dve.wait_ge(z_ready, i + 1)
                    variance(1, z)
                else:
                    dve.wait_ge(rstd_ready, i * 2 + 2)
                    dve.wait_ge(xT_psum, i)
                    c.link(nc.vector.tensor_scalar(xn[:], z[:], mv[:, 1, 0:1], rstd[:, 1:2], ALU.subtract, ALU.mult))
                    c.link(nc.vector.tensor_tensor(xn[:], xn[:], lnw[:], ALU.mult))
                    nc.vector.tensor_tensor(xn[:], xn[:], lnb[:], ALU.add).then_inc(xn_ready, 1)

            def chunk(i, last):
                for rec in range(2):
                    dve.wait_ge(proj_psum, i * 9 + (rec + 1))
                    nc.vector.tensor_tensor(sp[:, rec], pair[rec][:], ba[:, rec], ALU.add).then_inc(a_ready, 1)
                dve.wait_ge(sq_ready, i + 1)
                c.link(nc.vector.tensor_reduce(ss[:], per_head(tmp[:]), AX, ALU.add))
                nc.vector.tensor_scalar(ssm[:], ss[:], 1e-24, None, ALU.max).then_inc(ss_ready, 1)
                dve.wait_ge(proj_psum, i * 9 + 4)
                nc.vector.tensor_tensor(bg[:], pair[3][:, 256:256 + 2 * H], bbg[:], ALU.add).then_inc(bg_ready, 1)
                dve.wait_ge(bge_ready, i + 1)
                c.link(nc.vector.tensor_scalar(bge[:], bge[:], 1.0, None, ALU.add))
                nc.vector.reciprocal(sig[:], bge[:]).then_inc(sig_ready, 1)
                dve.wait_ge(sig_ready, i * 2 + 1)
                nc.vector.tensor_scalar(nsig[:], sig[:], -1.0, None, ALU.mult).then_inc(sig_ready, 1)
                dve.wait_ge(proj_psum, i * 9 + 5)
                dve.wait_ge(ft_psum, i * 7)
                nc.vector.tensor_copy(q[:], pair[0][:]).then_inc(q_ready, 1)
                dve.wait_ge(proj_psum, i * 9 + 6)
                nc.vector.tensor_copy(v[:], pair[1][:]).then_inc(v_ready, 1)
                dve.wait_ge(kinv_ready, i + 1)
                dve.wait_ge(sig_ready, i * 2 + 2)
                c.link(nc.vector.tensor_tensor(per_head(k[:]), per_head(k[:]), over_head(kinv[:]), ALU.mult))
                for rec in range(2):
                    dve.wait_ge(g_ready, i * 4 + 2 * rec + 1)
                    c.link(nc.vector.tensor_tensor(tmp[:], eG[:, rec], k[:], ALU.mult))
                    nc.vector.tensor_tensor(per_head(Kb[:, rec]), per_head(tmp[:]), over_head(nsig[:, rec * H:(rec + 1) * H]), ALU.mult).then_inc(kb_ready, 1)
                    if rec == 0:
                        c.link(nc.vector.scalar_tensor_tensor(Kprev, e[:, 0], 1.0, tmp[:], ALU.add, ALU.mult))
                    dve.wait_ge(g_ready, i * 4 + 2 * rec + 2)
                    nc.vector.tensor_tensor(Km[:, rec], eGn[:, rec], k[:], ALU.mult).then_inc(km_ready, 1)
                for slot in range(NG + 1):
                    g, s = slot, slot - 1
                    for at, what in enumerate(ORDER):
                        if slot == 2 and not last and at in LN_AT:
                            layer_norms(i + 1, LN_AT.index(at))
                        if what[0] in "GD":
                            if g >= NG:
                                continue
                            if what[0] == "G":
                                gram_mask(i, g, what[1])
                            else:
                                powers(i, g, what[1], what[2])
                        elif s >= 0:
                            if what == "W0":
                                if s == 0:
                                    dve.wait_ge(bv_ready, i + 1)
                                add_bv(i, s)
                            elif what == "I0":
                                clipped(i, s)
                            elif what[0] == "S":
                                update(i, s, int(what[1]))
                dve.wait_ge(out_psum, i + 1)
                dve.wait_ge(stored, i * (16 * B))
                nc.vector.tensor_tensor(y[:], pair[1][:, 0:D], xz[:], ALU.add).then_inc(out_ready, 1)

            for step in range(3):
                layer_norms(0, step)
            with dve.Fori(0, NCH - 1) as i:
                c.enter(i, 40)
                chunk(i, False)
                c.leave(NCH - 1)
            chunk(NCH - 1, True)

        @block.scalar
        def _(act):
            def copy_u(i, g, rec):
                act.wait_ge((u_psum, ur_psum)[rec], once(i, g))
                for b in range(B):
                    ins = nc.scalar.copy(U[b * C:(b + 1) * C, rec, :, :, b, :], wu_ps[b * C:(b + 1) * C, :, 2 + rec])
                ins.then_inc((u_ready, ur_ready)[rec], 1)

            def copy_xT(i):
                act.wait_ge(xT_psum, i + 1)
                nc.scalar.copy(xnT[:], pair[3][:, 0:D].rearrange("p (k t) -> p k t", k=KD)).then_inc(xT_ready, 1)

            def chunk(i, last):
                act.wait_ge(proj_psum, i * 9 + 3)
                nc.scalar.copy(k[:], pair[2][:]).then_inc(k_ready, 1)
                nc.scalar.activation(tmp[:], pair[2][:], ACT.Square).then_inc(sq_ready, 1)
                act.wait_ge(bg_ready, i + 1)
                nc.scalar.activation(bge[:], bg[:], ACT.Exp, scale=-1.0).then_inc(bge_ready, 1)
                for rec in range(2):
                    act.wait_ge(a_ready, i * 2 + (rec + 1))
                    nc.scalar.activation(e[:, rec], sp[:, rec], ACT.Exp, scale=-1.0).then_inc(e_ready, 1)
                for rec in range(2):
                    act.wait_ge(e_ready, i * 2 + (rec + 1))
                    nc.scalar.activation(sp[:, rec], e[:, rec], ACT.Ln, bias=1.0).then_inc(sp_ready, 1)
                for rec in range(2):
                    act.wait_ge(proj_psum, i * 9 + (7 + rec))
                    nc.scalar.activation(eG[:, rec], pair[2 + rec][:], ACT.Exp).then_inc(g_ready, 1)
                    nc.scalar.activation(eGn[:, rec], pair[2 + rec][:], ACT.Exp, scale=-1.0).then_inc(g_ready, 1)
                act.wait_ge(proj_psum, i * 9 + 9)
                for rec in range(2):
                    nc.scalar.activation(fac[:, rec].rearrange("p a b c -> p (a b c)"), pair[0][:, rec * 512:rec * 512 + NHP * 2 * B], ACT.Exp).then_inc(fac_ready, 1)
                for n, dst in ((0, FS[:, :, 1, :]), (1, FS[:, :, 0, :]), (2, FK[:, 0]), (3, FS[:, :, 2, :]), (4, FR[:, :, 0, :]), (5, FK[:, 1]), (6, FR[:, :, 1, :])):
                    act.wait_ge(ft_psum, i * 7 + (n + 1))
                    nc.scalar.copy(dst, pair[n % 4][:].rearrange("p (h t) -> p h t", t=P)).then_inc(ft_act, 1)
                for s in range(NG):
                    copy_u(i, s, 0)
                    copy_u(i, s, 1)
                    act.wait_ge(o_psum, once(i, s))
                    nc.scalar.copy(by_head(o[:, s * GW:(s + 1) * GW]), po_ps[:, :, 1]).then_inc(o_ready, 1)
                act.wait_ge(oT_psum, i + 1)
                nc.scalar.copy(oT, pair[0][:].rearrange("p (h t) -> p h t", t=P)).then_inc(oT_ready, 1)
                if not last:
                    copy_xT(i + 1)

            act.wait_ge(loaded, 16 * LOADS)
            copy_xT(0)
            every_chunk(act, chunk)

        @block.tensor
        def _(pe):
            mm = nc.tensor.matmul

            apart = lambda sem, at: wait_apart(pe, sem, at)

            heads = [(b, q_, j) for j in range(HJ) for q_ in range(2) for b in range(B)]
            rows_of = lambda b: slice(b * C, (b + 1) * C)
            feat = lambda q_: slice(DH * q_, DH * (q_ + 1))

            def gram(i, g, rec):
                F = (FS, FR)[rec]
                lo = 0 if rec == 0 else 1
                for b, q_, j in heads:
                    f, hp, rw = feat(q_), g * HJ + j, rows_of(b)
                    ins = mm(gram_ps[rw, q_, j, lo * C:3 * C], FK[f, rec, hp, rw], F[f, hp, lo - rec:3 - rec, rw], start=True, stop=True)
                ins.then_inc(gram_psum, 1)

            def double(i, g, lvl, rec):
                if lvl == 0:
                    apart(gram_ready, gram_at(i, g, rec))
                    apart(y_ready, i * (10 * NG) + 10 * g)
                else:
                    apart(y_ready, y_at(i, g, lvl - 1, rec))
                for b, q_, j in heads:
                    rw = rows_of(b)
                    out = power_ps[rec][rw, q_, j]
                    if lvl == 0:
                        ins = mm(out[:, 0, :], gm[rw, rec, g % 2, q_, j, C:2 * C], nn[rw, rec, q_, j], start=True, stop=True)
                    else:
                        lo = 1 if lvl == LEVELS - 1 else 0
                        ins = mm(out[:, lo:2, :], dbT[rw, rec, q_, j], db[rw, rec, (lvl - 1) % 2, q_, j, lo:2, :], start=True, stop=True)
                ins.then_inc(dbl_psum, 1)

            def state_w(i, g, rec):
                if rec == 0:
                    apart(ur_ready, i * NG + g)
                else:
                    apart(u_ready, once(i, g))
                F = (FS, FR)[rec]
                for b, q_, j in heads:
                    f, hp, rw = feat(q_), g * HJ + j, rows_of(b)
                    ins = mm(wu_ps[rw, q_, rec, j], F[f, hp, 1 - rec, rw], M[f, rec, hp, b, :], start=True, stop=True)
                if rec == 0:
                    ins.then_inc(w_psum, 1)

            def state_parts(i, g, rec):
                apart(o_ready, i * NG + g)
                for b, q_, j in heads:
                    f, hp, rw = feat(q_), g * HJ + j, rows_of(b)
                    mm(po_ps[rw, q_, 0, j], FS[f, hp, 0, rw], M[f, 0, hp, b, :], start=(j == 0), stop=False, skip_group_check=True)
                for b, q_, j in heads:
                    f, hp, rw = feat(q_), g * HJ + j, rows_of(b)
                    mm(po_ps[rw, q_, 1, j], FS[f, hp, 2, rw], M[f, 0, hp, b, :], start=False, stop=False, skip_group_check=True)
                    mm(po_ps[rw, q_, 1, j], FR[f, hp, 1, rw], M[f, 1, hp, b, :], start=False, stop=False, skip_group_check=True)

            def solve(i, g, rec):
                apart((w_ready, wr_ready)[rec], once(i, g))
                apart(y_ready, y_at(i, g, LEVELS - 1, rec))
                for b, q_, j in heads:
                    rw = rows_of(b)
                    ins = mm(wu_ps[rw, q_, 2 + rec, j], TT[rw, rec, g % 2, q_, j], W[rw, rec, q_, j], start=True, stop=True)
                ins.then_inc((u_psum, ur_psum)[rec], 1)

            def inner_parts(i, g, rec):
                apart((u_ready, ur_ready)[rec], once(i, g))
                for b, q_, j in heads:
                    rw = rows_of(b)
                    G = gm[rw, rec, g % 2, q_, j]
                    if rec == 0:
                        mm(po_ps[rw, q_, 0, j], G[:, 0:C], U[rw, 0, q_, j, b], start=False, stop=True, skip_group_check=True)
                    ins = mm(po_ps[rw, q_, 1, j], G[:, 2 * C:3 * C], U[rw, rec, q_, j, b], start=False, stop=(rec == 1), skip_group_check=True)
                ins.then_inc((pu_psum, o_psum)[rec], 1)

            def state_update(i, g, rec):
                for q_ in range(2):
                    for j in range(HJ):
                        col = (g * HG + 2 * j + q_) * DH
                        ins = mm(pair[0][feat(q_), rec * 512 + j * B * DH:rec * 512 + (j + 1) * B * DH], Km[:, rec, col:col + DH],
                                 U[:, rec, q_, j].rearrange("p b e -> p (b e)"), start=True, stop=True)
                ins.then_inc((ds_psum, dr_psum)[rec], 1)

            def project(out, j, n0):
                for half in range(2):
                    for kk in range(KD):
                        ins = mm(out[:, half * 512:(half + 1) * 512], xnT[:, kk, :], wx[:, kk, j, half * 512:(half + 1) * 512], start=(kk == 0), stop=(kk == KD - 1))
                ins.then_inc(proj_psum, 1)

            def transpose_x(i):
                pe.wait_ge(xn_ready, i + 1)
                for kk in range(KD):
                    ins = nc.tensor.transpose(pair[3][:, kk * P:(kk + 1) * P], xn[:, kk * P:(kk + 1) * P], ident[:])
                ins.then_inc(xT_psum, 1)

            def chunk(i, last):
                pe.wait_ge(xT_ready, i + 1)
                project(pair[0], 0, 0)
                pe.wait_ge(out_ready, i)
                project(pair[1], 1, 0)
                project(pair[2], 2, 0)
                for kk in range(KD):
                    ins = mm(pair[3][:, 256:256 + 2 * H], xnT[:, kk, :], wbg[:, kk, :], start=(kk == 0), stop=(kk == KD - 1))
                ins.then_inc(proj_psum, 1)
                pe.wait_ge(a_ready, i * 2 + 1)
                project(pair[0], 3, 0)
                pe.wait_ge(a_ready, i * 2 + 2)
                project(pair[1], 4, 0)
                pe.wait_ge(sq_ready, i + 1)
                pe.wait_ge(bg_ready, i + 1)
                for rec in range(2):
                    pe.wait_ge(sp_ready, i * 2 + (rec + 1))
                    for half in range(2):
                        ins = mm(pair[2 + rec][:, half * 512:(half + 1) * 512], cum[:], sp[:, rec, half * 512:(half + 1) * 512], start=True, stop=True)
                    ins.then_inc(proj_psum, 1)
                pe.wait_ge(q_ready, i + 1)
                for rec in range(2):
                    for hp in range(NHP):
                        ins = mm(pair[0][:, rec * 512 + hp * 2 * B:rec * 512 + (hp + 1) * 2 * B], sp[:, rec, hp * P:(hp + 1) * P], ends[:], start=True, stop=True)
                ins.then_inc(proj_psum, 1)
                for n, (src, ready) in enumerate((
                        (Kb[:, 0], [(kb_ready, i * 2 + 1), (fac_ready, i * 2 + 2)]), (Kprev, [(km_ready, i * 2 + 1), (v_ready, i + 1)]),
                        (Km[:, 0], [(km_ready, i * 2 + 1), (g_ready, i * 4 + 2)]), (Qp[0], [(qp_ready, i * 2 + 1), (g_ready, i * 4 + 4)]),
                        (Kb[:, 1], [(kb_ready, i * 2 + 2), (ft_act, i * 7 + 1)]), (Km[:, 1], [(km_ready, i * 2 + 2), (ft_act, i * 7 + 2)]),
                        (Qp[1], [(qp_ready, i * 2 + 2), (ft_act, i * 7 + 3)]))):
                    for sem, at in ready:
                        pe.wait_ge(sem, at)
                    for hp in range(NHP):
                        ins = nc.tensor.transpose(pair[n % 4][:, hp * P:(hp + 1) * P], src[:, hp * P:(hp + 1) * P], ident[:])
                    ins.then_inc(ft_psum, 1)
                pe.wait_ge(ft_act, i * 7 + 7)
                for slot in range(NG + 1):
                    g, s = slot, slot - 1
                    if slot == 1:
                        apart(state_scaled, i * 2 + 2)
                    for what in ORDER:
                        if what[0] in "GD":
                            if g >= NG:
                                continue
                            if what[0] == "D":
                                double(i, g, what[1], what[2])
                                continue
                            apart(*((r_updated, i * NG + max(s, 0)) if what[1] == 0 else (mask_done, gram_at(i, g, 0))))
                            gram(i, g, what[1])
                        elif s >= 0:
                            rec = int(what[1])
                            if what[0] == "S" and rec == 0:
                                apart(mask_done, gram_at(i, min(g, NG - 1), 1))
                            {"W": state_w, "V": state_parts, "U": solve, "I": inner_parts, "S": state_update}[what[0]](i, s, rec)
                pe.wait_ge(r_updated, (i + 1) * NG)
                pe.wait_ge(o_ready, (i + 1) * NG)
                for hp in range(NHP):
                    ins = nc.tensor.transpose(pair[0][:, hp * P:(hp + 1) * P], o[:, hp * P:(hp + 1) * P], ident[:])
                ins.then_inc(oT_psum, 1)
                if not last:
                    transpose_x(i + 1)
                pe.wait_ge(oT_ready, i + 1)
                for hp in range(NHP):
                    ins = mm(pair[1][:, 0:D], oT[:, hp, :], wo[:, hp, :], start=(hp == 0), stop=(hp == NHP - 1))
                ins.then_inc(out_psum, 1)

            pe.wait_ge(loaded, 16 * LOADS)
            transpose_x(0)
            every_chunk(pe, chunk)


FP4_BLOCK = 16
FP4_MAX = 6.0


def fp4_feed_forward(nc, x_in, consts, w, x_out, T, I):
    IC = -(-I // P)
    HI = I // 2
    NT = T // P
    UN = 4
    TRIPS = NT // UN
    with ExitStack() as stack:
        m = Scope(nc, stack, "ff")
        ident = m.sb("ident", [P, P]); mhalf = m.sb("mhalf", [P, 1])
        guT = [m.sb(f"guT{j}", [P, KD, I]) for j in range(2)]
        downT = m.sb("downT", [P, IC, D])
        x = m.sb("x", [P, UN, D]); y = m.sb("y", [P, UN, D]); z = m.sb("z", [P, UN, D]); zqT = m.sb("zqT", [P, UN, KD, P])
        st = m.sb("st", [P, UN, 6]); mv = m.sb("mv", [P, UN, 2]); ve = m.sb("ve", [P, UN, 1]); rstd = m.sb("rstd", [P, UN, 1])
        raw = m.sb("raw", [P, UN, I]); mag = m.sb("mag", [P, UN, I]); sgn = m.sb("sgn", [P, UN, I])
        ratio = m.sb("ratio", [P, I]); level = m.sb("level", [P, I]); above = m.sb("above", [P, I]); qz = m.sb("qz", [P, UN, D]); qh = m.sb("qh", [P, UN, I])
        amax = m.sb("amax", [P, I // FP4_BLOCK]); scl = m.sb("scl", [P, I // FP4_BLOCK]); inv = m.sb("inv", [P, I // FP4_BLOCK])
        silu = m.sb("silu", [P, UN, I]); hqT = m.sb("hqT", [P, UN, IC, P])
        ps_z = m.psum("ps_z"); ps_h = [m.psum(f"ps_h{i}") for i in range(2)]
        ps_g = [m.psum(f"ps_g{i}") for i in range(2)]; ps_u = [m.psum(f"ps_u{i}") for i in range(2)]; ps_y = m.psum("ps_y")
        loaded = m.sem("loaded"); w_loaded = [m.sem(f"w_loaded{i}") for i in range(2)]; w_signs = m.sem("w_signs"); w_quantised = m.sem("w_quantised")
        wT_psum = m.sem("wT_psum"); wT_ready = m.sem("wT_ready"); chain = m.sem("chain")
        x_loaded = [m.sem(f"x_loaded{i}") for i in range(UN)]; var_ready = m.sem("var_ready"); rstd_ready = m.sem("rstd_ready")
        z_ready = m.sem("z_ready"); z_signs = m.sem("z_signs"); qz_ready = m.sem("qz_ready"); zT_psum = m.sem("zT_psum")
        zT_ready = m.sem("zT_ready"); gu_psum = m.sem("gu_psum"); silu_ready = m.sem("silu_ready"); h_ready = m.sem("h_ready")
        h_signs = m.sem("h_signs"); qh_ready = m.sem("qh_ready"); hT_psum = m.sem("hT_psum"); hT_ready = m.sem("hT_ready")
        y_psum = m.sem("y_psum"); y_ready = m.sem("y_ready"); stored = [m.sem(f"stored{i}") for i in range(UN)]

        items = []
        for j, name in enumerate(("w_gate", "w_up")):
            for r in range(IC):
                n = min(P, I - r * P)
                items.append((w[name][r * P:r * P + n, :], n, D, [guT[j][:, k, r * P:r * P + n] for k in range(KD)]))
        for r in range(KD):
            items.append((w["w_down"][r * P:(r + 1) * P, :], P, I,
                          [downT[0:min(P, I - k * P), k, r * P:(r + 1) * P] for k in range(IC)]))

        block = stack.enter_context(nc.Block())

        @block.sync
        def _(sp):
            for dst, src in ((ident[:], consts["ident"]), (mhalf[:], consts["mhalf"])):
                sp.dma_start(dst, src).then_inc(loaded, 16)
            for n, (src, rows_, cols, _) in enumerate(items):
                if n >= 2:
                    sp.wait_ge(w_signs, n - 1)
                sp.dma_start(raw[0:rows_, n % 2, 0:cols], src).then_inc(w_loaded[n % 2], 16)

            def load_x(i, u):
                sp.dma_start(x[:, u, :], x_in[bass.ds(i * (UN * P) + u * P, P), :]).then_inc(x_loaded[u], 16)

            def store_y(i, u):
                sp.wait_ge(y_ready, i * UN + (u + 1))
                sp.dma_start(x_out[bass.ds(i * (UN * P) + u * P, P), :], y[:, u, :]).then_inc(stored[u], 16)

            for u in range(UN):
                load_x(0, u)
            with sp.Fori(0, TRIPS - 1) as i:
                for u in range(UN):
                    store_y(i, u)
                    load_x(i + 1, u)
            for u in range(UN):
                store_y(TRIPS - 1, u)
            for u in range(UN):
                sp.wait_ge(stored[u], 16 * TRIPS)

        @block.gpsimd
        def _(pool):
            pool.wait_ge(loaded, 32)
            with pool.Fori(0, TRIPS) as i:
                for u in range(UN):
                    pool.wait_ge(var_ready, i * UN + (u + 1))
                    nc.gpsimd.tensor_tensor(rstd[:, u, :], ve[:, u, :], mhalf[:], ALU.pow).then_inc(rstd_ready, 1)

        @block.vector
        def _(dve):
            c = Chain(dve, chain)

            def fp4(n, cols, magnitude, sign, out, done):
                nb = cols // FP4_BLOCK
                blocks = lambda a: a.rearrange("p (b e) -> p b e", e=FP4_BLOCK)
                per_block = lambda a: a[0:n, 0:nb].unsqueeze(2).to_broadcast([n, nb, FP4_BLOCK])
                r, l, a = ratio[0:n, 0:cols], level[0:n, 0:cols], above[0:n, 0:cols]
                c.link(nc.vector.tensor_reduce(amax[0:n, 0:nb], blocks(magnitude), AX, ALU.max))
                c.link(nc.vector.tensor_scalar(scl[0:n, 0:nb], amax[0:n, 0:nb], 1.0 / FP4_MAX, 1e-12, ALU.mult, ALU.max))
                c.link(nc.vector.reciprocal(inv[0:n, 0:nb], scl[0:n, 0:nb]))
                c.link(nc.vector.tensor_tensor(blocks(r), blocks(magnitude), per_block(inv), ALU.mult))
                nc.vector.tensor_scalar(a, r, 0.25, None, ALU.is_gt)
                c.link(nc.vector.tensor_scalar(l, r, 5.0, 2.0, ALU.is_gt, ALU.mult))
                for at in (3.5, 2.5):
                    c.link(nc.vector.scalar_tensor_tensor(l, r, at, l, ALU.is_gt, ALU.add))
                c.link(nc.vector.scalar_tensor_tensor(l, l, 2.0, a, ALU.mult, ALU.add))
                for at in (1.75, 1.25, 0.75):
                    c.link(nc.vector.scalar_tensor_tensor(l, r, at, l, ALU.is_gt, ALU.add))
                c.link(nc.vector.scalar_tensor_tensor(blocks(l), blocks(l), 0.5, per_block(scl), ALU.mult, ALU.mult))
                nc.vector.tensor_tensor(out, l, sign, ALU.mult).then_inc(done, 1)

            QL = 12
            for n, (_, rows_, cols, _) in enumerate(items):
                dve.wait_ge(w_signs, n + 1)
                if n >= 2:
                    dve.wait_ge(wT_psum, n - 1)
                fp4(rows_, cols, mag[0:rows_, n % 2, 0:cols], sgn[0:rows_, n % 2, 0:cols], qh[0:rows_, n % 2, 0:cols], w_quantised)

            def norm(i):
                for u in range(UN):
                    dve.wait_ge(x_loaded[u], i * 16 + 16)
                    ins = nc.vector.bn_stats(st[:, u, :], x[:, u, :])
                c.link(ins, apart=True)
                for u in range(UN):
                    ins = nc.vector.bn_aggr(mv[:, u, :], st[:, u, :])
                c.link(ins)
                for u in range(UN):
                    nc.vector.tensor_scalar(ve[:, u, :], mv[:, u, 1:2], LN_EPS, None, ALU.add).then_inc(var_ready, 1)
                for u in range(UN):
                    dve.wait_ge(rstd_ready, i * UN + (u + 1))
                    nc.vector.tensor_scalar(z[:, u, :], x[:, u, :], mv[:, u, 0:1], rstd[:, u, :], ALU.subtract, ALU.mult).then_inc(z_ready, 1)

            def round_z(i, u):
                dve.wait_ge(z_signs, i * UN + (u + 1))
                fp4(P, D, mag[:, u, 0:D], sgn[:, u, 0:D], qz[:, u, :], qz_ready)

            def hidden(i, u):
                dve.wait_ge(silu_ready, i * UN + (u + 1))
                for j in range(2):
                    nc.vector.tensor_tensor(raw[:, u, j * HI:(j + 1) * HI], silu[:, u, j * HI:(j + 1) * HI], ps_u[j][:, 0:HI], ALU.mult).then_inc(h_ready, 1)

            def round_h(i, u):
                dve.wait_ge(h_signs, i * UN + (u + 1))
                fp4(P, I, mag[:, u, :], sgn[:, u, :], qh[:, u, :], qh_ready)

            def result(i, u):
                dve.wait_ge(y_psum, i * UN + (u + 1))
                dve.wait_ge(stored[u], i * 16)
                nc.vector.tensor_tensor(y[:, u, :], ps_y[:, 0:D], x[:, u, :], ALU.add).then_inc(y_ready, 1)

            with dve.Fori(0, TRIPS) as i:
                c.enter(i, 2 + 2 * UN * QL)
                norm(i)
                for step, u in ((round_z, 0), (round_z, 1), (hidden, 0), (round_z, 2), (round_h, 0), (hidden, 1), (round_z, 3), (round_h, 1),
                                (result, 0), (hidden, 2), (round_h, 2), (result, 1), (hidden, 3), (round_h, 3), (result, 2), (result, 3)):
                    step(i, u)
                c.leave(TRIPS)

        @block.scalar
        def _(act):
            for n, (_, rows_, cols, dst) in enumerate(items):
                act.wait_ge(w_loaded[n % 2], 16 * (n // 2 + 1))
                if n >= 2:
                    act.wait_ge(w_quantised, n - 1)
                nc.scalar.activation(mag[0:rows_, n % 2, 0:cols], raw[0:rows_, n % 2, 0:cols], ACT.Abs)
                nc.scalar.activation(sgn[0:rows_, n % 2, 0:cols], raw[0:rows_, n % 2, 0:cols], ACT.Sign).then_inc(w_signs, 1)
                act.wait_ge(wT_psum, n + 1)
                for k, d in enumerate(dst):
                    ins = nc.scalar.copy(d, ps_h[k // 4][0:d.shape[0], (k % 4) * P:(k % 4) * P + rows_])
                ins.then_inc(wT_ready, 1)

            def signs_z(i, u):
                act.wait_ge(z_ready, i * UN + (u + 1))
                nc.scalar.activation(mag[:, u, 0:D], z[:, u, :], ACT.Abs)
                nc.scalar.activation(sgn[:, u, 0:D], z[:, u, :], ACT.Sign).then_inc(z_signs, 1)

            def copy_zT(i, u):
                act.wait_ge(zT_psum, i * UN + (u + 1))
                nc.scalar.copy(zqT[:, u], ps_z[:, 0:D].rearrange("p (k t) -> p k t", k=KD)).then_inc(zT_ready, 1)

            def silus(i, u):
                act.wait_ge(gu_psum, i * UN + (u + 1))
                for j in range(2):
                    ins = nc.scalar.activation(silu[:, u, j * HI:(j + 1) * HI], ps_g[j][:, 0:HI], ACT.Silu)
                ins.then_inc(silu_ready, 1)

            def signs_h(i, u):
                act.wait_ge(h_ready, (i * UN + (u + 1)) * 2)
                nc.scalar.activation(mag[:, u, :], raw[:, u, :], ACT.Abs)
                nc.scalar.activation(sgn[:, u, :], raw[:, u, :], ACT.Sign).then_inc(h_signs, 1)

            def copy_hT(i, u):
                act.wait_ge(hT_psum, i * UN + (u + 1))
                nc.scalar.copy(hqT[:, u, 0:4, :], ps_h[0][:].rearrange("p (k t) -> p k t", k=4))
                nc.scalar.copy(hqT[:, u, 4, :], ps_h[1][:, 0:P])
                nc.scalar.copy(hqT[0:I - 5 * P, u, 5, :], ps_h[1][0:I - 5 * P, P:2 * P]).then_inc(hT_ready, 1)

            with act.Fori(0, TRIPS) as i:
                for u in range(UN):
                    signs_z(i, u)
                for step, u in ((copy_zT, 0), (copy_zT, 1), (silus, 0), (signs_h, 0), (copy_zT, 2), (silus, 1), (signs_h, 1), (copy_hT, 0),
                                (silus, 2), (copy_zT, 3), (signs_h, 2), (copy_hT, 1), (silus, 3), (signs_h, 3), (copy_hT, 2), (copy_hT, 3)):
                    step(i, u)

        @block.tensor
        def _(pe):
            pe.wait_ge(loaded, 32)
            for n, (_, rows_, cols, dst) in enumerate(items):
                pe.wait_ge(w_quantised, n + 1)
                pe.wait_ge(wT_ready, n)
                for k in range(len(dst)):
                    width = min(P, cols - k * P)
                    ins = nc.tensor.transpose(ps_h[k // 4][0:width, (k % 4) * P:(k % 4) * P + rows_],
                                              qh[0:rows_, n % 2, k * P:k * P + width], ident[0:rows_, 0:rows_])
                ins.then_inc(wT_psum, 1)
            pe.wait_ge(wT_ready, len(items))

            def transpose_z(i, u):
                pe.wait_ge(qz_ready, i * UN + (u + 1))
                pe.wait_ge(zT_ready, i * UN + u)
                for k in range(KD):
                    ins = nc.tensor.transpose(ps_z[:, k * P:(k + 1) * P], qz[:, u, k * P:(k + 1) * P], ident[:])
                ins.then_inc(zT_psum, 1)

            def gate_up(i, u):
                pe.wait_ge(zT_ready, i * UN + (u + 1))
                pe.wait_ge(h_ready, (i * UN + u) * 2)
                for j in range(2):
                    for g, bank in ((0, ps_g[j]), (1, ps_u[j])):
                        for k in range(KD):
                            ins = nc.tensor.matmul(bank[:, 0:HI], zqT[:, u, k, :], guT[g][:, k, j * HI:(j + 1) * HI],
                                                   start=(k == 0), stop=(k == KD - 1))
                ins.then_inc(gu_psum, 1)

            def transpose_h(i, u):
                pe.wait_ge(qh_ready, i * UN + (u + 1))
                for k in range(IC):
                    width = min(P, I - k * P)
                    ins = nc.tensor.transpose(ps_h[k // 4][0:width, (k % 4) * P:(k % 4 + 1) * P], qh[:, u, k * P:k * P + width], ident[:])
                ins.then_inc(hT_psum, 1)

            def down(i, u):
                pe.wait_ge(hT_ready, i * UN + (u + 1))
                pe.wait_ge(y_ready, i * UN + u)
                for k in range(IC):
                    width = min(P, I - k * P)
                    ins = nc.tensor.matmul(ps_y[:, 0:D], hqT[0:width, u, k, :], downT[0:width, k, :], start=(k == 0), stop=(k == IC - 1))
                ins.then_inc(y_psum, 1)

            with pe.Fori(0, TRIPS) as i:
                for step, u in ((transpose_z, 0), (gate_up, 0), (transpose_z, 1), (gate_up, 1), (transpose_z, 2), (transpose_h, 0), (down, 0),
                                (gate_up, 2), (transpose_z, 3), (transpose_h, 1), (down, 1), (gate_up, 3),
                                (transpose_h, 2), (down, 2), (transpose_h, 3), (down, 3)):
                    step(i, u)


_OUT = (4, 1024, 256)


def build(nc, a, out):
    B, S, _ = _OUT
    T = B * S
    streams = [nc.dram_tensor(f"stream{i}", (T, D), F32).ap() for i in range(3)]
    consts = {n: a[n] for n in ("ident", "mhalf", "iota8", "cum", "ends", "mask", "eye")}
    local_attention(nc, a["x"], consts, {n: a["L0_" + n] for n in ("WpT", "WqT", "WkvT", "WoT", "bp", "bq", "bk", "bv", "bo")}, streams[0], B, S, 16)
    mixture_of_experts(nc, streams[0], consts, {n: a[n] for n in ("router_w", "router_b", "upT", "downT")}, streams[1], T, 8, 1024)
    delta_attention(nc, streams[1], consts, {n: a["L1_" + n] for n in ("WaT", "WaRT", "WkT", "WqT", "WvT", "WbgT", "WoT", "ba", "baR", "bbg", "ln_w", "ln_b")},
                    streams[2], B, S, 16, 64)
    fp4_feed_forward(nc, streams[2], consts, {n: a[n] for n in ("w_gate", "w_up", "w_down")}, out.rearrange("b s d -> (b s) d"), T, 704)


def kernel(**inputs):
    import concourse.bacc as _bacc
    from concourse.bass_utils import run_bass_kernel_spmd as _run

    g = {n: np.asarray(v) for n, v in inputs.items()}
    t = lambda n: g[n].T
    arrays = {
        "x": g["L0_attn_x"],
        "L0_WpT": t("L0_attn_Wp"), "L0_WqT": t("L0_attn_Wq"), "L0_WkvT": np.concatenate([t("L0_attn_Wk"), t("L0_attn_Wv")], axis=1), "L0_WoT": t("L0_attn_Wo"),
        "L0_bp": g["L0_attn_bp"].reshape(KD, P).T, "L0_bq": g["L0_attn_bq"], "L0_bk": g["L0_attn_bk"], "L0_bv": g["L0_attn_bv"], "L0_bo": g["L0_attn_bo"],
        "router_w": g["L0_ffn_router_w"], "router_b": g["L0_ffn_router_b"],
        "upT": g["L0_ffn_expert_up"].transpose(0, 2, 1), "downT": g["L0_ffn_expert_down"].transpose(0, 2, 1),
        "L1_WaT": t("L1_attn_Wa"), "L1_WaRT": t("L1_attn_WaR"), "L1_WkT": t("L1_attn_Wk"), "L1_WqT": t("L1_attn_Wq"), "L1_WvT": t("L1_attn_Wv"),
        "L1_WbgT": np.concatenate([t("L1_attn_Wb"), t("L1_attn_Wg")], axis=1), "L1_WoT": t("L1_attn_Wo"),
        "L1_ba": g["L1_attn_ba"], "L1_baR": g["L1_attn_baR"], "L1_bbg": np.concatenate([g["L1_attn_bb"], g["L1_attn_bg"]]),
        "L1_ln_w": g["L1_attn_ln_w"], "L1_ln_b": g["L1_attn_ln_b"],
        "w_gate": g["L1_ffn_w_gate"], "w_up": g["L1_ffn_w_up"], "w_down": g["L1_ffn_w_down"],
        "ident": np.eye(P, dtype=np.float32), "mhalf": np.full((P, 1), -0.5, np.float32), "iota8": np.arange(8, dtype=np.float32),
    }
    arrays.update(delta_consts())
    nc = _bacc.Bacc("TRN2", target_bir_lowering=False, num_devices=1)
    feeds, args = {}, {}
    for name, array in arrays.items():
        feeds[f"in_{name}"] = np.ascontiguousarray(array)
        args[name] = nc.dram_tensor(f"in_{name}", feeds[f"in_{name}"].shape, mybir.dt.from_np(feeds[f"in_{name}"].dtype), kind="ExternalInput").ap()
    out = nc.dram_tensor("out_0", _OUT, F32, kind="ExternalOutput").ap()
    build(nc, args, out)
    r = _run(nc, [feeds], core_ids=[0])
    return r.results[0]["out_0"]
```
